# Optimizing a Trainium2 kernel written in Bass

```python
import numpy as np
import jax
import jax.numpy as jnp

def _softmax(x, axis=-1):
    return jax.nn.softmax(x, axis=axis)

def _gelu(x):
    return jax.nn.gelu(x, approximate=True)

def _silu(x):
    return jax.nn.silu(x)

def _sigmoid(x):
    return jax.nn.sigmoid(x)

def _layernorm(x, axis=-1, eps=1e-05):
    m = jnp.mean(x, axis=axis, keepdims=True)
    v = jnp.var(x, axis=axis, keepdims=True)
    return (x - m) / jnp.sqrt(v + eps)

def _scatter_add(tgt, idx, src, axis=0):
    return tgt.at[idx].add(src)

def _segment_sum(src, seg, n):
    return jax.ops.segment_sum(src, seg, n)
kernel_name = 'mk_early_fusion_d1_tok_img768_r4_2cabc1'

def setup_inputs(seed: int=0):
    np.random.seed(seed)
    _w = jnp.asarray

    def _rec_inputs():
        import jax
        import jax.numpy as jnp
        _rk = jax.random.key(seed)
        x = -0.000222058 + 0.999998 * jax.random.normal(jax.random.fold_in(_rk, 1), (8, 3, 96, 96), jnp.float32)
        txt = 0.00051943 + 0.577438 * jax.random.normal(jax.random.fold_in(_rk, 2), (8, 512, 192), jnp.float32)
        return (x, txt)
    x, txt = _rec_inputs()

    def _L0_tok_setup():
        import jax, jax.numpy as jnp
        import numpy as np
        PATCH = 16
        EMBED = 192
        key = jax.random.key(seed)
        k1, k2, k3 = jax.random.split(key, 3)
        B, C, H, W_ = (32, 3, 128, 128)
        patch_dim = C * PATCH * PATCH
        images = jax.random.normal(k1, (B, C, H, W_), dtype=jnp.float32)
        bound = 1.0 / np.sqrt(patch_dim)
        W = jax.random.uniform(k2, (EMBED, patch_dim), dtype=jnp.float32, minval=-bound, maxval=bound)
        b = jax.random.uniform(k3, (EMBED,), dtype=jnp.float32, minval=-bound, maxval=bound)
        return {'images': images, 'W': W, 'b': b}
    _L0_tok_all = _L0_tok_setup()
    _L0_tok_in = {k: v for k, v in _L0_tok_all.items() if k in ('W', 'b')}
    del _L0_tok_all

    def _L0_attn_setup():
        import jax, jax.numpy as jnp
        import numpy as np
        D_MODEL = 192
        NUM_HEADS = 3
        HEAD_DIM = D_MODEL // NUM_HEADS
        GN_EPS = 1e-05

        def _xavier(key, shape, gain=0.5):
            fan_in, fan_out = (shape[1], shape[0])
            a = gain * np.sqrt(6.0 / (fan_in + fan_out))
            return jax.random.uniform(key, shape, jnp.float32, -a, a)
        key = jax.random.key(seed)
        ks = jax.random.split(key, 5)
        x = jax.random.normal(ks[0], (4, 512, D_MODEL), jnp.float32)
        Wq = _xavier(ks[1], (D_MODEL, D_MODEL))
        Wk = _xavier(ks[2], (D_MODEL, D_MODEL))
        Wv = _xavier(ks[3], (D_MODEL, D_MODEL))
        Wo = _xavier(ks[4], (D_MODEL, D_MODEL))
        gammas = jnp.array([0.9, 0.95, 0.99], jnp.float32)
        gn_weight = jnp.ones((D_MODEL,), jnp.float32)
        gn_bias = jnp.zeros((D_MODEL,), jnp.float32)
        return {'x': x, 'Wq': Wq, 'Wk': Wk, 'Wv': Wv, 'Wo': Wo, 'gammas': gammas, 'gn_weight': gn_weight, 'gn_bias': gn_bias}
    _L0_attn_all = _L0_attn_setup()
    _L0_attn_in = {k: v for k, v in _L0_attn_all.items() if k in ('Wq', 'Wk', 'Wv', 'Wo', 'gammas', 'gn_weight', 'gn_bias')}
    del _L0_attn_all

    def _L0_ffn_setup():
        import jax, jax.numpy as jnp
        import numpy as np
        N_EMBD = 192
        EXPERT_SIZES = [(8, 128), (8, 256)]
        TOP_K = 8
        NORM_TOPK_PROB = True
        EXPERT_WIDTHS = []
        for cnt, w in EXPERT_SIZES:
            EXPERT_WIDTHS += [w] * cnt
        EXPERT_OFFSETS = np.concatenate([[0], np.cumsum(EXPERT_WIDTHS)]).astype(np.int64)
        NUM_EXPERTS = len(EXPERT_WIDTHS)
        TOTAL_WIDTH = int(EXPERT_OFFSETS[-1])
        key = jax.random.key(seed)
        k1, k2, k3, k4 = jax.random.split(key, 4)
        x = jax.random.normal(k1, (1, 512, N_EMBD), dtype=jnp.float32)
        router_w = jax.random.normal(k2, (NUM_EXPERTS, N_EMBD), dtype=jnp.float32) * 0.02
        w1 = jnp.clip(jax.random.normal(k3, (N_EMBD, TOTAL_WIDTH), dtype=jnp.float32) * 0.02, -0.06, 0.06)
        w2 = jnp.clip(jax.random.normal(k4, (TOTAL_WIDTH, N_EMBD), dtype=jnp.float32) * 0.02, -0.06, 0.06)
        return {'x': x, 'router_w': router_w, 'w1': w1, 'w2': w2}
    _L0_ffn_all = _L0_ffn_setup()
    _L0_ffn_in = {k: v for k, v in _L0_ffn_all.items() if k in ('router_w', 'w1', 'w2')}
    del _L0_ffn_all
    return {'x': x, 'txt': txt, 'L0_tok_W': _L0_tok_in['W'], 'L0_tok_b': _L0_tok_in['b'], 'L0_attn_Wq': _L0_attn_in['Wq'], 'L0_attn_Wk': _L0_attn_in['Wk'], 'L0_attn_Wv': _L0_attn_in['Wv'], 'L0_attn_Wo': _L0_attn_in['Wo'], 'L0_attn_gammas': _L0_attn_in['gammas'], 'L0_attn_gn_weight': _L0_attn_in['gn_weight'], 'L0_attn_gn_bias': _L0_attn_in['gn_bias'], 'L0_ffn_router_w': _L0_ffn_in['router_w'], 'L0_ffn_w1': _L0_ffn_in['w1'], 'L0_ffn_w2': _L0_ffn_in['w2']}

def reference(x, txt, L0_tok_W, L0_tok_b, L0_attn_Wq, L0_attn_Wk, L0_attn_Wv, L0_attn_Wo, L0_attn_gammas, L0_attn_gn_weight, L0_attn_gn_bias, L0_ffn_router_w, L0_ffn_w1, L0_ffn_w2):
    import jax
    import jax.numpy as jnp

    def _L0_tok_ref(images, W, b):
        import jax, jax.numpy as jnp
        import numpy as np
        PATCH = 16
        EMBED = 192
        B, C, H, Wd = images.shape
        nh, nw = (H // PATCH, Wd // PATCH)
        p = images.reshape(B, C, nh, PATCH, nw, PATCH)
        p = p.transpose(0, 2, 4, 1, 3, 5).reshape(B, nh * nw, C * PATCH * PATCH)
        return jnp.einsum('bnd,ed->bne', p, W) + b

    def _L0_attn_ref(x, Wq, Wk, Wv, Wo, gammas, gn_weight, gn_bias):
        import jax, jax.numpy as jnp
        import numpy as np
        D_MODEL = 192
        NUM_HEADS = 3
        HEAD_DIM = D_MODEL // NUM_HEADS
        GN_EPS = 1e-05

        def _xavier(key, shape, gain=0.5):
            fan_in, fan_out = (shape[1], shape[0])
            a = gain * np.sqrt(6.0 / (fan_in + fan_out))
            return jax.random.uniform(key, shape, jnp.float32, -a, a)
        B, L, D = x.shape
        H = gammas.shape[0]
        hd = D // H
        q = (x @ Wq.T).reshape(B, L, H, hd)
        k = (x @ Wk.T).reshape(B, L, H, hd)
        v = (x @ Wv.T).reshape(B, L, H, hd)
        scores = jnp.einsum('blhe,bmhe->bhlm', q, k) / jnp.sqrt(jnp.float32(hd))
        pos = jnp.arange(L)
        diff = pos[None, :] - pos[:, None]
        mask = diff >= 0
        dclip = jnp.maximum(diff, 0).astype(jnp.float32)
        decay = jnp.where(mask, gammas[:, None, None] ** dclip, 0.0)
        scores = scores * decay[None]
        weights = jax.nn.softmax(scores, axis=-1)
        o = jnp.einsum('bhlm,bmhe->blhe', weights, v)
        mean = o.mean(axis=(1, 3), keepdims=True)
        var = o.var(axis=(1, 3), keepdims=True)
        o = (o - mean) / jnp.sqrt(var + GN_EPS)
        y = o.reshape(B, L, D) * gn_weight + gn_bias
        return y @ Wo.T

    def _L0_ffn_ref(x, router_w, w1, w2):
        import jax, jax.numpy as jnp
        import numpy as np
        N_EMBD = 192
        EXPERT_SIZES = [(8, 128), (8, 256)]
        TOP_K = 8
        NORM_TOPK_PROB = True
        EXPERT_WIDTHS = []
        for cnt, w in EXPERT_SIZES:
            EXPERT_WIDTHS += [w] * cnt
        EXPERT_OFFSETS = np.concatenate([[0], np.cumsum(EXPERT_WIDTHS)]).astype(np.int64)
        NUM_EXPERTS = len(EXPERT_WIDTHS)
        TOTAL_WIDTH = int(EXPERT_OFFSETS[-1])
        B, S, D = x.shape
        xt = x.reshape(-1, D)
        T = xt.shape[0]
        logits = jnp.einsum('td,ed->te', xt, router_w)
        probs = jax.nn.softmax(logits, axis=-1)
        topk_w, topk_idx = jax.lax.top_k(probs, TOP_K)
        if NORM_TOPK_PROB:
            topk_w = topk_w / jnp.sum(topk_w, axis=-1, keepdims=True)
        comb = jnp.zeros((T, NUM_EXPERTS), dtype=xt.dtype)
        comb = comb.at[jnp.arange(T)[:, None], topk_idx].add(topk_w)
        out = jnp.zeros_like(xt)
        for e in range(NUM_EXPERTS):
            off = int(EXPERT_OFFSETS[e])
            wd = EXPERT_WIDTHS[e]
            h = jax.nn.gelu(xt @ w1[:, off:off + wd])
            out = out + comb[:, e:e + 1] * (h @ w2[off:off + wd, :])
        return out.reshape(B, S, D)
    h = _L0_tok_ref(x, L0_tok_W, L0_tok_b)
    h = jnp.concatenate([h, txt], axis=1)
    h = h + _L0_attn_ref(_layernorm(h, axis=-1), L0_attn_Wq, L0_attn_Wk, L0_attn_Wv, L0_attn_Wo, L0_attn_gammas, L0_attn_gn_weight, L0_attn_gn_bias)
    h = h + _L0_ffn_ref(_layernorm(h, axis=-1), L0_ffn_router_w, L0_ffn_w1, L0_ffn_w2)
    return h

_drawn_inputs = setup_inputs


def setup_inputs(seed=0):
    import zlib

    import numpy as np

    out = dict(_drawn_inputs(seed))
    spreads = {'L0_attn_gn_weight': (1.0, 0.2), 'L0_attn_gn_bias': (0.0, 0.1)}
    factors = {'L0_ffn_router_w': 4.151, 'L0_ffn_w1': 2.967, 'L0_ffn_w2': 2.931}
    for name, (base, spread) in spreads.items():
        noise = np.random.default_rng([zlib.crc32(name.encode()), seed]).standard_normal(out[name].shape)
        drawn = base * np.exp(spread * noise) if base else spread * noise
        out[name] = jnp.asarray(drawn.astype(out[name].dtype))
    for name, factor in factors.items():
        out[name] = (out[name] * factor).astype(out[name].dtype)
    return out
```

```python
from contextlib import ExitStack

import concourse.bass as bass
from concourse import mybir

F32 = mybir.dt.float32
F32R = mybir.dt.float32r
ALU = mybir.AluOpType
ACT = mybir.ActivationFunctionType
AX = mybir.AxisListType

P = 128
B = 8
D = 192
IMG = 36
TXT = 512
L = IMG + TXT
NT = -(-L // P)
LAST = L - (NT - 1) * P
HALF = L // 2
H = 3
HD = D // H
KT = 6
EPS = 1e-5
NEG = -3.0e38

SUMS = 64
KEY_LAST = SUMS + NT - 1
LX = (NT - 1) * P + KEY_LAST
WIDTH = [LX - I * P for I in range(NT)]
OFF = [sum(WIDTH[:I]) for I in range(NT)]
PW = sum(WIDTH)

E = 16
EW = [128] * 8 + [256] * 8
TILE_E = [e for e in range(E) for _ in range(EW[e] // P)]
NW = len(TILE_E)
LAST_OF = [max(k for k in range(NW) if TILE_E[k] == e) for e in range(E)]
TOPK = 8
CREDIT = 1

QK_W, V_W, O_W, R_W = 512, 256, D, E
AW = QK_W + V_W + O_W + R_W
DECAY_L = 127 + L + 1


def rows(I):
    return P if I < NT - 1 else LAST


def nth(b, per, k):
    return b * per + k


def early_fusion(nc, patches, txt, tok_w, tok_b, gammas, gn_w, gn_b, attn_w, w1, w2, out):
    ctx = ExitStack()
    phase_a, staging = ExitStack(), ExitStack()

    def sb(name, shape, dt=F32, scope=ctx):
        return scope.enter_context(nc.sbuf_tensor(name, shape, dt))

    def sem(name):
        return ctx.enter_context(nc.semaphore(name))

    with ctx:
        h = sb("h", [P, B, NT, D])
        ident = sb("ident", [P, P])
        ps = ctx.enter_context(nc.psum_tensor("ps", [P, 8, 512], F32))
        psf = ps[:, :, :].rearrange("p b n -> p (b n)")

        def sa(name, shape, dt=F32):
            return sb(name, shape, dt, phase_a)

        aw_hi, aw_lo = sa("aw_hi", [P, 2, AW], F32R), sa("aw_lo", [P, 2, AW], F32R)
        decay = sa("decay", [P, H, L])
        head_mean = sa("head_mean", [P, P])
        gnw, gnb = sa("gnw", [P, 2]), sa("gnb", [P, 2])
        lower_count = sa("lower_count", [P, NT])
        xn, xn2 = sa("xn", [P, NT, 256]), sa("xn2", [P, NT, 256])
        xa_hi, xa_lo, xb = sa("xa_hi", [P, LX], F32R), sa("xa_lo", [P, LX], F32R), sa("xb", [P, LX], F32R)
        q01_hi, q01_lo = sa("q01_hi", [P, L], F32R), sa("q01_lo", [P, L], F32R)
        k01_hi, k01_lo = sa("k01_hi", [P, L], F32R), sa("k01_lo", [P, L], F32R)
        q2 = sa("q2", [P, L], F32R)
        k2_hi, k2_lo = sa("k2_hi", [P, L], F32R), sa("k2_lo", [P, L], F32R)
        v = sa("v", [P, NT, 3 * P])
        sc = [sa(f"sc{i}", [P, PW]) for i in range(2)]
        pr = [sa(f"pr{i}", [P, PW]) for i in range(2)]
        pt = [sa(f"pt{i}", [P, 4, 512]) for i in range(2)]
        ot = sa("ot", [P, 2, L])
        y = sa("y", [P, 2, L])
        y01_hi, y01_lo, y2 = sa("y01_hi", [P, L], F32R), sa("y01_lo", [P, L], F32R), sa("y2", [P, L], F32R)
        x2 = sa("x2", [P, 3, L], F32R)
        lt = sa("lt", [E, NT * P])
        ct = sa("ct", [E, NT * P])
        st6, mv, veps = sa("st6", [P, NT, 6]), sa("mv", [P, NT, 2]), sa("veps", [P, NT])
        rstd = sa("rstd", [P, NT])
        st6b, mvb, vepsb, rstdb = sa("st6b", [P, NT, 6]), sa("mvb", [P, NT, 2]), sa("vepsb", [P, NT]), sa("rstdb", [P, NT])
        neg_half = sa("neg_half", [P, NT])
        mx = [sa(f"mx{i}", [P, NT]) for i in range(2)]
        nm = [sa(f"nm{i}", [P, NT]) for i in range(2)]
        zero_score = [sa(f"zero_score{i}", [P, NT]) for i in range(2)]
        row_sum = [sa(f"row_sum{i}", [P, NT]) for i in range(2)]
        den = [sa(f"den{i}", [P, NT]) for i in range(2)]
        inv_den = [sa(f"inv_den{i}", [P, NT]) for i in range(2)]
        gst, gmv, gtot = sa("gst", [P, 2, 12]), sa("gmv", [P, 2, 2]), sa("gtot", [P, 2, 2])
        gvar, grstd = sa("gvar", [P, 2]), sa("grstd", [P, 2])
        gscale, gshift, gtmp = sa("gscale", [P, 2]), sa("gshift", [P, 2]), sa("gtmp", [P, 2])
        lmax, lsub, lexp = sa("lmax", [P, NT]), sa("lsub", [P, NT, E]), sa("lexp", [P, NT, E])
        top, left = sa("top", [P, NT, TOPK]), sa("left", [P, NT, E])
        chosen, tsum, tinv, comb = sa("chosen", [P, NT, E]), sa("tsum", [P, NT]), sa("tinv", [P, NT]), sa("comb", [P, NT, E])
        def sg(name, shape, dt=F32):
            return sb(name, shape, dt, staging)

        aw_raw = sg("aw_raw", [P, 2, AW])
        pat, tokw = sg("pat", [P, KT, B * IMG]), sg("tokw", [P, KT, D])
        tokb = sg("tokb", [P, 2])
        emb = sg("emb", [P, 2, B * IMG])
        gam = sg("gam", [P, H])
        drow = sg("drow", [P, H, DECAY_L])
        staging.close()
        phase_a.close()

        w1_hi, w1_lo = sb("w1_hi", [P, 2, NW * P], F32R), sb("w1_lo", [P, 2, NW * P], F32R)
        w2_hi, w2_lo = sb("w2_hi", [P, NW, P], F32R), sb("w2_lo", [P, NW, P], F32R)
        w2_r = sb("w2_r", [P, NW, P], F32R)
        raw_scope = ExitStack()
        w1_raw = sb("w1_raw", [P, 2, NW * P], F32, raw_scope)
        w2_raw = sb("w2_raw", [P, NW, 256], F32, raw_scope)
        raw_scope.close()
        x2_all = sb("x2_all", [P, 3, B, L], F32R)
        act = [sb(f"act{i}", [P, 2, HALF]) for i in range(3)]
        act_hi = [sb(f"act_hi{i}", [P, 2, HALF], F32R) for i in range(3)]
        act_lo = [sb(f"act_lo{i}", [P, 2, HALF], F32R) for i in range(3)]
        gate = [sb(f"gate{i}", [P, 2, HALF]) for i in range(4)]
        out_a, out_r, out_t = sb("out_a", [P, L]), sb("out_r", [P, L]), sb("out_t", [P, NT, HD])

        decay_rows = nc.dram_tensor("decay_rows", [H, P * DECAY_L], F32).ap()
        x2_dram = nc.dram_tensor("x2_dram", [B, P, 3 * L], F32).ap()
        comb_dram = nc.dram_tensor("comb_dram", [B, E, L], F32).ap()

        ld_aw, ld_pat, ld_small = sem("ld_aw"), sem("ld_pat"), sem("ld_small")
        ld_h0, ld_h = sem("ld_h0"), sem("ld_h")
        consts = sem("consts")
        decay_built, decay_stored, ld_decay = sem("decay_built"), sem("decay_stored"), sem("ld_decay")
        aw_hi_ready, aw_lo_ready = sem("aw_hi_ready"), sem("aw_lo_ready")
        emb_done, emb_copied, embt_done, embt_copied = sem("emb_done"), sem("emb_copied"), sem("embt_done"), sem("embt_copied")
        ln1_var, ln1_rstd, ln1_normed, xn_ready = sem("ln1_var"), sem("ln1_rstd"), sem("ln1_normed"), sem("xn_ready")
        ln2_rstd, ln2_normed = sem("ln2_rstd"), sem("ln2_normed")
        xt_done, xt_ext, xt_hi, xt_lo = sem("xt_done"), sem("xt_ext"), sem("xt_hi"), sem("xt_lo")
        qk_done, qk_hi, qk_lo = sem("qk_done"), sem("qk_hi"), sem("qk_lo")
        v_done, v_copied = sem("v_done"), sem("v_copied")
        s_done, decayed, nm_ready = sem("s_done"), sem("decayed"), sem("nm_ready")
        exp_done, den_ready, probs_ready = sem("exp_done"), sem("den_ready"), sem("probs_ready")
        pt_done, pt_dve, pt_act = sem("pt_done"), sem("pt_dve"), sem("pt_act")
        o_done, o_copied = sem("o_done"), sem("o_copied")
        gn_part, gn_sum, gn_var, gn_rstd = sem("gn_part"), sem("gn_sum"), sem("gn_var"), sem("gn_rstd")
        y_ready, y_hi, y_lo = sem("y_ready"), sem("y_hi"), sem("y_lo")
        wo_done, wo_added, ln2_var, xn2_ready = sem("wo_done"), sem("wo_added"), sem("ln2_var"), sem("xn2_ready")
        x2t_done, x2_hi, x2_lo, x2_stored = sem("x2t_done"), sem("x2_hi"), sem("x2_lo"), sem("x2_stored")
        lg_done, lt_copied, lgn_done, l_sub, l_exp = sem("lg_done"), sem("lt_copied"), sem("lgn_done"), sem("l_sub"), sem("l_exp")
        comb_ready, ct_done, ct_copied, ct_stored = sem("comb_ready"), sem("ct_done"), sem("ct_copied"), sem("ct_stored")
        phase = sem("phase")
        tick = {n: sem(f"tick_{n}") for n in ("dve", "pool", "pe")}
        ld_w = sem("ld_w")
        w_hi_ready, w_lo_ready = sem("w_hi_ready"), sem("w_lo_ready")
        ld_x2, ld_gate = sem("ld_x2"), [sem(f"ld_gate{i}") for i in range(4)]
        up_done, gelu_done, gated, act_hi_ready, act_lo_ready = sem("up_done"), sem("gelu_done"), sem("gated"), sem("act_hi_ready"), sem("act_lo_ready")
        down_done, acc_a_copied, acc_r_copied = sem("down_done"), sem("acc_a_copied"), sem("acc_r_copied")
        outt_done, out_ready, out_stored = sem("outt_done"), sem("out_ready"), sem("out_stored")

        block = ctx.enter_context(nc.Block())

        def apart(eng, name):
            eng.sem_inc(tick[name], 1)

        def batches(eng, body):
            body(0, tail=False, head=True, more=True)
            with eng.Fori(1, B - 1) as b:
                body(b, tail=True, head=True, more=True)
            body(B - 1, tail=True, head=True, more=False)
            body(B, tail=True, head=False, more=False)

        def end_of_phase_a(eng):
            eng.drain().then_inc(phase, 1)
            eng.wait_ge(phase, 5)

        def tokens(ap, b, I):
            return ap[:rows(I), bass.ds(b, 1), I, :].rearrange("p a d -> p (a d)")

        @block.sync
        def _(sp):
            def load_h(b0, b1, s):
                src = txt[b0:b1]
                sp.dma_start(h[IMG:P, b0:b1, 0, :], src[:, 0:P - IMG, :].rearrange("b p d -> p b d")).then_inc(s, 16)
                for I in range(1, NT - 1):
                    lo = I * P - IMG
                    sp.dma_start(h[:, b0:b1, I, :], src[:, lo:lo + P, :].rearrange("b p d -> p b d")).then_inc(s, 16)
                sp.dma_start(h[0:LAST, b0:b1, NT - 1, :], src[:, TXT - LAST:TXT, :].rearrange("b p d -> p b d")).then_inc(s, 16)

            sp.dma_start(gam[:, :], gammas.partition_broadcast(P)).then_inc(ld_small, 16)
            sp.dma_start(pat[:, :, :], patches).then_inc(ld_pat, 16)
            sp.dma_start(tokw[:, :, :], tok_w).then_inc(ld_pat, 16)
            sp.dma_start(tokb[:, :], tok_b).then_inc(ld_pat, 16)
            load_h(0, 1, ld_h0)
            sp.dma_start(aw_raw[:, :, :], attn_w).then_inc(ld_aw, 16)
            load_h(1, B, ld_h)
            sp.dma_start(gnw[:, :], gn_w).then_inc(ld_small, 16)
            sp.dma_start(gnb[:, :], gn_b).then_inc(ld_small, 16)
            sp.wait_ge(decay_built, 1)
            sp.dma_start(decay_rows.rearrange("h (p l) -> p h l", l=DECAY_L), drow[:, :, :]).then_inc(decay_stored, 16)
            sp.wait_ge(decay_stored, 16)
            shifted = decay_rows[:, 127:127 + P * (DECAY_L - 1)].rearrange("h (p l) -> p h l", l=DECAY_L - 1)
            sp.dma_start(decay[:, :, :], shifted[:, :, 0:L]).then_inc(ld_decay, 16)

            def stores(b, tail, head, more):
                if not tail:
                    return
                t = b - 1
                sp.wait_ge(x2_lo, nth(t, 3, 3))
                sp.dma_start(x2_dram[bass.ds(t, 1), :, :].rearrange("a p n -> p (a n)"),
                             x2[:, :, :].rearrange("p c n -> p (c n)").bitcast(F32)).then_inc(x2_stored, 16)
                sp.wait_ge(ct_copied, CREDIT + nth(t, 1, 1))
                sp.dma_start(comb_dram[bass.ds(t, 1), :, :].rearrange("a e n -> e (a n)"),
                             ct[:, 0:L]).then_inc(ct_stored, 16)

            batches(sp, stores)
            sp.wait_ge(x2_stored, CREDIT + 16 * B)
            sp.wait_ge(ct_stored, CREDIT + 16 * B)
            end_of_phase_a(sp)
            sp.dma_start(w1_raw[:, :, :], w1).then_inc(ld_w, 16)
            sp.dma_start(w2_raw[:, :, :], w2).then_inc(ld_w, 16)
            sp.wait_ge(w_hi_ready, 1)
            sp.wait_ge(w_lo_ready, 1)
            for b in range(B):
                if b:
                    sp.wait_ge(ld_x2, 16 * b)
                sp.dma_start(x2_all[:, :, b, :].bitcast(F32), x2_dram[b].rearrange("p (c n) -> p c n", c=3)).then_inc(ld_x2, 16)
                if b < 4:
                    sp.dma_start(gate[b][:, :, :].rearrange("p a n -> p (a n)"),
                                 comb_dram[0, b, :].partition_broadcast(P)).then_inc(ld_gate[b], 16)

            def gates(b, first):
                for e in range(first, E):
                    last = LAST_OF[(e - 4) % E] + 1
                    sp.wait_ge(gated, nth(b, NW, last) if e >= 4 else nth(b - 1, NW, last))
                    src = comb_dram[bass.ds(b, 1), e, :].rearrange("a n -> (a n)").partition_broadcast(P)
                    sp.dma_start(gate[e % 4][:, :, :].rearrange("p a n -> p (a n)"), src).then_inc(ld_gate[e % 4], 16)

            def store_out(b):
                sp.wait_ge(out_ready, nth(b, 1, 1))
                dst = out[bass.ds(b, 1), :, :].rearrange("a n d -> (a n) d")
                src = h[:, bass.ds(b, 1), :, :].rearrange("p a t d -> p (a t) d")
                sp.dma_start(dst[0:(NT - 1) * P, :].rearrange("(t p) d -> p t d", p=P), src[:, 0:NT - 1, :]).then_inc(out_stored, 16)
                sp.dma_start(dst[(NT - 1) * P:L, :], src[0:LAST, NT - 1, :]).then_inc(out_stored, 16)

            gates(0, 4)
            with sp.Fori(1, B) as b:
                gates(b, 0)
                store_out(b - 1)
            store_out(B - 1)
            sp.wait_ge(out_stored, 32 * B)

        @block.gpsimd
        def _(pool):
            pool.memset(ident[:, :], 0.0)
            pool.drain()
            pool.affine_select(out=ident[:, :], in_=ident[:, :], compare_op=ALU.not_equal, fill=1.0,
                               base=0, pattern=[[-1, P]], channel_multiplier=1).then_inc(consts, 1)
            pool.memset(neg_half[:, :], -0.5).then_inc(consts, 1)
            pool.drain()

            def rstd_of(b, var_sem, rs, ve, ready):
                pool.wait_ge(var_sem, nth(b, 1, 1))
                pool.tensor_tensor(rs[:, :], ve[:, :], neg_half[:, :], ALU.pow).then_inc(ready, 1)

            def twice(b, normed, dst, ready):
                pool.wait_ge(normed, nth(b, 1, 1))
                apart(pool, "pool")
                pool.tensor_copy(dst[:, :, D:256], dst[:, :, P:D]).then_inc(ready, 1)

            rstd_of(0, ln1_var, rstd, veps, ln1_rstd)
            twice(0, ln1_normed, xn, xn_ready)

            def scale_probs(b, hh):
                s = hh % 2
                pool.wait_ge(den_ready, nth(b, H, hh + 1))
                apart(pool, "pool")
                for I in range(NT):
                    r = rows(I)
                    t = pr[s][:r, OFF[I]:OFF[I] + WIDTH[I]]
                    last = pool.tensor_scalar(t, t, inv_den[s][:r, I:I + 1], None, ALU.mult)
                last.then_inc(probs_ready, 1)

            def body(b, tail, head, more):
                if tail:
                    pool.wait_ge(gn_var, nth(b - 1, 1, 1))
                    pool.tensor_tensor(grstd[:, :], gvar[:, :], neg_half[:, 0:2], ALU.pow).then_inc(gn_rstd, 1)
                if head:
                    scale_probs(b, 0)
                if tail:
                    rstd_of(b - 1, ln2_var, rstdb, vepsb, ln2_rstd)
                    twice(b - 1, ln2_normed, xn2, xn2_ready)
                if head:
                    scale_probs(b, 1)
                    scale_probs(b, 2)
                if more:
                    rstd_of(b + 1, ln1_var, rstd, veps, ln1_rstd)
                    twice(b + 1, ln1_normed, xn, xn_ready)

            batches(pool, body)
            end_of_phase_a(pool)

        @block.scalar
        def _(sc_eng):
            a = sc_eng

            def copy(dst, src):
                return a.activation(dst, src, ACT.Copy)

            a.wait_ge(ld_aw, 16)
            copy(aw_hi[:, :, :], aw_raw[:, :, :]).then_inc(aw_hi_ready, 1)
            a.wait_ge(emb_done, 1)
            a.activation(emb[:, 0, :], ps[:, 0, 0:B * IMG], ACT.Identity, bias=tokb[:, 0:1])
            a.activation(emb[0:HD, 1, :], ps[0:HD, 1, 0:B * IMG], ACT.Identity, bias=tokb[0:HD, 1:2]).then_inc(emb_copied, 1)

            def x_hi(b):
                a.wait_ge(xt_ext, nth(b, 1, 1))
                copy(xa_hi[:, :], psf[:, 0:LX]).then_inc(xt_hi, 1)
                copy(xb[:, :], psf[:, 1024:1024 + LX]).then_inc(xt_hi, 1)

            def halves(bank):
                return ps[:, bank:bank + 2, 0:HALF]

            def two(ap):
                return ap.rearrange("p (a n) -> p a n", a=2)

            def qk_round(b):
                for i, (dst, bank) in enumerate(((q01_hi, 4), (q2, 0), (k01_hi, 6), (k2_hi, 2))):
                    a.wait_ge(qk_done, nth(b, 4, i + 1))
                    copy(two(dst[:, :]), halves(bank)).then_inc(qk_hi, 1)

            def v_copy(b):
                for i, (bank, t0, n) in enumerate(((4, 0, 2), (5, 2, 2), (6, 4, 1))):
                    r = P if n == 2 else KEY_LAST
                    a.wait_ge(v_done, nth(b, 3, i + 1))
                    src = ps[:r, bank, 0:256 * n].rearrange("p (t d) -> p t d", t=n)
                    copy(v[:r, t0:t0 + n, 0:HD], src[:, :, 0:HD])
                    copy(v[:r, t0:t0 + n, P + HD:3 * P], src[:, :, HD:256]).then_inc(v_copied, 1)

            def exps(b, hh):
                s = hh % 2
                a.wait_ge(nm_ready, nth(b, H, hh + 1))
                a.activation(zero_score[s][:, :], nm[s][:, :], ACT.Exp)
                for I in range(NT):
                    r = rows(I)
                    cols = slice(OFF[I], OFF[I] + WIDTH[I])
                    last = a.activation(pr[s][:r, cols], sc[s][:r, cols], ACT.Exp, bias=nm[s][:r, I:I + 1],
                                        accum_out=row_sum[s][:r, I:I + 1])
                last.then_inc(exp_done, 1)

            def pt_copy(b, hh):
                s = hh % 2
                a.wait_ge(pt_done, nth(b, 4 * H, 4 * hh + 2))
                copy(pt[s][:KEY_LAST, 1, 0:LAST], ps[:KEY_LAST, 5, 0:LAST])
                copy(pt[s][:, 1, 64:64 + 3 * P], ps[:, 5, 64:64 + 3 * P]).then_inc(pt_act, 1)
                a.wait_ge(pt_done, nth(b, 4 * H, 4 * hh + 4))
                copy(pt[s][:, 3, 0:3 * P], ps[:, 5, 0:3 * P]).then_inc(pt_act, 1)

            def o_copy(b, i):
                a.wait_ge(o_done, nth(b, 2, i + 1))
                tail = 64 * i
                copy(ot[:, i, 0:512], ps[:, 6, :])
                copy(ot[:, i, 512:L], ps[:, 7, tail:tail + LAST]).then_inc(o_copied, 1)

            def y_round(t):
                a.wait_ge(y_ready, nth(t, 2, 1))
                copy(y01_hi[:, :], y[:, 0, :]).then_inc(y_hi, 1)
                a.wait_ge(y_ready, nth(t, 2, 2))
                copy(y2[:, :], y[:, 1, :]).then_inc(y_hi, 1)

            def x2_round(t):
                a.wait_ge(x2t_done, nth(t, 3, 1))
                a.wait_ge(x2_stored, CREDIT + 16 * t)
                copy(x2[:, 0, 0:512], ps[:, 4, :]).then_inc(x2_hi, 1)
                a.wait_ge(x2t_done, nth(t, 3, 2))
                copy(x2[:, 2, 0:512], ps[:, 5, :]).then_inc(x2_hi, 1)
                a.wait_ge(x2t_done, nth(t, 3, 3))
                copy(x2[:, 0, 512:L], ps[:, 4, 0:LAST])
                copy(x2[:, 2, 512:L], ps[:, 4, 64:64 + LAST]).then_inc(x2_hi, 1)

            def logits_copy(t):
                a.wait_ge(lg_done, nth(t, 1, 1))
                copy(lt[:, 0:HALF], ps[0:E, 5, 0:HALF])
                copy(lt[:, HALF:L], ps[0:E, 4, 0:HALF]).then_inc(lt_copied, 1)

            def logits_exp(t):
                a.wait_ge(l_sub, nth(t, 1, 1))
                a.activation(lexp[:, :, :], lsub[:, :, :], ACT.Exp).then_inc(l_exp, 1)

            def comb_copy(t):
                a.wait_ge(ct_done, nth(t, 1, 1))
                a.wait_ge(ct_stored, CREDIT + 16 * t)
                copy(ct[:, 0:512], ps[0:E, 4, :])
                copy(ct[:, 512:NT * P], ps[0:E, 5, 0:P]).then_inc(ct_copied, 1)

            def body(b, tail, head, more):
                t = b - 1
                if head:
                    x_hi(b)
                    qk_round(b)
                    v_copy(b)
                    exps(b, 0)
                if tail:
                    y_round(t)
                if head:
                    exps(b, 1)
                    pt_copy(b, 0)
                    exps(b, 2)
                if tail:
                    x2_round(t)
                if head:
                    pt_copy(b, 1)
                if tail:
                    logits_copy(t)
                if head:
                    o_copy(b, 0)
                if tail:
                    logits_exp(t)
                if head:
                    pt_copy(b, 2)
                    o_copy(b, 1)
                if tail:
                    comb_copy(t)

            for s in (x2_stored, ct_stored, ct_copied):
                a.sem_inc(s, CREDIT)
            batches(a, body)
            end_of_phase_a(a)

            a.wait_ge(ld_w, 32)
            copy(w1_hi[:, :, :], w1_raw[:, :, :])
            copy(w2_hi[:, :, :], w2_raw[:, :, 0:P])
            copy(w2_r[:, :, :], w2_raw[:, :, P:256]).then_inc(w_hi_ready, 1)

            def gelu(b, k):
                a.wait_ge(up_done, nth(b, NW, k + 1))
                if not (isinstance(b, int) and k < 3):
                    a.wait_ge(act_lo_ready, nth(b, NW, k - 2))
                a.activation(act[k % 3][:, :, :], ps[:, 2 * (k % 2):2 * (k % 2) + 2, 0:HALF],
                             ACT.Gelu_apprx_tanh).then_inc(gelu_done, 1)

            def act_round(b, k):
                a.wait_ge(gated, nth(b, NW, k + 1))
                if not (isinstance(b, int) and k < 3):
                    a.wait_ge(down_done, nth(b, NW, k - 2))
                copy(act_hi[k % 3][:, :, :], act[k % 3][:, :, :]).then_inc(act_hi_ready, 1)

            def ffn(b):
                for k in range(NW):
                    gelu(b, k)
                    if k >= 1:
                        act_round(b, k - 1)
                act_round(b, NW - 1)
                a.wait_ge(down_done, nth(b, NW, NW))
                copy(out_a[:, :].rearrange("p (a n) -> p a n", a=2), ps[:, 4:6, 0:HALF]).then_inc(acc_a_copied, 1)

            ffn(0)
            with a.Fori(1, B) as b:
                ffn(b)

        @block.vector
        def _(dve):
            for t in (0, 1):
                dve.memset(sc[t][:, :], NEG)
                dve.memset(mx[t][:, :], 0.0)
                dve.memset(row_sum[t][:, :], 1.0)
            dve.memset(mv[:, :, :], 1.0)
            dve.memset(mvb[:, :, :], 1.0)
            dve.memset(v[:, :, :], 0.0)
            dve.memset(lt[:, :], 0.0)
            dve.memset(xn[:, NT - 1, :], 0.0)
            dve.memset(xn2[:, NT - 1, :], 0.0)
            dve.memset(head_mean[:, :], 0.0)
            dve.memset(drow[:, :, :], 0.0)
            dve.drain()
            dve.memset(head_mean[0:HD, 0:HD], 1.0 / HD)
            dve.memset(head_mean[HD:P, HD:P], 1.0 / HD)
            for I in range(NT):
                dve.memset(lower_count[:, I:I + 1], float((P - 1) * I))
                for t in (0, 1):
                    if I:
                        at = OFF[I] + WIDTH[I] - (NT - 1)
                        dve.memset(sc[t][:, at:at + I], 0.0)
            dve.memset(drow[:, :, 127:128], 1.0).then_inc(consts, 1)
            dve.wait_ge(ld_small, 16 * 3)
            for hh in range(H):
                dve.tensor_copy(drow[:, hh, 128:129], gam[:, hh:hh + 1])
            n = 1
            while n < L - 1:
                m = min(n, L - 1 - n)
                dve.drain()
                for hh in range(H):
                    last = dve.tensor_scalar(drow[:, hh, 128 + n:128 + n + m], drow[:, hh, 128:128 + m],
                                             drow[:, hh, 127 + n:128 + n], None, ALU.mult)
                n += m
            last.then_inc(decay_built, 1)

            def layer_norm(b, s6, m2, ve, signal, rs, rs_ready, dst, normed):
                for I in range(NT):
                    dve.bn_stats(s6[:rows(I), I, :], tokens(h, b, I))
                dve.drain()
                for I in range(NT):
                    dve.bn_aggr(m2[:rows(I), I, :], s6[:rows(I), I, :])
                dve.drain()
                dve.tensor_scalar(ve[:, :], m2[:, :, 1], EPS, None, ALU.add).then_inc(signal, 1)
                dve.wait_ge(rs_ready, nth(b, 1, 1))
                for I in range(NT):
                    r = rows(I)
                    last = dve.tensor_scalar(dst[:r, I, 0:D], tokens(h, b, I), m2[:r, I, 0:1], rs[:r, I:I + 1],
                                             ALU.subtract, ALU.mult)
                last.then_inc(normed, 1)

            dve.wait_ge(ld_h0, 16 * NT)
            dve.wait_ge(ld_h, 16 * NT)
            dve.wait_ge(embt_done, 1)
            for i in range(B // 2):
                last = dve.tensor_copy(h[0:IMG, 2 * i:2 * i + 2, 0, :],
                                       ps[0:IMG, 2 + i, 0:2 * D].rearrange("p (b d) -> p b d", b=2))
            last.then_inc(embt_copied, 1)
            dve.drain()
            layer_norm(0, st6, mv, veps, ln1_var, rstd, ln1_rstd, xn, ln1_normed)
            dve.wait_ge(aw_hi_ready, 1)
            dve.tensor_tensor(aw_lo[:, :, :], aw_raw[:, :, :], aw_hi[:, :, :], ALU.subtract).then_inc(aw_lo_ready, 1)
            dve.wait_ge(ld_decay, 16)

            def sub(dst, src, hi):
                return dve.tensor_tensor(dst, src, hi, ALU.subtract)

            def halves(bank, p0=0):
                return ps[p0:P, bank:bank + 2, 0:HALF]

            def two(ap):
                return ap.rearrange("p (a n) -> p a n", a=2)

            def x_ext(b):
                dve.wait_ge(xt_done, nth(b, 1, 1))
                for bank in (0, 2):
                    dve.memset(ps[:, bank + 1, LAST:SUMS], 0.0)
                    last = dve.tensor_reduce(ps[:, bank + 1, SUMS:KEY_LAST],
                                             ps[:, bank, :].rearrange("p (t n) -> p t n", n=P), AX.X, ALU.add)
                last.then_inc(xt_ext, 1)

            def x_lo(b):
                dve.wait_ge(xt_hi, nth(b, 2, 1))
                sub(xa_lo[:, :], psf[:, 0:LX], xa_hi[:, :]).then_inc(xt_lo, 1)
                dve.wait_ge(xt_hi, nth(b, 2, 2))
                sub(xb[HD:P, :], psf[HD:P, 1024:1024 + LX], xb[HD:P, :]).then_inc(xt_lo, 1)

            def qk_rest(b):
                for i, (dst, hi, bank) in enumerate(((q01_lo, q01_hi, 4), (q2, q2, 0), (k01_lo, k01_hi, 6), (k2_lo, k2_hi, 2))):
                    p0 = HD if dst is q2 else 0
                    dve.wait_ge(qk_hi, nth(b, 4, i + 1))
                    sub(two(dst[p0:P, :]), halves(bank, p0), two(hi[p0:P, :])).then_inc(qk_lo, 1)

            def apply_decay(b, hh):
                s = hh % 2
                for I in range(NT):
                    r, n = rows(I), L - P * I
                    if I <= 2:
                        dve.wait_ge(s_done, nth(b, 3 * H, 3 * hh + I + 1))
                        apart(dve, "dve")
                    dst, tab = sc[s][:r, OFF[I]:OFF[I] + n], decay[:r, hh, 0:n]
                    if I == 0:
                        dst, tab, src = two(dst), two(tab), ps[:, 0:2, 0:HALF]
                    elif I == 1:
                        src = ps[:, 2, 0:n]
                    else:
                        src = ps[:r, 3, S_AT[I]:S_AT[I] + n]
                    dve.tensor_tensor_reduce(out=dst, in0=src, in1=tab, scale=1.0 / 8, scalar=0.0 if I else NEG,
                                             op0=ALU.mult, op1=ALU.max,
                                             accum_out=mx[s][:r, I:I + 1]).then_inc(decayed, 1)
                dve.drain()
                dve.tensor_scalar(nm[s][:, :], mx[s][:, :], -1.0, None, ALU.mult).then_inc(nm_ready, 1)

            def denominators(b, hh):
                s = hh % 2
                dve.wait_ge(exp_done, nth(b, H, hh + 1))
                dve.tensor_tensor(den[s][:, :], zero_score[s][:, :], lower_count[:, :], ALU.mult)
                dve.drain()
                dve.tensor_tensor(den[s][:, :], den[s][:, :], row_sum[s][:, :], ALU.add)
                dve.drain()
                dve.reciprocal(inv_den[s][:, :], den[s][:, :]).then_inc(den_ready, 1)

            def pt_copy(b, hh):
                s = hh % 2
                dve.wait_ge(pt_done, nth(b, 4 * H, 4 * hh + 1))
                dve.tensor_copy(pt[s][:KEY_LAST, 0, :], ps[:KEY_LAST, 4, :]).then_inc(pt_dve, 1)
                dve.wait_ge(pt_done, nth(b, 4 * H, 4 * hh + 3))
                dve.tensor_copy(pt[s][:, 2, :], ps[:, 4, :]).then_inc(pt_dve, 1)

            def gn_partial(t):
                dve.wait_ge(o_copied, nth(t, 2, 2))
                for i in range(2):
                    for j in range(2):
                        dve.bn_stats(gst[:, i, 6 * j:6 * j + 6], ot[:, i, j * HALF:(j + 1) * HALF])
                dve.drain()
                for i in range(2):
                    dve.bn_aggr(gmv[:, i, :], gst[:, i, :])
                dve.drain()
                dve.tensor_tensor(gtmp[:, :], gmv[:, :, 0], gmv[:, :, 0], ALU.mult)
                dve.drain()
                dve.tensor_tensor(gmv[:, :, 1], gmv[:, :, 1], gtmp[:, :], ALU.add).then_inc(gn_part, 1)

            def gn_variance(t):
                dve.wait_ge(gn_sum, nth(t, 1, 1))
                dve.tensor_copy(gtot[:, :, :], ps[:, 7, 0:4].rearrange("p (i k) -> p i k", i=2))
                dve.drain()
                dve.tensor_tensor(gtmp[:, :], gtot[:, :, 0], gtot[:, :, 0], ALU.mult)
                dve.drain()
                dve.tensor_tensor(gvar[:, :], gtot[:, :, 1], gtmp[:, :], ALU.subtract)
                dve.drain()
                dve.tensor_scalar(gvar[:, :], gvar[:, :], 0.0, EPS, ALU.max, ALU.add).then_inc(gn_var, 1)

            def gn_apply(t):
                dve.wait_ge(gn_rstd, nth(t, 1, 1))
                dve.tensor_tensor(gscale[:, :], grstd[:, :], gnw[:, :], ALU.mult)
                dve.drain()
                dve.tensor_tensor(gtmp[:, :], gtot[:, :, 0], gscale[:, :], ALU.mult)
                dve.drain()
                dve.tensor_tensor(gshift[:, :], gnb[:, :], gtmp[:, :], ALU.subtract)
                dve.drain()
                for i in range(2):
                    dve.tensor_scalar(y[:, i, :], ot[:, i, :], gscale[:, i:i + 1], gshift[:, i:i + 1],
                                      ALU.mult, ALU.add).then_inc(y_ready, 1)

            def y_rest(t):
                dve.wait_ge(y_hi, nth(t, 2, 1))
                sub(y01_lo[:, :], y[:, 0, :], y01_hi[:, :]).then_inc(y_lo, 1)
                dve.wait_ge(y_hi, nth(t, 2, 2))
                sub(y2[HD:P, :], y[HD:P, 1, :], y2[HD:P, :]).then_inc(y_lo, 1)

            def add_attention(t):
                for i, (bank, t0, n) in enumerate(((4, 0, 2), (5, 2, 2), (6, 4, 1))):
                    r = P if n == 2 else LAST
                    dve.wait_ge(wo_done, nth(t, 3, i + 1))
                    dst = h[:r, bass.ds(t, 1), t0:t0 + n, :].rearrange("p a t d -> p (a t) d")
                    src = ps[:r, bank, 0:256 * n].rearrange("p (t d) -> p t d", t=n)[:, :, 0:D]
                    dve.tensor_tensor(dst, src, dst, ALU.add).then_inc(wo_added, 1)
                dve.drain()
                layer_norm(t, st6b, mvb, vepsb, ln2_var, rstdb, ln2_rstd, xn2, ln2_normed)

            def x2_rest(t):
                dve.wait_ge(x2_hi, nth(t, 3, 1))
                sub(x2[:, 1, 0:512], ps[:, 4, :], x2[:, 0, 0:512]).then_inc(x2_lo, 1)
                dve.wait_ge(x2_hi, nth(t, 3, 2))
                sub(x2[HD:P, 2, 0:512], ps[HD:P, 5, :], x2[HD:P, 2, 0:512]).then_inc(x2_lo, 1)
                dve.wait_ge(x2_hi, nth(t, 3, 3))
                sub(x2[:, 1, 512:L], ps[:, 4, 0:LAST], x2[:, 0, 512:L])
                sub(x2[HD:P, 2, 512:L], ps[HD:P, 4, 64:64 + LAST], x2[HD:P, 2, 512:L]).then_inc(x2_lo, 1)

            def wide(ap, n):
                return ap.unsqueeze(2).broadcast_to([P, NT, n])

            def router_shift(t):
                dve.wait_ge(lgn_done, nth(t, 1, 1))
                logits = ps[:, 5, 0:NT * E].rearrange("p (t e) -> p t e", t=NT)
                dve.tensor_reduce(lmax[:, :], logits, AX.X, ALU.max)
                dve.drain()
                dve.tensor_tensor(lsub[:, :, :], logits, wide(lmax[:, :], E), ALU.subtract).then_inc(l_sub, 1)

            def router_choose(t):
                dve.wait_ge(l_exp, nth(t, 1, 1))
                apart(dve, "dve")
                for I in range(NT):
                    dve.max(top[:, I, :], lexp[:, I, :])
                dve.drain()
                for I in range(NT):
                    dve.match_replace(left[:, I, :], top[:, I, :], lexp[:, I, :], -1.0)
                dve.tensor_reduce(tsum[:, :], top[:, :, :], AX.X, ALU.add)
                dve.drain()
                dve.reciprocal(tinv[:, :], tsum[:, :])
                dve.tensor_scalar(left[:, :, :], left[:, :, :], 0.0, None, ALU.is_lt)
                dve.drain()
                dve.tensor_tensor(chosen[:, :, :], left[:, :, :], lexp[:, :, :], ALU.mult)
                dve.drain()
                dve.tensor_tensor(comb[:, :, :], chosen[:, :, :], wide(tinv[:, :], E), ALU.mult).then_inc(comb_ready, 1)

            def body(b, tail, head, more):
                t = b - 1
                if tail:
                    gn_partial(t)
                if head:
                    x_ext(b)
                    x_lo(b)
                    qk_rest(b)
                if tail:
                    gn_variance(t)
                if head:
                    apply_decay(b, 0)
                if tail:
                    gn_apply(t)
                if head:
                    apply_decay(b, 1)
                if tail:
                    y_rest(t)
                if head:
                    denominators(b, 0)
                if tail:
                    add_attention(t)
                if head:
                    denominators(b, 1)
                    pt_copy(b, 0)
                    apply_decay(b, 2)
                if tail:
                    x2_rest(t)
                if head:
                    pt_copy(b, 1)
                    denominators(b, 2)
                if tail:
                    router_shift(t)
                if head:
                    pt_copy(b, 2)
                if tail:
                    router_choose(t)
                if more:
                    layer_norm(b + 1, st6, mv, veps, ln1_var, rstd, ln1_rstd, xn, ln1_normed)

            batches(dve, body)
            end_of_phase_a(dve)

            dve.wait_ge(w_hi_ready, 1)
            sub(w1_lo[:, :, :], w1_raw[:, :, :], w1_hi[:, :, :])
            sub(w2_lo[:, :, :], w2_raw[:, :, 0:P], w2_hi[:, :, :])
            sub(w2_r[:, :, HD:P], w2_raw[:, :, P + HD:256], w2_r[:, :, HD:P]).then_inc(w_lo_ready, 1)

            def weigh(b, k):
                e = TILE_E[k]
                dve.wait_ge(gelu_done, nth(b, NW, k + 1))
                dve.wait_ge(ld_gate[e % 4], 16 * (b * (E // 4) + e // 4 + 1))
                dve.tensor_tensor(act[k % 3][:, :, :], act[k % 3][:, :, :], gate[e % 4][:, :, :],
                                  ALU.mult).then_inc(gated, 1)

            def act_rest(b, k):
                dve.wait_ge(act_hi_ready, nth(b, NW, k + 1))
                sub(act_lo[k % 3][:, :, :], act[k % 3][:, :, :], act_hi[k % 3][:, :, :]).then_inc(act_lo_ready, 1)

            def ffn(b):
                for k in range(NW):
                    weigh(b, k)
                    if k >= 1:
                        act_rest(b, k - 1)
                act_rest(b, NW - 1)
                dve.wait_ge(down_done, nth(b, NW, NW))
                dve.tensor_copy(out_r[:, :].rearrange("p (a n) -> p a n", a=2), ps[:, 6:8, 0:HALF]).then_inc(acc_r_copied, 1)
                dve.wait_ge(outt_done, nth(b, 1, 1))
                for r, t0, n, bank_a, bank_r in ((P, 0, NT - 1, 4, 6), (LAST, NT - 1, 1, 5, 7)):
                    hb = h[:r, bass.ds(b, 1), t0:t0 + n, :].rearrange("p a t d -> p (a t) d")
                    main = ps[:r, bank_a, 0:P * n].rearrange("p (t d) -> p t d", t=n)
                    rest = ps[:r, bank_r, 0:P * n].rearrange("p (t d) -> p t d", t=n)
                    part = out_t[:r, t0:t0 + n, :]
                    dve.tensor_tensor(part, rest[:, :, HD:P], hb[:, :, P:D], ALU.add)
                    dve.tensor_tensor(hb[:, :, 0:P], main, hb[:, :, 0:P], ALU.add)
                    dve.drain()
                    last = dve.tensor_tensor(hb[:, :, P:D], rest[:, :, 0:HD], part, ALU.add)
                last.then_inc(out_ready, 1)

            ffn(0)
            with dve.Fori(1, B) as b:
                ffn(b)

        @block.tensor
        def _(pe):
            def mm(dst, w, x, start, stop):
                return pe.matmul(dst, w, x, start=start, stop=stop)

            def series(dst, pairs):
                for i, (w, x) in enumerate(pairs):
                    last = mm(dst, w, x, i == 0, i == len(pairs) - 1)
                return last

            pe.wait_ge(ld_pat, 48)
            for bank, f0, f1 in ((0, 0, P), (1, P, D)):
                last = series(ps[0:f1 - f0, bank, 0:B * IMG], [(tokw[:, k, f0:f1], pat[:, k, :]) for k in range(KT)])
            last.then_inc(emb_done, 1)
            pe.wait_ge(emb_copied, 1)
            pe.wait_ge(consts, 3)
            for b in range(B):
                at = (b % 2) * D
                pe.transpose(ps[0:IMG, 2 + b // 2, at:at + P], emb[:, 0, b * IMG:(b + 1) * IMG], ident[:, :])
                last = pe.transpose(ps[0:IMG, 2 + b // 2, at + P:at + D], emb[0:HD, 1, b * IMG:(b + 1) * IMG], ident[0:HD, 0:HD])
            last.then_inc(embt_done, 1)
            pe.wait_ge(aw_lo_ready, 1)

            def weights(c0, c1):
                return aw_hi[:, 0, c0:c1], aw_lo[:, 0, c0:c1], aw_hi[:, 1, c0:c1], aw_lo[:, 1, c0:c1]

            def x_transpose(b):
                pe.wait_ge(xn_ready, nth(b, 1, 1))
                if not isinstance(b, int) or b:
                    pe.wait_ge(decayed, nth(b - 1, NT * H, NT * H))
                for I in range(NT):
                    r = rows(I)
                    bank, at = (0, I * P) if I < NT - 1 else (1, 0)
                    pe.transpose(ps[:, bank, at:at + r], xn[:r, I, 0:P], ident[:r, :r])
                    last = pe.transpose(ps[:, bank + 2, at:at + r], xn[:r, I, P:256], ident[:r, :r])
                last.then_inc(xt_done, 1)

            def qk(b, tail):
                pe.wait_ge(xt_lo, nth(b, 2, 2))
                for tile, bank in ((0, 4), (2, 0), (1, 6), (3, 2)):
                    if bank == 4 and tail:
                        pe.wait_ge(pt_dve, nth(b - 1, 2 * H, 2 * H))
                        pe.wait_ge(pt_act, nth(b - 1, 2 * H, 2 * H))
                        pe.wait_ge(ct_copied, CREDIT + b - 1)
                    if bank == 6 and tail:
                        pe.wait_ge(o_copied, nth(b - 1, 2, 2))
                    ah, al, bh, bl = weights(tile * P, (tile + 1) * P)
                    for n in range(2):
                        c = slice(n * HALF, (n + 1) * HALF)
                        last = series(ps[:, bank + n, 0:HALF],
                                      [(ah, xa_hi[:, c]), (al, xa_hi[:, c]), (ah, xa_lo[:, c]), (bh, xb[:, c]), (bl, xb[:, c])])
                    last.then_inc(qk_done, 1)

            def values(b):
                ah, al, bh, bl = weights(QK_W, QK_W + V_W)
                pe.wait_ge(qk_lo, nth(b, 4, 1))
                for I in range(NT):
                    if I == NT - 1:
                        pe.wait_ge(qk_lo, nth(b, 4, 3))
                    r = P if I < NT - 1 else KEY_LAST
                    c = slice(I * P, I * P + r)
                    at = (I % 2) * 256
                    last = series(ps[:r, 4 + I // 2, at:at + 256],
                                  [(xa_hi[:, c], ah), (xa_hi[:, c], al), (xa_lo[:, c], ah), (xb[:, c], bh), (xb[:, c], bl)])
                    if I in (1, 3, 4):
                        last.then_inc(v_done, 1)

            def scores(b, hh):
                if hh < 2:
                    g = slice(HD * hh, HD * hh + HD)
                    pairs = ((q01_hi, k01_hi), (q01_hi, k01_lo), (q01_lo, k01_hi))
                else:
                    g = slice(0, P)
                    pairs = ((q2, k2_hi), (q2, k2_lo))
                for I in range(NT):
                    if hh == 0 and I == 0:
                        pe.wait_ge(qk_lo, nth(b, 4, 4))
                    elif hh and I in (0, 1, 2):
                        k = (hh - 1) * NT + (1, 2, NT)[I]
                        pe.wait_ge(decayed, nth(b, NT * H, k))
                    r, n = rows(I), L - P * I
                    q = slice(I * P, I * P + r)
                    if I == 0:
                        parts = [(ps[:, 0, 0:HALF], 0, HALF), (ps[:, 1, 0:HALF], HALF, L)]
                    elif I == 1:
                        parts = [(ps[:, 2, 0:n], P, L)]
                    else:
                        parts = [(ps[:r, 3, S_AT[I]:S_AT[I] + n], I * P, L)]
                    for dst, m0, m1 in parts:
                        last = series(dst, [(a_[g, q], b_[g, m0:m1]) for a_, b_ in pairs])
                    if I in (0, 1, 4):
                        last.then_inc(s_done, 1)

            def gn_sums(b, head):
                if head:
                    pe.wait_ge(qk_lo, nth(b, 4, 3))
                pe.wait_ge(gn_part, nth(b - 1, 1, 1))
                mm(ps[:, 7, 0:4], head_mean[:, :], gmv[:, :, :].rearrange("p i k -> p (i k)"), True, True).then_inc(gn_sum, 1)

            def project(b, head):
                t = b - 1
                ah, al, bh, bl = weights(QK_W + V_W, QK_W + V_W + O_W)
                pe.wait_ge(y_lo, nth(t, 2, 2))
                if head:
                    pe.wait_ge(v_copied, nth(b, 3, 3))
                else:
                    pe.wait_ge(ct_copied, CREDIT + t)
                for I in range(NT):
                    r = rows(I)
                    c = slice(I * P, I * P + r)
                    at = (I % 2) * 256
                    last = series(ps[:r, 4 + I // 2, at:at + D],
                                  [(y01_hi[:, c], ah), (y01_hi[:, c], al), (y01_lo[:, c], ah), (y2[:, c], bh), (y2[:, c], bl)])
                    if I in (1, 3, 4):
                        last.then_inc(wo_done, 1)

            def probs_transpose(b, hh, tail):
                s = hh % 2
                pe.wait_ge(probs_ready, nth(b, H, hh + 1))

                def tile(dst, I, J):
                    n = P if J < NT - 1 else KEY_LAST
                    r, at = rows(I), OFF[I] + (J - I) * P
                    return pe.transpose(dst, pr[s][:r, at:at + n], ident[:r, :r])

                if hh == 0:
                    pe.wait_ge(v_copied, nth(b, 3, 3))
                    if tail:
                        pe.wait_ge(wo_added, nth(b - 1, 3, 3))
                else:
                    pe.wait_ge(pt_dve, nth(b, 2 * H, 2 * hh))
                    pe.wait_ge(pt_act, nth(b, 2 * H, 2 * hh))
                    if tail and hh == 1:
                        pe.wait_ge(x2_lo, nth(b - 1, 3, 3))
                    if tail and hh == 2:
                        pe.wait_ge(lt_copied, nth(b - 1, 1, 1))
                        pe.wait_ge(l_sub, nth(b - 1, 1, 1))
                for I in range(NT - 1):
                    last = tile(ps[:KEY_LAST, 4, I * P:(I + 1) * P], I, NT - 1)
                last.then_inc(pt_done, 1)
                tile(ps[:KEY_LAST, 5, 0:LAST], NT - 1, NT - 1)
                for I in range(3):
                    last = tile(ps[:, 5, 64 + I * P:64 + (I + 1) * P], I, 2)
                last.then_inc(pt_done, 1)
                pe.wait_ge(pt_dve, nth(b, 2 * H, 2 * hh + 1))
                for I in range(4):
                    last = tile(ps[:, 4, I * P:(I + 1) * P], I, 3)
                last.then_inc(pt_done, 1)
                pe.wait_ge(pt_act, nth(b, 2 * H, 2 * hh + 1))
                for I in range(2):
                    tile(ps[:, 5, I * P:(I + 1) * P], I, 1)
                tile(ps[:, 5, 2 * P:3 * P], 0, 0).then_inc(pt_done, 1)

            def attend(b, hh):
                s, first, last_head = hh % 2, hh != 1, hh != 0
                tail = 64 if hh == 2 else 0
                if hh == 2:
                    pe.wait_ge(o_copied, nth(b, 2, 1))
                pe.wait_ge(pt_act, nth(b, 2 * H, 2 * hh + 2))
                pe.wait_ge(pt_dve, nth(b, 2 * H, 2 * hh + 2))
                cols = slice(hh * P, (hh + 1) * P)
                mm(ps[:, 6, :], v[:KEY_LAST, 4, cols], pt[s][:KEY_LAST, 0, :], first, False)
                mm(ps[:, 7, tail:tail + LAST], v[:KEY_LAST, 4, cols], pt[s][:KEY_LAST, 1, 0:LAST], first, last_head)
                mm(ps[:, 6, :], v[:, 3, cols], pt[s][:, 2, :], False, False)
                mm(ps[:, 6, 0:3 * P], v[:, 2, cols], pt[s][:, 1, 64:64 + 3 * P], False, False)
                mm(ps[:, 6, 0:2 * P], v[:, 1, cols], pt[s][:, 3, 0:2 * P], False, False)
                last = mm(ps[:, 6, 0:P], v[:, 0, cols], pt[s][:, 3, 2 * P:3 * P], False, last_head)
                if last_head:
                    last.then_inc(o_done, 1)

            def x2_transpose(b, head):
                t = b - 1
                pe.wait_ge(xn2_ready, nth(t, 1, 1))
                if head:
                    pe.wait_ge(pt_dve, nth(b, 2 * H, 2))
                    pe.wait_ge(pt_act, nth(b, 2 * H, 2))
                else:
                    pe.wait_ge(wo_added, nth(t, 3, 3))
                for c, bank in ((0, 4), (1, 5)):
                    for I in range(NT - 1):
                        last = pe.transpose(ps[:, bank, I * P:(I + 1) * P], xn2[:, I, c * P:(c + 1) * P], ident[:, :])
                    last.then_inc(x2t_done, 1)
                pe.wait_ge(x2_lo, nth(t, 3, 1))
                apart(pe, "pe")
                for c in range(2):
                    last = pe.transpose(ps[:, 4, 64 * c:64 * c + LAST], xn2[:LAST, NT - 1, c * P:(c + 1) * P], ident[:LAST, :LAST])
                last.then_inc(x2t_done, 1)

            def logits(b, head):
                t = b - 1
                ah, al, bh, bl = weights(QK_W + V_W + O_W, AW)
                pe.wait_ge(x2_lo, nth(t, 3, 3))
                if head:
                    pe.wait_ge(pt_act, nth(b, 2 * H, 4))
                    pe.wait_ge(pt_dve, nth(b, 2 * H, 4))
                for n, bank in ((0, 5), (1, 4)):
                    c = slice(n * HALF, (n + 1) * HALF)
                    last = series(ps[0:E, bank, 0:HALF],
                                  [(ah, x2[:, 0, c]), (al, x2[:, 0, c]), (ah, x2[:, 1, c]), (bh, x2[:, 2, c]), (bl, x2[:, 2, c])])
                last.then_inc(lg_done, 1)

            def logits_transpose(t):
                pe.wait_ge(lt_copied, nth(t, 1, 1))
                apart(pe, "pe")
                for I in range(NT):
                    last = pe.transpose(ps[:, 5, I * E:(I + 1) * E], lt[:, I * P:(I + 1) * P], ident[0:E, 0:E])
                last.then_inc(lgn_done, 1)

            def comb_transpose(b, head):
                t = b - 1
                pe.wait_ge(comb_ready, nth(t, 1, 1))
                if head:
                    pe.wait_ge(pt_dve, nth(b, 2 * H, 2 * H))
                    pe.wait_ge(pt_act, nth(b, 2 * H, 2 * H))
                for I in range(NT):
                    bank, at = (4, I * P) if I < NT - 1 else (5, 0)
                    last = pe.transpose(ps[0:E, bank, at:at + P], comb[:, I, :], ident[:, :])
                last.then_inc(ct_done, 1)

            def body(b, tail, head, more):
                if head:
                    x_transpose(b)
                    qk(b, tail)
                    values(b)
                if tail:
                    gn_sums(b, head)
                if head:
                    scores(b, 0)
                    scores(b, 1)
                if tail:
                    project(b, head)
                if head:
                    probs_transpose(b, 0, tail)
                    attend(b, 0)
                    scores(b, 2)
                if tail:
                    x2_transpose(b, head)
                if head:
                    probs_transpose(b, 1, tail)
                if tail:
                    logits(b, head)
                if head:
                    attend(b, 1)
                if tail:
                    logits_transpose(b - 1)
                if head:
                    probs_transpose(b, 2, tail)
                    attend(b, 2)
                if tail:
                    comb_transpose(b, head)

            batches(pe, body)
            end_of_phase_a(pe)

            pe.wait_ge(w_lo_ready, 1)

            def up(b, k):
                if k == 0:
                    pe.wait_ge(ld_x2, 16 * (b + 1))
                if k >= 2 or not isinstance(b, int) or b:
                    pe.wait_ge(gelu_done, nth(b, NW, k - 1))
                w = slice(k * P, (k + 1) * P)
                for n in range(2):
                    def x(c):
                        return x2_all[:, c, bass.ds(b, 1), n * HALF:(n + 1) * HALF].rearrange("p a n -> p (a n)")
                    last = series(ps[:, 2 * (k % 2) + n, 0:HALF],
                                  [(w1_hi[:, 0, w], x(0)), (w1_lo[:, 0, w], x(0)), (w1_hi[:, 0, w], x(1)),
                                   (w1_hi[:, 1, w], x(2)), (w1_lo[:, 1, w], x(2))])
                last.then_inc(up_done, 1)

            def down(b, k):
                pe.wait_ge(act_lo_ready, nth(b, NW, k + 1))
                if k == 0 and (not isinstance(b, int) or b):
                    pe.wait_ge(out_ready, nth(b - 1, 1, 1))
                first, last_k = k == 0, k == NW - 1
                hi, lo = act_hi[k % 3], act_lo[k % 3]
                for n in range(2):
                    mm(ps[:, 4 + n, 0:HALF], w2_hi[:, k, :], hi[:, n, :], first, False)
                    mm(ps[:, 4 + n, 0:HALF], w2_lo[:, k, :], hi[:, n, :], False, False)
                    mm(ps[:, 4 + n, 0:HALF], w2_hi[:, k, :], lo[:, n, :], False, last_k)
                    mm(ps[:, 6 + n, 0:HALF], w2_r[:, k, :], hi[:, n, :], first, False)
                    last = mm(ps[:, 6 + n, 0:HALF], w2_r[:, k, :], lo[:, n, :], False, last_k)
                last.then_inc(down_done, 1)

            def ffn(b, more):
                for k in range(NW):
                    if k + 2 < NW:
                        up(b, k + 2)
                    elif more:
                        up(b + 1, k + 2 - NW)
                    down(b, k)
                pe.wait_ge(acc_a_copied, nth(b, 1, 1))
                pe.wait_ge(acc_r_copied, nth(b, 1, 1))
                for I in range(NT):
                    r = rows(I)
                    bank, at = (4, I * P) if I < NT - 1 else (5, 0)
                    pe.transpose(ps[:r, bank, at:at + P], out_a[:, I * P:I * P + r], ident[:, :])
                    last = pe.transpose(ps[:r, bank + 2, at:at + P], out_r[:, I * P:I * P + r], ident[:, :])
                last.then_inc(outt_done, 1)

            up(0, 0)
            up(0, 1)
            ffn(0, True)
            with pe.Fori(1, B - 1) as b:
                ffn(b, True)
            ffn(B - 1, False)


S_AT = {2: 0, 3: L - 2 * P, 4: (L - 2 * P) + (L - 3 * P)}


def _stack(np, wt):
    return np.ascontiguousarray(np.stack([wt[0:128], np.concatenate([wt[128:192], wt[128:192]])], axis=1))


def kernel(x, txt, L0_tok_W, L0_tok_b, L0_attn_Wq, L0_attn_Wk, L0_attn_Wv, L0_attn_Wo, L0_attn_gammas,
           L0_attn_gn_weight, L0_attn_gn_bias, L0_ffn_router_w, L0_ffn_w1, L0_ffn_w2):
    import concourse.bacc as bacc
    import numpy as np
    from concourse.bass_utils import run_bass_kernel_spmd

    f = lambda t: np.asarray(t)
    img = f(x).reshape(B, 3, 6, 16, 6, 16).transpose(1, 3, 5, 0, 2, 4).reshape(KT, P, B * IMG)
    wq, wk, wv, wo, wr = f(L0_attn_Wq).T, f(L0_attn_Wk).T, f(L0_attn_Wv).T, f(L0_attn_Wo).T, f(L0_ffn_router_w).T
    q2, k2 = wq[:, 128:], wk[:, 128:]
    attn = np.concatenate([wq[:, 0:128], wk[:, 0:128], q2, q2, k2, k2, wv, wv[:, 128:], wo, wr], axis=1)
    w2 = f(L0_ffn_w2).reshape(NW, P, D).transpose(1, 0, 2)

    def columns(vec):
        return np.stack([vec[0:128], np.concatenate([vec[128:192], vec[128:192]])], axis=1)

    arrays = {
        "patches": img.transpose(1, 0, 2),
        "txt": f(txt),
        "tok_w": f(L0_tok_W).T.reshape(KT, P, D).transpose(1, 0, 2),
        "tok_b": columns(f(L0_tok_b)),
        "gammas": f(L0_attn_gammas),
        "gn_w": columns(f(L0_attn_gn_weight)),
        "gn_b": columns(f(L0_attn_gn_bias)),
        "attn_w": _stack(np, attn),
        "w1": _stack(np, f(L0_ffn_w1)),
        "w2": np.concatenate([w2, w2[:, :, 128:]], axis=2),
    }
    arrays = {n: np.ascontiguousarray(a) for n, a in arrays.items()}
    nc = bacc.Bacc("TRN2", target_bir_lowering=False, num_devices=1)
    args = [nc.dram_tensor(n, a.shape, F32, kind="ExternalInput").ap() for n, a in arrays.items()]
    out = nc.dram_tensor("out", (B, L, D), F32, kind="ExternalOutput").ap()
    early_fusion(nc, *args, out)
    r = run_bass_kernel_spmd(nc, [arrays], core_ids=[0])
    return r.results[0]["out"]
```

```python
from contextlib import ExitStack

import concourse.bass as bass
from concourse import mybir

F32 = mybir.dt.float32
F32R = mybir.dt.float32r
ALU = mybir.AluOpType
ACT = mybir.ActivationFunctionType
AX = mybir.AxisListType

P = 128
B = 8
D = 192
IMG = 36
TXT = 512
L = IMG + TXT
NT = -(-L // P)
LAST = L - (NT - 1) * P
HALF = L // 2
H = 3
HD = D // H
KT = 6
EPS = 1e-5
NEG = -3.0e38

SUMS = 64
KEY_LAST = SUMS + NT - 1
LX = (NT - 1) * P + KEY_LAST
WIDTH = [LX - I * P for I in range(NT)]
OFF = [sum(WIDTH[:I]) for I in range(NT)]
PW = sum(WIDTH)

E = 16
EW = [128] * 8 + [256] * 8
TILE_E = [e for e in range(E) for _ in range(EW[e] // P)]
NW = len(TILE_E)
LAST_OF = [max(k for k in range(NW) if TILE_E[k] == e) for e in range(E)]
TOPK = 8
W1_SHARE = NW * P // B
W2_PART = NW // 4
CREDIT = 1

QK_W, V_W, O_W, R_W = 512, 256, D, E
AW = QK_W + V_W + O_W + R_W
DECAY_L = 127 + L + 1


def rows(I):
    return P if I < NT - 1 else LAST


def nth(b, per, k):
    return b * per + k


def early_fusion(nc, patches, txt, tok_w, tok_b, gammas, gn_w, gn_b, attn_w, w1, w2, out):
    ctx = ExitStack()
    phase_a, staging = ExitStack(), ExitStack()

    def sb(name, shape, dt=F32, scope=ctx):
        return scope.enter_context(nc.sbuf_tensor(name, shape, dt))

    def sem(name):
        return ctx.enter_context(nc.semaphore(name))

    with ctx:
        h = sb("h", [P, B, NT, D])
        ident = sb("ident", [P, P])
        ps = ctx.enter_context(nc.psum_tensor("ps", [P, 8, 512], F32))
        psf = ps[:, :, :].rearrange("p b n -> p (b n)")

        def sg(name, shape, dt=F32):
            return sb(name, shape, dt, staging)

        aw_raw = sg("aw_raw", [P, 2, AW])
        pat, tokw = sg("pat", [P, KT, B * IMG]), sg("tokw", [P, KT, D])
        tokb = sg("tokb", [P, 2])
        emb = sg("emb", [P, 2, B * IMG])
        gam = sg("gam", [P, H])
        drow = sg("drow", [P, H, DECAY_L])
        staging.close()
        w1_hi, w1_lo = sb("w1_hi", [P, 2, NW * P], F32R), sb("w1_lo", [P, 2, NW * P], F32R)
        w_raw = sb("w_raw", [P, W2_PART * 256])
        w1_raw = w_raw[:, 0:2 * W1_SHARE].rearrange("p (c n) -> p c n", c=2)
        w2_first = w_raw[:, :].rearrange("p (k n) -> p k n", k=W2_PART)

        def sa(name, shape, dt=F32):
            return sb(name, shape, dt, phase_a)

        aw_hi, aw_lo = sa("aw_hi", [P, 2, AW], F32R), sa("aw_lo", [P, 2, AW], F32R)
        decay = sa("decay", [P, H, L])
        head_mean = sa("head_mean", [P, P])
        gnw, gnb = sa("gnw", [P, 2]), sa("gnb", [P, 2])
        lower_count = sa("lower_count", [P, NT])
        xn, xn2 = sa("xn", [P, NT, 256]), sa("xn2", [P, NT, 256])
        xa_hi, xa_lo, xb = sa("xa_hi", [P, LX], F32R), sa("xa_lo", [P, LX], F32R), sa("xb", [P, LX], F32R)
        q01_hi, q01_lo = sa("q01_hi", [P, L], F32R), sa("q01_lo", [P, L], F32R)
        k01_hi, k01_lo = sa("k01_hi", [P, L], F32R), sa("k01_lo", [P, L], F32R)
        q2 = sa("q2", [P, L], F32R)
        k2_hi, k2_lo = sa("k2_hi", [P, L], F32R), sa("k2_lo", [P, L], F32R)
        v = sa("v", [P, NT, 3 * P])
        sc = [sa(f"sc{i}", [P, PW]) for i in range(2)]
        pr = [sa(f"pr{i}", [P, PW]) for i in range(2)]
        pt = sa("pt", [P, 4, 512])
        ot = sa("ot", [P, 2, L])
        y01_hi, y01_lo, y2 = sa("y01_hi", [P, L], F32R), sa("y01_lo", [P, L], F32R), sa("y2", [P, L], F32R)
        x2 = sa("x2", [P, 3, L], F32R)
        lt = sa("lt", [E, NT * P])
        ct = sa("ct", [E, NT * P])
        st6, mv, veps = sa("st6", [P, NT, 6]), sa("mv", [P, NT, 2]), sa("veps", [P, NT])
        rstd = sa("rstd", [P, NT])
        st6b, mvb, vepsb, rstdb = sa("st6b", [P, NT, 6]), sa("mvb", [P, NT, 2]), sa("vepsb", [P, NT]), sa("rstdb", [P, NT])
        neg_half = sa("neg_half", [P, NT])
        mx = [sa(f"mx{i}", [P, NT]) for i in range(2)]
        nm = [sa(f"nm{i}", [P, NT]) for i in range(2)]
        zero_score = [sa(f"zero_score{i}", [P, NT]) for i in range(2)]
        row_sum = [sa(f"row_sum{i}", [P, NT]) for i in range(2)]
        den = [sa(f"den{i}", [P, NT]) for i in range(2)]
        inv_den = [sa(f"inv_den{i}", [P, NT]) for i in range(2)]
        gst, gmv, gtot = sa("gst", [P, 2, 12]), sa("gmv", [P, 2, 2]), sa("gtot", [P, 2, 2])
        gvar, grstd = sa("gvar", [P, 2]), sa("grstd", [P, 2])
        gscale, gshift, gtmp = sa("gscale", [P, 2]), sa("gshift", [P, 2]), sa("gtmp", [P, 2])
        lmax, lsub, lexp = sa("lmax", [P, NT]), sa("lsub", [P, NT, E]), sa("lexp", [P, NT, E])
        top, left = sa("top", [P, NT, TOPK]), sa("left", [P, NT, E])
        chosen, tsum, tinv, comb = sa("chosen", [P, NT, E]), sa("tsum", [P, NT]), sa("tinv", [P, NT]), sa("comb", [P, NT, E])
        phase_a.close()

        w2_hi, w2_lo = sb("w2_hi", [P, NW, P], F32R), sb("w2_lo", [P, NW, P], F32R)
        w2_r = sb("w2_r", [P, NW, P], F32R)
        w2_staging = ExitStack()
        sb("x2_first", [P, B - 3, 3, L], F32, w2_staging)
        w2_others = sb("w2_others", [P, NW - W2_PART, 256], F32, w2_staging)
        w2_staging.close()
        x2_all = sb("x2_all", [P, B, 3, L], F32R)
        act = [sb(f"act{i}", [P, 2, HALF]) for i in range(3)]
        act_hi = [sb(f"act_hi{i}", [P, 2, HALF], F32R) for i in range(3)]
        act_lo = [sb(f"act_lo{i}", [P, 2, HALF], F32R) for i in range(3)]
        gate = [sb(f"gate{i}", [P, 2, HALF]) for i in range(4)]
        out_a, out_r, out_t = sb("out_a", [P, L]), sb("out_r", [P, L]), sb("out_t", [P, NT, HD])

        decay_rows = nc.dram_tensor("decay_rows", [H, P * DECAY_L], F32).ap()
        x2_dram = nc.dram_tensor("x2_dram", [B, P, 3 * L], F32).ap()
        comb_dram = nc.dram_tensor("comb_dram", [B, E, L], F32).ap()

        ld_aw, ld_pat, ld_small = sem("ld_aw"), sem("ld_pat"), sem("ld_small")
        ld_h0, ld_h = sem("ld_h0"), sem("ld_h")
        consts = sem("consts")
        decay_built, decay_stored, ld_decay = sem("decay_built"), sem("decay_stored"), sem("ld_decay")
        aw_hi_ready, aw_lo_ready = sem("aw_hi_ready"), sem("aw_lo_ready")
        emb_done, emb_copied, embt_done, embt_copied = sem("emb_done"), sem("emb_copied"), sem("embt_done"), sem("embt_copied")
        ln1_var, ln1_rstd, ln1_normed, xn_ready = sem("ln1_var"), sem("ln1_rstd"), sem("ln1_normed"), sem("xn_ready")
        ln2_rstd, ln2_normed = sem("ln2_rstd"), sem("ln2_normed")
        xt_done, xt_ext, xt_hi, xt_lo = sem("xt_done"), sem("xt_ext"), sem("xt_hi"), sem("xt_lo")
        qk_done, qk_hi, qk_lo = sem("qk_done"), sem("qk_hi"), sem("qk_lo")
        v_done, v_copied = sem("v_done"), sem("v_copied")
        s_done, decayed, nm_ready = sem("s_done"), sem("decayed"), sem("nm_ready")
        exp_done, den_ready, probs_ready = sem("exp_done"), sem("den_ready"), sem("probs_ready")
        pt_done, pt_copied = sem("pt_done"), sem("pt_copied")
        o_done, o_copied = sem("o_done"), sem("o_copied")
        gn_part, gn_sum, gn_var, gn_rstd = sem("gn_part"), sem("gn_sum"), sem("gn_var"), sem("gn_rstd")
        y_coeff, y_hi, y_lo = sem("y_coeff"), sem("y_hi"), sem("y_lo")
        wo_done, wo_added, ln2_var, xn2_ready = sem("wo_done"), sem("wo_added"), sem("ln2_var"), sem("xn2_ready")
        x2t_done, x2_hi, x2_lo, x2_stored = sem("x2t_done"), sem("x2_hi"), sem("x2_lo"), sem("x2_stored")
        lg_done, lt_copied, lgn_done, l_sub, l_exp = sem("lg_done"), sem("lt_copied"), sem("lgn_done"), sem("l_sub"), sem("l_exp")
        comb_ready, ct_done, ct_copied, ct_stored = sem("comb_ready"), sem("ct_done"), sem("ct_copied"), sem("ct_stored")
        phase = sem("phase")
        tick = {n: sem(f"tick_{n}") for n in ("dve", "pool", "pe")}
        ld_w1, ld_w2, w1_split = sem("ld_w1"), sem("ld_w2"), sem("w1_split")
        w2_hi_ready, w2_lo_ready = sem("w2_hi_ready"), sem("w2_lo_ready")
        ld_x2, ld_gate = sem("ld_x2"), [sem(f"ld_gate{i}") for i in range(4)]
        up_done, gelu_done, gated, act_hi_ready, act_lo_ready = sem("up_done"), sem("gelu_done"), sem("gated"), sem("act_hi_ready"), sem("act_lo_ready")
        down_done, acc_a_copied, acc_r_copied = sem("down_done"), sem("acc_a_copied"), sem("acc_r_copied")
        outt_done, out_ready, out_stored = sem("outt_done"), sem("out_ready"), sem("out_stored")

        block = ctx.enter_context(nc.Block())

        def apart(eng, name):
            eng.sem_inc(tick[name], 1)

        def iterations(eng, body):
            body(0, head=True, tail=False, router=False, more=True)
            body(1, head=True, tail=True, router=False, more=True)
            with eng.Fori(2, B - 1) as b:
                body(b, head=True, tail=True, router=True, more=True)
            body(B - 1, head=True, tail=True, router=True, more=False)
            body(B, head=False, tail=True, router=True, more=False)
            body(B + 1, head=False, tail=False, router=True, more=False)

        def end_of_phase_a(eng):
            eng.drain().then_inc(phase, 1)
            eng.wait_ge(phase, 5)

        def tokens(ap, b, I):
            return ap[:rows(I), bass.ds(b, 1), I, :].rearrange("p a d -> p (a d)")

        @block.sync
        def _(sp):
            def load_h(b0, b1, s):
                src = txt[b0:b1]
                sp.dma_start(h[IMG:P, b0:b1, 0, :], src[:, 0:P - IMG, :].rearrange("b p d -> p b d")).then_inc(s, 16)
                for I in range(1, NT - 1):
                    lo = I * P - IMG
                    sp.dma_start(h[:, b0:b1, I, :], src[:, lo:lo + P, :].rearrange("b p d -> p b d")).then_inc(s, 16)
                sp.dma_start(h[0:LAST, b0:b1, NT - 1, :], src[:, TXT - LAST:TXT, :].rearrange("b p d -> p b d")).then_inc(s, 16)

            sp.dma_start(gam[:, :], gammas.partition_broadcast(P)).then_inc(ld_small, 16)
            sp.dma_start(pat[:, :, :], patches).then_inc(ld_pat, 16)
            sp.dma_start(tokw[:, :, :], tok_w).then_inc(ld_pat, 16)
            sp.dma_start(tokb[:, :], tok_b).then_inc(ld_pat, 16)
            load_h(0, 1, ld_h0)
            sp.dma_start(aw_raw[:, :, :], attn_w).then_inc(ld_aw, 16)
            load_h(1, B, ld_h)
            sp.dma_start(w1_raw, w1[:, :, 0:W1_SHARE]).then_inc(ld_w1, 16)
            sp.dma_start(gnw[:, :], gn_w).then_inc(ld_small, 16)
            sp.dma_start(gnb[:, :], gn_b).then_inc(ld_small, 16)
            sp.wait_ge(decay_built, 1)
            sp.dma_start(decay_rows.rearrange("h (p l) -> p h l", l=DECAY_L), drow[:, :, :]).then_inc(decay_stored, 16)
            sp.wait_ge(decay_stored, 16)
            shifted = decay_rows[:, 127:127 + P * (DECAY_L - 1)].rearrange("h (p l) -> p h l", l=DECAY_L - 1)
            sp.dma_start(decay[:, :, :], shifted[:, :, 0:L]).then_inc(ld_decay, 16)

            def stores(b, head, tail, router, more):
                if head:
                    sp.wait_ge(w1_split, nth(b, 1, 1))
                    if more:
                        sp.dma_start(w1_raw, w1[:, :, bass.ds((b + 1) * W1_SHARE, W1_SHARE)]).then_inc(ld_w1, 16)
                    else:
                        sp.dma_start(w2_first, w2[:, 0:W2_PART, :]).then_inc(ld_w2, 16)
                if router:
                    u = b - 2
                    sp.wait_ge(ct_copied, CREDIT + nth(u, 1, 1))
                    sp.dma_start(comb_dram[bass.ds(u, 1), :, :].rearrange("a e n -> e (a n)"),
                                 ct[:, 0:L]).then_inc(ct_stored, 16)
                if tail:
                    t = b - 1
                    sp.wait_ge(x2_lo, nth(t, 3, 3))
                    sp.dma_start(x2_dram[bass.ds(t, 1), :, :].rearrange("a p n -> p (a n)"),
                                 x2[:, :, :].rearrange("p c n -> p (c n)").bitcast(F32)).then_inc(x2_stored, 16)

            iterations(sp, stores)
            sp.wait_ge(x2_stored, CREDIT + 16 * B)
            sp.wait_ge(ct_stored, CREDIT + 16 * B)
            end_of_phase_a(sp)
            def load_x2(b):
                if b:
                    sp.wait_ge(ld_x2, 16 * b)
                sp.dma_start(x2_all[:, b, :, :].bitcast(F32), x2_dram[b].rearrange("p (c n) -> p c n", c=3)).then_inc(ld_x2, 16)

            load_x2(0)
            for e in range(4):
                sp.dma_start(gate[e][:, :, :].rearrange("p a n -> p (a n)"),
                             comb_dram[0, e, :].partition_broadcast(P)).then_inc(ld_gate[e], 16)
            sp.wait_ge(ld_w2, 16)
            sp.dma_start(w2_others[:, :, :], w2[:, W2_PART:NW, :]).then_inc(ld_w2, 16)
            for b in range(1, B - 3):
                load_x2(b)

            def gates(b, first):
                for e in range(first, E):
                    last = LAST_OF[(e - 4) % E] + 1
                    sp.wait_ge(gated, nth(b, NW, last) if e >= 4 else nth(b - 1, NW, last))
                    src = comb_dram[bass.ds(b, 1), e, :].rearrange("a n -> (a n)").partition_broadcast(P)
                    sp.dma_start(gate[e % 4][:, :, :].rearrange("p a n -> p (a n)"), src).then_inc(ld_gate[e % 4], 16)

            def store_out(b):
                sp.wait_ge(out_ready, nth(b, 1, 1))
                dst = out[bass.ds(b, 1), :, :].rearrange("a n d -> (a n) d")
                src = h[:, bass.ds(b, 1), :, :].rearrange("p a t d -> p (a t) d")
                sp.dma_start(dst[0:(NT - 1) * P, :].rearrange("(t p) d -> p t d", p=P), src[:, 0:NT - 1, :]).then_inc(out_stored, 16)
                sp.dma_start(dst[(NT - 1) * P:L, :], src[0:LAST, NT - 1, :]).then_inc(out_stored, 16)

            gates(0, 4)
            sp.wait_ge(w2_lo_ready, NW // W2_PART)
            for b in range(B - 3, B):
                load_x2(b)
            with sp.Fori(1, B) as b:
                gates(b, 0)
                store_out(b - 1)
            store_out(B - 1)
            sp.wait_ge(out_stored, 32 * B)

        @block.gpsimd
        def _(pool):
            pool.memset(ident[:, :], 0.0)
            pool.drain()
            pool.affine_select(out=ident[:, :], in_=ident[:, :], compare_op=ALU.not_equal, fill=1.0,
                               base=0, pattern=[[-1, P]], channel_multiplier=1).then_inc(consts, 1)
            pool.memset(neg_half[:, :], -0.5).then_inc(consts, 1)
            pool.drain()

            def rstd_of(b, var_sem, rs, ve, ready):
                pool.wait_ge(var_sem, nth(b, 1, 1))
                pool.tensor_tensor(rs[:, :], ve[:, :], neg_half[:, :], ALU.pow).then_inc(ready, 1)

            def twice(b, normed, dst, ready):
                pool.wait_ge(normed, nth(b, 1, 1))
                apart(pool, "pool")
                pool.tensor_copy(dst[:, :, D:256], dst[:, :, P:D]).then_inc(ready, 1)

            def halve_w1(b):
                pool.wait_ge(ld_w1, nth(b, 16, 16))
                apart(pool, "pool")
                if isinstance(b, int) and b == 0:
                    pool.wait_ge(aw_lo_ready, 1)
                    pool.wait_ge(embt_copied, 1)
                    pool.wait_ge(ld_decay, 16)
                cols = bass.ds(b * W1_SHARE, W1_SHARE)
                for c in range(2):
                    pool.tensor_copy(w1_hi[:, c, cols], w1_raw[:, c, :])
                pool.drain()
                for c in range(2):
                    last = pool.tensor_tensor(w1_lo[:, c, cols], w1_raw[:, c, :], w1_hi[:, c, cols], ALU.subtract)
                last.then_inc(w1_split, 1)

            rstd_of(0, ln1_var, rstd, veps, ln1_rstd)
            twice(0, ln1_normed, xn, xn_ready)

            def body(b, head, tail, router, more):
                if head:
                    halve_w1(b)
                if tail:
                    pool.wait_ge(gn_var, nth(b - 1, 1, 1))
                    pool.tensor_tensor(grstd[:, :], gvar[:, :], neg_half[:, 0:2], ALU.pow).then_inc(gn_rstd, 1)
                if more:
                    rstd_of(b + 1, ln1_var, rstd, veps, ln1_rstd)
                    twice(b + 1, ln1_normed, xn, xn_ready)
                if tail:
                    rstd_of(b - 1, ln2_var, rstdb, vepsb, ln2_rstd)
                    twice(b - 1, ln2_normed, xn2, xn2_ready)

            iterations(pool, body)
            end_of_phase_a(pool)

        @block.scalar
        def _(sc_eng):
            a = sc_eng

            def copy(dst, src):
                return a.activation(dst, src, ACT.Copy)

            a.wait_ge(ld_aw, 16)
            copy(aw_hi[:, :, :], aw_raw[:, :, :]).then_inc(aw_hi_ready, 1)
            a.wait_ge(emb_done, 1)
            a.activation(emb[:, 0, :], ps[:, 0, 0:B * IMG], ACT.Identity, bias=tokb[:, 0:1])
            a.activation(emb[0:HD, 1, :], ps[0:HD, 1, 0:B * IMG], ACT.Identity, bias=tokb[0:HD, 1:2]).then_inc(emb_copied, 1)

            def x_hi(b):
                a.wait_ge(xt_ext, nth(b, 1, 1))
                copy(xa_hi[:, :], psf[:, 0:LX]).then_inc(xt_hi, 1)
                copy(xb[:, :], psf[:, 1024:1024 + LX]).then_inc(xt_hi, 1)

            def halves(bank):
                return ps[:, bank:bank + 2, 0:HALF]

            def two(ap):
                return ap.rearrange("p (a n) -> p a n", a=2)

            def qk_round(b):
                for i, (dst, bank) in enumerate(((q2, 0), (k2_hi, 2), (q01_hi, 4), (k01_hi, 6))):
                    a.wait_ge(qk_done, nth(b, 4, i + 1))
                    copy(two(dst[:, :]), halves(bank)).then_inc(qk_hi, 1)

            def v_copy(b):
                for i, (bank, t0, n) in enumerate(((4, 0, 2), (5, 2, 2), (3, 4, 1))):
                    r = P if n == 2 else KEY_LAST
                    a.wait_ge(v_done, nth(b, 3, i + 1))
                    src = ps[:r, bank, 0:256 * n].rearrange("p (t d) -> p t d", t=n)
                    copy(v[:r, t0:t0 + n, 0:HD], src[:, :, 0:HD])
                    copy(v[:r, t0:t0 + n, P + HD:3 * P], src[:, :, HD:256]).then_inc(v_copied, 1)

            def exps(b, hh):
                s = hh % 2
                if hh == 0 and not (isinstance(b, int) and b == 0):
                    a.wait_ge(pt_done, nth(b - 1, 4 * H, 4 * H))
                for I in range(NT):
                    if I == 0:
                        a.wait_ge(nm_ready, nth(b, 2 * H, 2 * hh + 1))
                    elif I == 1:
                        a.wait_ge(nm_ready, nth(b, 2 * H, 2 * hh + 2))
                        a.activation(zero_score[s][:, :], nm[s][:, :], ACT.Exp)
                    r = rows(I)
                    cols = slice(OFF[I], OFF[I] + WIDTH[I])
                    last = a.activation(pr[s][:r, cols], sc[s][:r, cols], ACT.Exp, bias=nm[s][:r, I:I + 1],
                                        accum_out=row_sum[s][:r, I:I + 1])
                last.then_inc(exp_done, 1)

            def pt_copy(b, hh):
                for g in range(4):
                    a.wait_ge(pt_done, nth(b, 4 * H, 4 * hh + g + 1))
                    if g == 0:
                        last = copy(pt[:KEY_LAST, 0, :], ps[:KEY_LAST, 4, :])
                    elif g == 1:
                        copy(pt[:KEY_LAST, 1, 0:LAST], ps[:KEY_LAST, 5, 0:LAST])
                        last = copy(pt[:, 1, 64:64 + 3 * P], ps[:, 5, 64:64 + 3 * P])
                    elif g == 2:
                        last = copy(pt[:, 2, :], ps[:, 4, :])
                    else:
                        last = copy(pt[:, 3, 0:3 * P], ps[:, 5, 0:3 * P])
                    last.then_inc(pt_copied, 1)

            def o_copy(b, i):
                a.wait_ge(o_done, nth(b, 2, i + 1))
                if i == 0 and not (isinstance(b, int) and b == 0):
                    a.wait_ge(y_lo, nth(b - 1, 2, 2))
                tail = 64 * i
                copy(ot[:, i, 0:512], ps[:, 6, :])
                copy(ot[:, i, 512:L], ps[:, 7, tail:tail + LAST]).then_inc(o_copied, 1)

            def y_round(t):
                a.wait_ge(y_coeff, nth(t, 1, 1))
                for i, dst in enumerate((y01_hi, y2)):
                    a.activation(dst[:, :], ot[:, i, :], ACT.Identity, bias=gshift[:, i:i + 1],
                                 scale=gscale[:, i:i + 1]).then_inc(y_hi, 1)

            def x2_round(t):
                a.wait_ge(x2t_done, nth(t, 3, 1))
                a.wait_ge(x2_stored, CREDIT + 16 * t)
                copy(x2[:, 0, 0:512], ps[:, 4, :]).then_inc(x2_hi, 1)
                a.wait_ge(x2t_done, nth(t, 3, 2))
                copy(x2[:, 2, 0:512], ps[:, 5, :]).then_inc(x2_hi, 1)
                a.wait_ge(x2t_done, nth(t, 3, 3))
                copy(x2[:, 0, 512:L], ps[:, 4, 0:LAST])
                copy(x2[:, 2, 512:L], ps[:, 4, 64:64 + LAST]).then_inc(x2_hi, 1)

            def logits_copy(t):
                a.wait_ge(lg_done, nth(t, 1, 1))
                copy(lt[:, 0:HALF], ps[0:E, 5, 0:HALF])
                copy(lt[:, HALF:L], ps[0:E, 4, 0:HALF]).then_inc(lt_copied, 1)

            def logits_exp(t):
                a.wait_ge(l_sub, nth(t, 1, 1))
                a.activation(lexp[:, :, :], lsub[:, :, :], ACT.Exp).then_inc(l_exp, 1)

            def comb_copy(t):
                a.wait_ge(ct_done, nth(t, 1, 1))
                a.wait_ge(ct_stored, CREDIT + 16 * t)
                copy(ct[:, 0:512], ps[0:E, 4, :])
                copy(ct[:, 512:NT * P], ps[0:E, 5, 0:P]).then_inc(ct_copied, 1)

            def body(b, head, tail, router, more):
                t, u = b - 1, b - 2
                if head:
                    qk_round(b)
                if router:
                    logits_copy(u)
                if tail:
                    pt_copy(t, 2)
                if head:
                    exps(b, 0)
                if tail:
                    o_copy(t, 1)
                if head:
                    v_copy(b)
                if router:
                    logits_exp(u)
                if head:
                    pt_copy(b, 0)
                if tail:
                    y_round(t)
                if head:
                    exps(b, 1)
                    pt_copy(b, 1)
                    exps(b, 2)
                    o_copy(b, 0)
                if router:
                    comb_copy(u)
                if more:
                    x_hi(b + 1)
                if tail:
                    x2_round(t)

            for s in (x2_stored, ct_stored, ct_copied):
                a.sem_inc(s, CREDIT)
            x_hi(0)
            iterations(a, body)
            end_of_phase_a(a)

            def w2_round(q):
                a.wait_ge(ld_w2, 16 if q == 0 else 32)
                part = slice(q * W2_PART, (q + 1) * W2_PART)
                src = w2_first if q == 0 else w2_others[:, (q - 1) * W2_PART:q * W2_PART, :]
                copy(w2_hi[:, part, :], src[:, :, 0:P])
                copy(w2_r[:, part, :], src[:, :, P:256]).then_inc(w2_hi_ready, 1)

            def gelu(b, k):
                a.wait_ge(up_done, nth(b, NW, k + 1))
                if k >= 3 or not isinstance(b, int) or b:
                    a.wait_ge(act_lo_ready, nth(b, NW, k - 2))
                a.activation(act[k % 3][:, :, :], ps[:, 2 * (k % 2):2 * (k % 2) + 2, 0:HALF],
                             ACT.Gelu_apprx_tanh).then_inc(gelu_done, 1)

            def act_round(b, k):
                a.wait_ge(gated, nth(b, NW, k + 1))
                if k >= 3 or not isinstance(b, int) or b:
                    a.wait_ge(down_done, nth(b, NW, k - 2))
                copy(act_hi[k % 3][:, :, :], act[k % 3][:, :, :]).then_inc(act_hi_ready, 1)

            def ffn(b, more):
                gelu(b, 1)
                for k in range(1, NW - 1):
                    gelu(b, k + 1)
                    act_round(b, k)
                    if isinstance(b, int) and b == 0 and k % W2_PART == 1 and k < NW - W2_PART:
                        w2_round(k // W2_PART + 1)
                if more:
                    gelu(b + 1, 0)
                act_round(b, NW - 1)
                a.wait_ge(down_done, nth(b, NW, NW))
                copy(out_a[:, :].rearrange("p (a n) -> p a n", a=2), ps[:, 4:6, 0:HALF]).then_inc(acc_a_copied, 1)
                if more:
                    act_round(b + 1, 0)

            w2_round(0)
            gelu(0, 0)
            act_round(0, 0)
            ffn(0, True)
            with a.Fori(1, B - 1) as b:
                ffn(b, True)
            ffn(B - 1, False)

        @block.vector
        def _(dve):
            for t in (0, 1):
                dve.memset(sc[t][:, :], NEG)
                dve.memset(mx[t][:, :], 0.0)
                dve.memset(row_sum[t][:, :], 1.0)
            dve.memset(mv[:, :, :], 1.0)
            dve.memset(mvb[:, :, :], 1.0)
            dve.memset(v[:, :, :], 0.0)
            dve.memset(lt[:, :], 0.0)
            dve.memset(xn[:, NT - 1, :], 0.0)
            dve.memset(xn2[:, NT - 1, :], 0.0)
            dve.memset(head_mean[:, :], 0.0)
            dve.memset(drow[:, :, :], 0.0)
            dve.drain()
            dve.memset(head_mean[0:HD, 0:HD], 1.0 / HD)
            dve.memset(head_mean[HD:P, HD:P], 1.0 / HD)
            for I in range(NT):
                dve.memset(lower_count[:, I:I + 1], float((P - 1) * I))
                for t in (0, 1):
                    if I:
                        at = OFF[I] + WIDTH[I] - (NT - 1)
                        dve.memset(sc[t][:, at:at + I], 0.0)
            dve.memset(drow[:, :, 127:128], 1.0).then_inc(consts, 1)
            dve.wait_ge(ld_small, 16 * 3)
            for hh in range(H):
                dve.tensor_copy(drow[:, hh, 128:129], gam[:, hh:hh + 1])
            n = 1
            while n < L - 1:
                m = min(n, L - 1 - n)
                dve.drain()
                for hh in range(H):
                    last = dve.tensor_scalar(drow[:, hh, 128 + n:128 + n + m], drow[:, hh, 128:128 + m],
                                             drow[:, hh, 127 + n:128 + n], None, ALU.mult)
                n += m
            last.then_inc(decay_built, 1)

            def norm_stats(b, s6, m2, ve, signal):
                for I in range(NT):
                    dve.bn_stats(s6[:rows(I), I, :], tokens(h, b, I))
                dve.drain()
                for I in range(NT):
                    dve.bn_aggr(m2[:rows(I), I, :], s6[:rows(I), I, :])
                dve.drain()
                dve.tensor_scalar(ve[:, :], m2[:, :, 1], EPS, None, ALU.add).then_inc(signal, 1)

            def norm_apply(b, m2, rs, rs_ready, dst, normed):
                dve.wait_ge(rs_ready, nth(b, 1, 1))
                for I in range(NT):
                    r = rows(I)
                    last = dve.tensor_scalar(dst[:r, I, 0:D], tokens(h, b, I), m2[:r, I, 0:1], rs[:r, I:I + 1],
                                             ALU.subtract, ALU.mult)
                last.then_inc(normed, 1)

            dve.wait_ge(ld_h0, 16 * NT)
            dve.wait_ge(embt_done, 1)
            for i in range(B // 2):
                last = dve.tensor_copy(h[0:IMG, 2 * i:2 * i + 2, 0, :],
                                       ps[0:IMG, 2 + i, 0:2 * D].rearrange("p (b d) -> p b d", b=2))
            last.then_inc(embt_copied, 1)
            dve.drain()
            norm_stats(0, st6, mv, veps, ln1_var)
            norm_apply(0, mv, rstd, ln1_rstd, xn, ln1_normed)
            dve.wait_ge(aw_hi_ready, 1)
            dve.tensor_tensor(aw_lo[:, :, :], aw_raw[:, :, :], aw_hi[:, :, :], ALU.subtract).then_inc(aw_lo_ready, 1)

            def sub(dst, src, hi):
                return dve.tensor_tensor(dst, src, hi, ALU.subtract)

            def halves(bank, p0=0):
                return ps[p0:P, bank:bank + 2, 0:HALF]

            def two(ap):
                return ap.rearrange("p (a n) -> p a n", a=2)

            def x_ext(b):
                dve.wait_ge(xt_done, nth(b, 1, 1))
                for bank in (0, 2):
                    dve.memset(ps[:, bank + 1, LAST:SUMS], 0.0)
                    last = dve.tensor_reduce(ps[:, bank + 1, SUMS:KEY_LAST],
                                             ps[:, bank, :].rearrange("p (t n) -> p t n", n=P), AX.X, ALU.add)
                last.then_inc(xt_ext, 1)

            def x_lo(b):
                dve.wait_ge(xt_hi, nth(b, 2, 1))
                sub(xa_lo[:, :], psf[:, 0:LX], xa_hi[:, :]).then_inc(xt_lo, 1)
                dve.wait_ge(xt_hi, nth(b, 2, 2))
                sub(xb[HD:P, :], psf[HD:P, 1024:1024 + LX], xb[HD:P, :]).then_inc(xt_lo, 1)

            def qk_rest(b):
                for i, (dst, hi, bank) in enumerate(((q2, q2, 0), (k2_lo, k2_hi, 2), (q01_lo, q01_hi, 4), (k01_lo, k01_hi, 6))):
                    p0 = HD if dst is q2 else 0
                    dve.wait_ge(qk_hi, nth(b, 4, i + 1))
                    sub(two(dst[p0:P, :]), halves(bank, p0), two(hi[p0:P, :])).then_inc(qk_lo, 1)

            def apply_decay(b, hh):
                s = hh % 2
                for I in range(NT):
                    r, n = rows(I), L - P * I
                    if I <= 2:
                        dve.wait_ge(s_done, nth(b, 3 * H, 3 * hh + I + 1))
                        apart(dve, "dve")
                    dst, tab = sc[s][:r, OFF[I]:OFF[I] + n], decay[:r, hh, 0:n]
                    if I == 0:
                        dst, tab, src = two(dst), two(tab), ps[:, 0:2, 0:HALF]
                    elif I == 1:
                        src = ps[:, 2, 0:n]
                    else:
                        src = ps[:r, 3, S_AT[I]:S_AT[I] + n]
                    dve.tensor_tensor_reduce(out=dst, in0=src, in1=tab, scale=1.0 / 8, scalar=0.0 if I else NEG,
                                             op0=ALU.mult, op1=ALU.max,
                                             accum_out=mx[s][:r, I:I + 1]).then_inc(decayed, 1)
                    if I in (0, NT - 1):
                        dve.drain()
                        cols = slice(0, 1) if I == 0 else slice(1, NT)
                        dve.tensor_scalar(nm[s][:, cols], mx[s][:, cols], -1.0, None, ALU.mult).then_inc(nm_ready, 1)

            def normalise(b, hh):
                s = hh % 2
                dve.wait_ge(exp_done, nth(b, H, hh + 1))
                dve.tensor_tensor(den[s][:, :], zero_score[s][:, :], lower_count[:, :], ALU.mult)
                dve.drain()
                dve.tensor_tensor(den[s][:, :], den[s][:, :], row_sum[s][:, :], ALU.add)
                dve.drain()
                dve.reciprocal(inv_den[s][:, :], den[s][:, :])
                dve.drain()
                for I in range(NT):
                    t = pr[s][:rows(I), OFF[I]:OFF[I] + WIDTH[I]]
                    last = dve.tensor_scalar(t, t, inv_den[s][:rows(I), I:I + 1], None, ALU.mult)
                last.then_inc(probs_ready, 1)

            def gn_partial(t):
                dve.wait_ge(o_copied, nth(t, 2, 2))
                for i in range(2):
                    for j in range(2):
                        dve.bn_stats(gst[:, i, 6 * j:6 * j + 6], ot[:, i, j * HALF:(j + 1) * HALF])
                dve.drain()
                for i in range(2):
                    dve.bn_aggr(gmv[:, i, :], gst[:, i, :])
                dve.drain()
                dve.tensor_tensor(gtmp[:, :], gmv[:, :, 0], gmv[:, :, 0], ALU.mult)
                dve.drain()
                dve.tensor_tensor(gmv[:, :, 1], gmv[:, :, 1], gtmp[:, :], ALU.add).then_inc(gn_part, 1)

            def gn_variance(t):
                dve.wait_ge(gn_sum, nth(t, 1, 1))
                dve.tensor_copy(gtot[:, :, :], ps[:, 7, 128:132].rearrange("p (i k) -> p i k", i=2))
                dve.drain()
                dve.tensor_tensor(gtmp[:, :], gtot[:, :, 0], gtot[:, :, 0], ALU.mult)
                dve.drain()
                dve.tensor_tensor(gvar[:, :], gtot[:, :, 1], gtmp[:, :], ALU.subtract)
                dve.drain()
                dve.tensor_scalar(gvar[:, :], gvar[:, :], 0.0, EPS, ALU.max, ALU.add).then_inc(gn_var, 1)

            def gn_coefficients(t):
                dve.wait_ge(gn_rstd, nth(t, 1, 1))
                dve.tensor_tensor(gscale[:, :], grstd[:, :], gnw[:, :], ALU.mult)
                dve.drain()
                dve.tensor_tensor(gtmp[:, :], gtot[:, :, 0], gscale[:, :], ALU.mult)
                dve.drain()
                dve.tensor_tensor(gshift[:, :], gnb[:, :], gtmp[:, :], ALU.subtract).then_inc(y_coeff, 1)
                dve.drain()

            def y_rest(t):
                for i, (p0, lo, hi) in enumerate(((0, y01_lo, y01_hi), (HD, y2, y2))):
                    dve.wait_ge(y_hi, nth(t, 2, i + 1))
                    o = ot[p0:P, i, :]
                    dve.tensor_scalar(o, o, gscale[p0:P, i:i + 1], gshift[p0:P, i:i + 1], ALU.mult, ALU.add)
                    dve.drain()
                    sub(lo[p0:P, :], o, hi[p0:P, :]).then_inc(y_lo, 1)

            def add_attention(t):
                for i, (bank, t0, n) in enumerate(((4, 0, 2), (5, 2, 2), (3, 4, 1))):
                    r = P if n == 2 else LAST
                    dve.wait_ge(wo_done, nth(t, 3, i + 1))
                    dst = h[:r, bass.ds(t, 1), t0:t0 + n, :].rearrange("p a t d -> p (a t) d")
                    src = ps[:r, bank, 0:256 * n].rearrange("p (t d) -> p t d", t=n)[:, :, 0:D]
                    dve.tensor_tensor(dst, src, dst, ALU.add).then_inc(wo_added, 1)
                dve.drain()
                norm_stats(t, st6b, mvb, vepsb, ln2_var)

            def x2_rest(t):
                dve.wait_ge(x2_hi, nth(t, 3, 1))
                sub(x2[:, 1, 0:512], ps[:, 4, :], x2[:, 0, 0:512]).then_inc(x2_lo, 1)
                dve.wait_ge(x2_hi, nth(t, 3, 2))
                sub(x2[HD:P, 2, 0:512], ps[HD:P, 5, :], x2[HD:P, 2, 0:512]).then_inc(x2_lo, 1)
                dve.wait_ge(x2_hi, nth(t, 3, 3))
                sub(x2[:, 1, 512:L], ps[:, 4, 0:LAST], x2[:, 0, 512:L])
                sub(x2[HD:P, 2, 512:L], ps[HD:P, 4, 64:64 + LAST], x2[HD:P, 2, 512:L]).then_inc(x2_lo, 1)

            def wide(ap, n):
                return ap.unsqueeze(2).broadcast_to([P, NT, n])

            def router_shift(t):
                dve.wait_ge(lgn_done, nth(t, 1, 1))
                logits = ps[:, 2, 0:NT * E].rearrange("p (t e) -> p t e", t=NT)
                dve.tensor_reduce(lmax[:, :], logits, AX.X, ALU.max)
                dve.drain()
                dve.tensor_tensor(lsub[:, :, :], logits, wide(lmax[:, :], E), ALU.subtract).then_inc(l_sub, 1)

            def router_choose(t):
                dve.wait_ge(l_exp, nth(t, 1, 1))
                apart(dve, "dve")
                for I in range(NT):
                    dve.max(top[:, I, :], lexp[:, I, :])
                dve.drain()
                for I in range(NT):
                    dve.match_replace(left[:, I, :], top[:, I, :], lexp[:, I, :], -1.0)
                dve.tensor_reduce(tsum[:, :], top[:, :, :], AX.X, ALU.add)
                dve.drain()
                dve.reciprocal(tinv[:, :], tsum[:, :])
                dve.tensor_scalar(left[:, :, :], left[:, :, :], 0.0, None, ALU.is_lt)
                dve.drain()
                dve.tensor_tensor(chosen[:, :, :], left[:, :, :], lexp[:, :, :], ALU.mult)
                dve.drain()
                dve.tensor_tensor(comb[:, :, :], chosen[:, :, :], wide(tinv[:, :], E), ALU.mult).then_inc(comb_ready, 1)

            def body(b, head, tail, router, more):
                t, u = b - 1, b - 2
                if head:
                    if isinstance(b, int) and b == 0:
                        dve.wait_ge(ld_h, 16 * NT)
                    qk_rest(b)
                    if isinstance(b, int) and b == 0:
                        dve.wait_ge(ld_decay, 16)
                    apply_decay(b, 0)
                    normalise(b, 0)
                if tail:
                    gn_partial(t)
                if router:
                    router_shift(u)
                if tail:
                    gn_variance(t)
                if head:
                    apply_decay(b, 1)
                if tail:
                    gn_coefficients(t)
                if router:
                    router_choose(u)
                if tail:
                    y_rest(t)
                if head:
                    apply_decay(b, 2)
                    normalise(b, 1)
                if more:
                    norm_stats(b + 1, st6, mv, veps, ln1_var)
                if tail:
                    add_attention(t)
                if more:
                    norm_apply(b + 1, mv, rstd, ln1_rstd, xn, ln1_normed)
                if tail:
                    norm_apply(t, mvb, rstdb, ln2_rstd, xn2, ln2_normed)
                if head:
                    normalise(b, 2)
                if more:
                    x_ext(b + 1)
                    x_lo(b + 1)
                if tail:
                    x2_rest(t)

            x_ext(0)
            x_lo(0)
            iterations(dve, body)
            end_of_phase_a(dve)

            def w2_rest(q):
                dve.wait_ge(w2_hi_ready, q + 1)
                part = slice(q * W2_PART, (q + 1) * W2_PART)
                src = w2_first if q == 0 else w2_others[:, (q - 1) * W2_PART:q * W2_PART, :]
                sub(w2_lo[:, part, :], src[:, :, 0:P], w2_hi[:, part, :])
                sub(w2_r[:, part, HD:P], src[:, :, P + HD:256], w2_r[:, part, HD:P]).then_inc(w2_lo_ready, 1)

            def weigh(b, k):
                e = TILE_E[k]
                dve.wait_ge(gelu_done, nth(b, NW, k + 1))
                dve.wait_ge(ld_gate[e % 4], 16 * (b * (E // 4) + e // 4 + 1))
                dve.tensor_tensor(act[k % 3][:, :, :], act[k % 3][:, :, :], gate[e % 4][:, :, :],
                                  ALU.mult).then_inc(gated, 1)

            def act_rest(b, k):
                dve.wait_ge(act_hi_ready, nth(b, NW, k + 1))
                sub(act_lo[k % 3][:, :, :], act[k % 3][:, :, :], act_hi[k % 3][:, :, :]).then_inc(act_lo_ready, 1)

            def ffn(b, more):
                weigh(b, 1)
                for k in range(1, NW - 1):
                    weigh(b, k + 1)
                    act_rest(b, k)
                    if isinstance(b, int) and b == 0 and k % W2_PART == 1 and k < NW - W2_PART:
                        w2_rest(k // W2_PART + 1)
                if more:
                    weigh(b + 1, 0)
                act_rest(b, NW - 1)
                dve.wait_ge(down_done, nth(b, NW, NW))
                dve.tensor_copy(out_r[:, :].rearrange("p (a n) -> p a n", a=2), ps[:, 6:8, 0:HALF]).then_inc(acc_r_copied, 1)
                if more:
                    act_rest(b + 1, 0)
                dve.wait_ge(outt_done, nth(b, 1, 1))
                for r, t0, n, bank_a, bank_r in ((P, 0, NT - 1, 4, 6), (LAST, NT - 1, 1, 5, 7)):
                    hb = h[:r, bass.ds(b, 1), t0:t0 + n, :].rearrange("p a t d -> p (a t) d")
                    main = ps[:r, bank_a, 0:P * n].rearrange("p (t d) -> p t d", t=n)
                    rest = ps[:r, bank_r, 0:P * n].rearrange("p (t d) -> p t d", t=n)
                    part = out_t[:r, t0:t0 + n, :]
                    dve.tensor_tensor(part, rest[:, :, HD:P], hb[:, :, P:D], ALU.add)
                    dve.tensor_tensor(hb[:, :, 0:P], main, hb[:, :, 0:P], ALU.add)
                    dve.drain()
                    last = dve.tensor_tensor(hb[:, :, P:D], rest[:, :, 0:HD], part, ALU.add)
                last.then_inc(out_ready, 1)

            w2_rest(0)
            weigh(0, 0)
            act_rest(0, 0)
            ffn(0, True)
            with dve.Fori(1, B - 1) as b:
                ffn(b, True)
            ffn(B - 1, False)

        @block.tensor
        def _(pe):
            def mm(dst, w, x, start, stop):
                return pe.matmul(dst, w, x, start=start, stop=stop)

            def series(dst, pairs):
                for i, (w, x) in enumerate(pairs):
                    last = mm(dst, w, x, i == 0, i == len(pairs) - 1)
                return last

            pe.wait_ge(ld_pat, 48)
            for bank, f0, f1 in ((0, 0, P), (1, P, D)):
                last = series(ps[0:f1 - f0, bank, 0:B * IMG], [(tokw[:, k, f0:f1], pat[:, k, :]) for k in range(KT)])
            last.then_inc(emb_done, 1)
            pe.wait_ge(emb_copied, 1)
            pe.wait_ge(consts, 3)
            for b in range(B):
                at = (b % 2) * D
                pe.transpose(ps[0:IMG, 2 + b // 2, at:at + P], emb[:, 0, b * IMG:(b + 1) * IMG], ident[:, :])
                last = pe.transpose(ps[0:IMG, 2 + b // 2, at + P:at + D], emb[0:HD, 1, b * IMG:(b + 1) * IMG], ident[0:HD, 0:HD])
            last.then_inc(embt_done, 1)
            pe.wait_ge(aw_lo_ready, 1)

            def weights(c0, c1):
                return aw_hi[:, 0, c0:c1], aw_lo[:, 0, c0:c1], aw_hi[:, 1, c0:c1], aw_lo[:, 1, c0:c1]

            def x_transpose(b):
                pe.wait_ge(xn_ready, nth(b, 1, 1))
                if not isinstance(b, int) or b:
                    pe.wait_ge(decayed, nth(b - 1, NT * H, NT * H))
                    if not isinstance(b, int) or b > 1:
                        pe.wait_ge(wo_added, nth(b - 2, 3, 3))
                for I in range(NT):
                    r = rows(I)
                    bank, at = (0, I * P) if I < NT - 1 else (1, 0)
                    pe.transpose(ps[:, bank, at:at + r], xn[:r, I, 0:P], ident[:r, :r])
                    last = pe.transpose(ps[:, bank + 2, at:at + r], xn[:r, I, P:256], ident[:r, :r])
                last.then_inc(xt_done, 1)

            def qk(b, tail, router):
                pe.wait_ge(xt_lo, nth(b, 2, 2))
                for tile, bank in ((2, 0), (3, 2), (0, 4), (1, 6)):
                    if bank == 4 and tail:
                        pe.wait_ge(pt_copied, nth(b - 1, 4 * H, 8))
                        if router:
                            pe.wait_ge(x2_lo, nth(b - 2, 3, 3))
                    if bank == 6 and tail:
                        pe.wait_ge(o_copied, nth(b - 1, 2, 1))
                    ah, al, bh, bl = weights(tile * P, (tile + 1) * P)
                    for n in range(2):
                        c = slice(n * HALF, (n + 1) * HALF)
                        last = series(ps[:, bank + n, 0:HALF],
                                      [(ah, xa_hi[:, c]), (al, xa_hi[:, c]), (ah, xa_lo[:, c]), (bh, xb[:, c]), (bl, xb[:, c])])
                    last.then_inc(qk_done, 1)

            def values(b, tail):
                ah, al, bh, bl = weights(QK_W, QK_W + V_W)
                if tail:
                    pe.wait_ge(pt_copied, nth(b - 1, 4 * H, 4 * H))
                for I in range(NT):
                    if I == NT - 1:
                        pe.wait_ge(decayed, nth(b, NT * H, NT))
                    r = P if I < NT - 1 else KEY_LAST
                    c = slice(I * P, I * P + r)
                    bank, at = (4 + I // 2, (I % 2) * 256) if I < NT - 1 else (3, 0)
                    last = series(ps[:r, bank, at:at + 256],
                                  [(xa_hi[:, c], ah), (xa_hi[:, c], al), (xa_lo[:, c], ah), (xb[:, c], bh), (xb[:, c], bl)])
                    if I in (1, 3, 4):
                        last.then_inc(v_done, 1)

            def scores(b, hh, router):
                if hh < 2:
                    g = slice(HD * hh, HD * hh + HD)
                    pairs = ((q01_hi, k01_hi), (q01_hi, k01_lo), (q01_lo, k01_hi))
                else:
                    g = slice(0, P)
                    pairs = ((q2, k2_hi), (q2, k2_lo))
                for I in range(NT):
                    if hh == 0 and I == 0:
                        pe.wait_ge(qk_lo, nth(b, 4, 4))
                    elif hh and I in (0, 1, 2):
                        k = (hh - 1) * NT + (1, 2, NT)[I]
                        pe.wait_ge(decayed, nth(b, NT * H, k))
                        if hh == 1 and I == 1 and router:
                            pe.wait_ge(l_sub, nth(b - 2, 1, 1))
                        if hh == 1 and I == 2:
                            pe.wait_ge(v_copied, nth(b, 3, 3))
                    r, n = rows(I), L - P * I
                    q = slice(I * P, I * P + r)
                    if I == 0:
                        parts = [(ps[:, 0, 0:HALF], 0, HALF), (ps[:, 1, 0:HALF], HALF, L)]
                    elif I == 1:
                        parts = [(ps[:, 2, 0:n], P, L)]
                    else:
                        parts = [(ps[:r, 3, S_AT[I]:S_AT[I] + n], I * P, L)]
                    for dst, m0, m1 in parts:
                        last = series(dst, [(a_[g, q], b_[g, m0:m1]) for a_, b_ in pairs])
                    if I in (0, 1, 4):
                        last.then_inc(s_done, 1)

            def gn_sums(t):
                pe.wait_ge(gn_part, nth(t, 1, 1))
                mm(ps[:, 7, 128:132], head_mean[:, :], gmv[:, :, :].rearrange("p i k -> p (i k)"), True, True).then_inc(gn_sum, 1)

            def project(b, head):
                t = b - 1
                ah, al, bh, bl = weights(QK_W + V_W, QK_W + V_W + O_W)
                pe.wait_ge(y_lo, nth(t, 2, 2))
                if head:
                    pe.wait_ge(pt_copied, nth(b, 4 * H, 4))
                for I in range(NT):
                    if I == NT - 1 and head:
                        pe.wait_ge(decayed, nth(b, NT * H, NT * H))
                    r = rows(I)
                    c = slice(I * P, I * P + r)
                    bank, at = (4 + I // 2, (I % 2) * 256) if I < NT - 1 else (3, 0)
                    last = series(ps[:r, bank, at:at + D],
                                  [(y01_hi[:, c], ah), (y01_hi[:, c], al), (y01_lo[:, c], ah), (y2[:, c], bh), (y2[:, c], bl)])
                    if I in (1, 3, 4):
                        last.then_inc(wo_done, 1)

            def probs_transpose(b, hh):
                s = hh % 2
                pe.wait_ge(probs_ready, nth(b, H, hh + 1))

                def tile(dst, I, J):
                    n = P if J < NT - 1 else KEY_LAST
                    r, at = rows(I), OFF[I] + (J - I) * P
                    return pe.transpose(dst, pr[s][:r, at:at + n], ident[:r, :r])

                for I in range(NT - 1):
                    last = tile(ps[:KEY_LAST, 4, I * P:(I + 1) * P], I, NT - 1)
                last.then_inc(pt_done, 1)
                tile(ps[:KEY_LAST, 5, 0:LAST], NT - 1, NT - 1)
                for I in range(3):
                    last = tile(ps[:, 5, 64 + I * P:64 + (I + 1) * P], I, 2)
                last.then_inc(pt_done, 1)
                pe.wait_ge(pt_copied, nth(b, 4 * H, 4 * hh + 1))
                for I in range(4):
                    last = tile(ps[:, 4, I * P:(I + 1) * P], I, 3)
                last.then_inc(pt_done, 1)
                pe.wait_ge(pt_copied, nth(b, 4 * H, 4 * hh + 2))
                for I in range(2):
                    tile(ps[:, 5, I * P:(I + 1) * P], I, 1)
                tile(ps[:, 5, 2 * P:3 * P], 0, 0).then_inc(pt_done, 1)

            def attend(b, hh):
                first, last_head = hh != 1, hh != 0
                tail = 64 if hh == 2 else 0
                cols = slice(hh * P, (hh + 1) * P)
                pe.wait_ge(pt_copied, nth(b, 4 * H, 4 * hh + 2))
                mm(ps[:, 6, :], v[:KEY_LAST, 4, cols], pt[:KEY_LAST, 0, :], first, False)
                mm(ps[:, 7, tail:tail + LAST], v[:KEY_LAST, 4, cols], pt[:KEY_LAST, 1, 0:LAST], first, last_head)
                mm(ps[:, 6, 0:3 * P], v[:, 2, cols], pt[:, 1, 64:64 + 3 * P], False, False)
                pe.wait_ge(pt_copied, nth(b, 4 * H, 4 * hh + 3))
                mm(ps[:, 6, :], v[:, 3, cols], pt[:, 2, :], False, False)
                pe.wait_ge(pt_copied, nth(b, 4 * H, 4 * hh + 4))
                mm(ps[:, 6, 0:2 * P], v[:, 1, cols], pt[:, 3, 0:2 * P], False, False)
                last = mm(ps[:, 6, 0:P], v[:, 0, cols], pt[:, 3, 2 * P:3 * P], False, last_head)
                if last_head:
                    last.then_inc(o_done, 1)

            def x2_transpose(b, head, router):
                t = b - 1
                pe.wait_ge(xn2_ready, nth(t, 1, 1))
                if router:
                    pe.wait_ge(ct_copied, CREDIT + nth(b - 2, 1, 1))
                elif head:
                    pe.wait_ge(pt_copied, nth(b, 4 * H, 8))
                for c, bank in ((0, 4), (1, 5)):
                    for I in range(NT - 1):
                        last = pe.transpose(ps[:, bank, I * P:(I + 1) * P], xn2[:, I, c * P:(c + 1) * P], ident[:, :])
                    last.then_inc(x2t_done, 1)
                pe.wait_ge(x2_lo, nth(t, 3, 1))
                apart(pe, "pe")
                for c in range(2):
                    last = pe.transpose(ps[:, 4, 64 * c:64 * c + LAST], xn2[:LAST, NT - 1, c * P:(c + 1) * P], ident[:LAST, :LAST])
                last.then_inc(x2t_done, 1)

            def logits(b, head):
                u = b - 2
                ah, al, bh, bl = weights(QK_W + V_W + O_W, AW)
                pe.wait_ge(x2_lo, nth(u, 3, 3))
                if head:
                    pe.wait_ge(qk_lo, nth(b, 4, 3))
                for n, bank in ((0, 5), (1, 4)):
                    c = slice(n * HALF, (n + 1) * HALF)
                    last = series(ps[0:E, bank, 0:HALF],
                                  [(ah, x2[:, 0, c]), (al, x2[:, 0, c]), (ah, x2[:, 1, c]), (bh, x2[:, 2, c]), (bl, x2[:, 2, c])])
                last.then_inc(lg_done, 1)

            def logits_transpose(b, head):
                pe.wait_ge(lt_copied, nth(b - 2, 1, 1))
                if head:
                    pe.wait_ge(decayed, nth(b, NT * H, 2))
                apart(pe, "pe")
                for I in range(NT):
                    last = pe.transpose(ps[:, 2, I * E:(I + 1) * E], lt[:, I * P:(I + 1) * P], ident[0:E, 0:E])
                last.then_inc(lgn_done, 1)

            def comb_transpose(b, head, tail):
                pe.wait_ge(comb_ready, nth(b - 2, 1, 1))
                if head:
                    pe.wait_ge(pt_copied, nth(b, 4 * H, 8))
                elif tail:
                    pe.wait_ge(wo_added, nth(b - 1, 3, 3))
                for I in range(NT):
                    bank, at = (4, I * P) if I < NT - 1 else (5, 0)
                    last = pe.transpose(ps[0:E, bank, at:at + P], comb[:, I, :], ident[:, :])
                last.then_inc(ct_done, 1)

            def body(b, head, tail, router, more):
                t = b - 1
                if head:
                    qk(b, tail, router)
                if router:
                    logits(b, head)
                if head:
                    scores(b, 0, router)
                if tail:
                    if router:
                        pe.wait_ge(lt_copied, nth(b - 2, 1, 1))
                    probs_transpose(t, 2)
                    pe.wait_ge(o_copied, nth(t, 2, 1))
                    attend(t, 2)
                if router:
                    logits_transpose(b, head)
                if head:
                    values(b, tail)
                if tail:
                    gn_sums(t)
                if head:
                    scores(b, 1, router)
                    pe.wait_ge(v_copied, nth(b, 3, 3))
                    probs_transpose(b, 0)
                    if tail:
                        pe.wait_ge(gn_var, nth(t, 1, 1))
                    attend(b, 0)
                    scores(b, 2, router)
                if tail:
                    project(b, head)
                if head:
                    if tail:
                        pe.wait_ge(wo_added, nth(t, 3, 3))
                    probs_transpose(b, 1)
                    attend(b, 1)
                if router:
                    comb_transpose(b, head, tail)
                if more:
                    x_transpose(b + 1)
                if tail:
                    x2_transpose(b, head, router)

            x_transpose(0)
            iterations(pe, body)
            end_of_phase_a(pe)

            pe.wait_ge(w1_split, B)

            def up(b, k):
                if k == 0:
                    pe.wait_ge(ld_x2, 16 * (b + 1))
                if k >= 2 or not isinstance(b, int) or b:
                    pe.wait_ge(gelu_done, nth(b, NW, k - 1))
                w = slice(k * P, (k + 1) * P)
                for n in range(2):
                    def x(c):
                        return x2_all[:, bass.ds(b, 1), c, n * HALF:(n + 1) * HALF].rearrange("p a n -> p (a n)")
                    last = series(ps[:, 2 * (k % 2) + n, 0:HALF],
                                  [(w1_hi[:, 0, w], x(0)), (w1_lo[:, 0, w], x(0)), (w1_hi[:, 0, w], x(1)),
                                   (w1_hi[:, 1, w], x(2)), (w1_lo[:, 1, w], x(2))])
                last.then_inc(up_done, 1)

            def down(b, k):
                pe.wait_ge(act_lo_ready, nth(b, NW, k + 1))
                if isinstance(b, int) and b == 0 and k % W2_PART == 0:
                    pe.wait_ge(w2_lo_ready, k // W2_PART + 1)
                if k == 0 and (not isinstance(b, int) or b):
                    pe.wait_ge(out_ready, nth(b - 1, 1, 1))
                first, last_k = k == 0, k == NW - 1
                hi, lo = act_hi[k % 3], act_lo[k % 3]
                for n in range(2):
                    mm(ps[:, 4 + n, 0:HALF], w2_hi[:, k, :], hi[:, n, :], first, False)
                    mm(ps[:, 4 + n, 0:HALF], w2_lo[:, k, :], hi[:, n, :], False, False)
                    mm(ps[:, 4 + n, 0:HALF], w2_hi[:, k, :], lo[:, n, :], False, last_k)
                    mm(ps[:, 6 + n, 0:HALF], w2_r[:, k, :], hi[:, n, :], first, False)
                    last = mm(ps[:, 6 + n, 0:HALF], w2_r[:, k, :], lo[:, n, :], False, last_k)
                last.then_inc(down_done, 1)

            def ffn(b, more):
                for k in range(NW):
                    if k + 2 < NW:
                        up(b, k + 2)
                    elif k + 2 == NW and more:
                        up(b + 1, 0)
                    down(b, k)
                if more:
                    up(b + 1, 1)
                pe.wait_ge(acc_a_copied, nth(b, 1, 1))
                pe.wait_ge(acc_r_copied, nth(b, 1, 1))
                for I in range(NT):
                    r = rows(I)
                    bank, at = (4, I * P) if I < NT - 1 else (5, 0)
                    pe.transpose(ps[:r, bank, at:at + P], out_a[:, I * P:I * P + r], ident[:, :])
                    last = pe.transpose(ps[:r, bank + 2, at:at + P], out_r[:, I * P:I * P + r], ident[:, :])
                last.then_inc(outt_done, 1)

            up(0, 0)
            up(0, 1)
            ffn(0, True)
            with pe.Fori(1, B - 1) as b:
                ffn(b, True)
            ffn(B - 1, False)


S_AT = {2: 0, 3: L - 2 * P, 4: (L - 2 * P) + (L - 3 * P)}


def _stack(np, wt):
    return np.ascontiguousarray(np.stack([wt[0:128], np.concatenate([wt[128:192], wt[128:192]])], axis=1))


def kernel(x, txt, L0_tok_W, L0_tok_b, L0_attn_Wq, L0_attn_Wk, L0_attn_Wv, L0_attn_Wo, L0_attn_gammas,
           L0_attn_gn_weight, L0_attn_gn_bias, L0_ffn_router_w, L0_ffn_w1, L0_ffn_w2):
    import concourse.bacc as bacc
    import numpy as np
    from concourse.bass_utils import run_bass_kernel_spmd

    f = lambda t: np.asarray(t)
    img = f(x).reshape(B, 3, 6, 16, 6, 16).transpose(1, 3, 5, 0, 2, 4).reshape(KT, P, B * IMG)
    wq, wk, wv, wo, wr = f(L0_attn_Wq).T, f(L0_attn_Wk).T, f(L0_attn_Wv).T, f(L0_attn_Wo).T, f(L0_ffn_router_w).T
    q2, k2 = wq[:, 128:], wk[:, 128:]
    attn = np.concatenate([wq[:, 0:128], wk[:, 0:128], q2, q2, k2, k2, wv, wv[:, 128:], wo, wr], axis=1)
    w2 = f(L0_ffn_w2).reshape(NW, P, D).transpose(1, 0, 2)

    def columns(vec):
        return np.stack([vec[0:128], np.concatenate([vec[128:192], vec[128:192]])], axis=1)

    arrays = {
        "patches": img.transpose(1, 0, 2),
        "txt": f(txt),
        "tok_w": f(L0_tok_W).T.reshape(KT, P, D).transpose(1, 0, 2),
        "tok_b": columns(f(L0_tok_b)),
        "gammas": f(L0_attn_gammas),
        "gn_w": columns(f(L0_attn_gn_weight)),
        "gn_b": columns(f(L0_attn_gn_bias)),
        "attn_w": _stack(np, attn),
        "w1": _stack(np, f(L0_ffn_w1)),
        "w2": np.concatenate([w2, w2[:, :, 128:]], axis=2),
    }
    arrays = {n: np.ascontiguousarray(a) for n, a in arrays.items()}
    nc = bacc.Bacc("TRN2", target_bir_lowering=False, num_devices=1)
    args = [nc.dram_tensor(n, a.shape, F32, kind="ExternalInput").ap() for n, a in arrays.items()]
    out = nc.dram_tensor("out", (B, L, D), F32, kind="ExternalOutput").ap()
    early_fusion(nc, *args, out)
    r = run_bass_kernel_spmd(nc, [arrays], core_ids=[0])
    return r.results[0]["out"]
```

```python
from contextlib import ExitStack

import concourse.bass as bass
from concourse import mybir

F32 = mybir.dt.float32
F32R = mybir.dt.float32r
ALU = mybir.AluOpType
ACT = mybir.ActivationFunctionType
AX = mybir.AxisListType

P = 128
B = 8
D = 192
IMG = 36
TXT = 512
L = IMG + TXT
NT = -(-L // P)
LAST = L - (NT - 1) * P
HALF = L // 2
H = 3
HD = D // H
KT = 6
EPS = 1e-5
NEG = -3.0e38

SUMS = 64
KEY_LAST = SUMS + NT - 1
LX = (NT - 1) * P + KEY_LAST
WIDTH = [LX - I * P for I in range(NT)]
OFF = [sum(WIDTH[:I]) for I in range(NT)]
PW = sum(WIDTH)

E = 16
EW = [128] * 8 + [256] * 8
TILE_E = [e for e in range(E) for _ in range(EW[e] // P)]
NW = len(TILE_E)
LAST_OF = [max(k for k in range(NW) if TILE_E[k] == e) for e in range(E)]
TOPK = 8
W1_SHARE = NW * P // B
W2_PART = NW // 4
W2_HEAD = 1
CREDIT = 1

QK_W, V_W, O_W, R_W = 512, 256, D, E
AW = QK_W + V_W + O_W + R_W
DECAY_L = 127 + L + 1


def rows(I):
    return P if I < NT - 1 else LAST


def nth(b, per, k):
    return b * per + k


def early_fusion(nc, patches, txt, tok_w, tok_b, gammas, gn_w, gn_b, attn_w, w1, w2, out):
    ctx = ExitStack()
    phase_a, staging = ExitStack(), ExitStack()

    def sb(name, shape, dt=F32, scope=ctx):
        return scope.enter_context(nc.sbuf_tensor(name, shape, dt))

    def sem(name):
        return ctx.enter_context(nc.semaphore(name))

    with ctx:
        h = sb("h", [P, B, NT, D])
        ident = sb("ident", [P, P])
        ct = sb("ct", [E, L])
        ps = ctx.enter_context(nc.psum_tensor("ps", [P, 8, 512], F32))
        psf = ps[:, :, :].rearrange("p b n -> p (b n)")

        def sg(name, shape, dt=F32):
            return sb(name, shape, dt, staging)

        aw_raw = sg("aw_raw", [P, 2, AW])
        pat, tokw = sg("pat", [P, KT, B * IMG]), sg("tokw", [P, KT, D])
        tokb = sg("tokb", [P, 2])
        emb = sg("emb", [P, 2, B * IMG])
        gam = sg("gam", [P, H])
        drow = sg("drow", [P, H, DECAY_L])
        staging.close()
        w1_hi, w1_lo = sb("w1_hi", [P, 2, NW * P], F32R), sb("w1_lo", [P, 2, NW * P], F32R)
        w_raw = sb("w_raw", [P, W2_PART * 256])
        w1_raw = w_raw[:, 0:2 * W1_SHARE].rearrange("p (c n) -> p c n", c=2)
        w2_first = w_raw[:, :].rearrange("p (k n) -> p k n", k=W2_PART)

        def sa(name, shape, dt=F32):
            return sb(name, shape, dt, phase_a)

        decay = sa("decay", [P, H, L])
        xn = sa("xn", [P, NT, 256])
        xa_hi, xa_lo, xb = sa("xa_hi", [P, LX], F32R), sa("xa_lo", [P, LX], F32R), sa("xb", [P, LX], F32R)
        q01_hi, q01_lo = sa("q01_hi", [P, L], F32R), sa("q01_lo", [P, L], F32R)
        k01_hi, k01_lo = sa("k01_hi", [P, L], F32R), sa("k01_lo", [P, L], F32R)
        q2 = sa("q2", [P, L], F32R)
        k2_hi, k2_lo = sa("k2_hi", [P, L], F32R), sa("k2_lo", [P, L], F32R)
        sc = [sa(f"sc{i}", [P, PW]) for i in range(2)]
        pr1 = sa("pr1", [P, PW])
        v = sa("v", [P, NT, 3 * P])
        pt = sa("pt", [P, 4, 512])
        pr = [sa("pr0", [P, PW]), pr1]
        aw_hi, aw_lo = sa("aw_hi", [P, 2, AW], F32R), sa("aw_lo", [P, 2, AW], F32R)
        head_mean = sa("head_mean", [P, P])
        gnw, gnb = sa("gnw", [P, 2]), sa("gnb", [P, 2])
        lower_count = sa("lower_count", [P, NT])
        xn2 = sa("xn2", [P, NT, 256])
        ot = sa("ot", [P, 2, L])
        y = sa("y", [P, 3, L], F32R)
        y01_hi, y01_lo, y2 = y[:, 0, :], y[:, 1, :], y[:, 2, :]
        x2 = sa("x2", [P, 3, L], F32R)
        lt = sa("lt", [E, NT * P])
        st6, mv, veps = sa("st6", [P, NT, 6]), sa("mv", [P, NT, 2]), sa("veps", [P, NT])
        rstd = sa("rstd", [P, NT])
        st6b, mvb, vepsb, rstdb = sa("st6b", [P, NT, 6]), sa("mvb", [P, NT, 2]), sa("vepsb", [P, NT]), sa("rstdb", [P, NT])
        nmr, nmrb = sa("nmr", [P, NT]), sa("nmrb", [P, NT])
        neg_half, zeros = sa("neg_half", [P, NT]), sa("zeros", [P, NT])
        mx = [sa(f"mx{i}", [P, NT]) for i in range(2)]
        nm = [sa(f"nm{i}", [P, NT]) for i in range(2)]
        zero_score = [sa(f"zero_score{i}", [P, NT]) for i in range(2)]
        row_sum = [sa(f"row_sum{i}", [P, NT]) for i in range(2)]
        den = [sa(f"den{i}", [P, NT]) for i in range(2)]
        inv_den = [sa(f"inv_den{i}", [P, NT]) for i in range(2)]
        gst, gmv, gtot = sa("gst", [P, 2, 12]), sa("gmv", [P, 2, 2]), sa("gtot", [P, 2, 2])
        gvar, grstd = sa("gvar", [P, 2]), sa("grstd", [P, 2])
        gscale, gshift, gtmp = sa("gscale", [P, 2]), sa("gshift", [P, 2]), sa("gtmp", [P, 2])
        gsub = sa("gsub", [P, 2])
        lmax, lsub, lexp = sa("lmax", [P, NT]), sa("lsub", [P, NT, E]), sa("lexp", [P, NT, E])
        top, left = sa("top", [P, NT, TOPK]), sa("left", [P, NT, E])
        chosen, tsum, tinv, comb = sa("chosen", [P, NT, E]), sa("tsum", [P, NT]), sa("tinv", [P, NT]), sa("comb", [P, NT, E])
        phase_a.close()

        w2_staging = ExitStack()
        sb("x2_first", [P, B - 3, 3, L], F32, w2_staging)
        w2_others = sb("w2_others", [P, NW - W2_PART, 256], F32, w2_staging)
        w2_staging.close()
        x2_all = sb("x2_all", [P, B, 3, L], F32R)
        gate = [sb(f"gate{i}", [P, 2, HALF]) for i in range(4)]
        act = [sb(f"act{i}", [P, 2, HALF]) for i in range(3)]
        act_hi = [sb(f"act_hi{i}", [P, 2, HALF], F32R) for i in range(3)]
        act_lo = [sb(f"act_lo{i}", [P, 2, HALF], F32R) for i in range(3)]
        w2_hi, w2_lo = sb("w2_hi", [P, NW, P], F32R), sb("w2_lo", [P, NW, P], F32R)
        w2_r = sb("w2_r", [P, NW, P], F32R)
        out_a, out_r, out_t = sb("out_a", [P, L]), sb("out_r", [P, L]), sb("out_t", [P, NT, HD])

        decay_rows = nc.dram_tensor("decay_rows", [H, P * DECAY_L], F32).ap()
        x2_dram = nc.dram_tensor("x2_dram", [B, P, 3 * L], F32).ap()
        comb_dram = nc.dram_tensor("comb_dram", [B, E, L], F32).ap()

        ld_aw, ld_pat, ld_gam, ld_gn = sem("ld_aw"), [sem("ld_pat0"), sem("ld_pat1")], sem("ld_gam"), sem("ld_gn")
        ld_h0, ld_h = sem("ld_h0"), sem("ld_h")
        consts = sem("consts")
        decay_built, decay_stored, ld_decay = sem("decay_built"), sem("decay_stored"), sem("ld_decay")
        aw_hi_ready, aw_lo_ready = sem("aw_hi_ready"), sem("aw_lo_ready")
        emb_done, emb_copied, embt_done, embt_copied = sem("emb_done"), sem("emb_copied"), sem("embt_done"), sem("embt_copied")
        ln1_var, ln1_rstd, ln1_normed, xn_ready = sem("ln1_var"), sem("ln1_rstd"), sem("ln1_normed"), sem("xn_ready")
        ln2_rstd, ln2_normed = sem("ln2_rstd"), sem("ln2_normed")
        xt_done, xt_ext, xt_hi, xt_lo = sem("xt_done"), sem("xt_ext"), sem("xt_hi"), sem("xt_lo")
        qk_done, qk_hi, qk_lo = sem("qk_done"), sem("qk_hi"), sem("qk_lo")
        v_done, v_copied = sem("v_done"), sem("v_copied")
        s_done, decayed, nm_ready = sem("s_done"), sem("decayed"), sem("nm_ready")
        exp_done, den_ready, probs_ready = sem("exp_done"), sem("den_ready"), sem("probs_ready")
        probs_scaled = sem("probs_scaled")
        pt_done, pt_copied = sem("pt_done"), sem("pt_copied")
        o_done, o_copied = sem("o_done"), sem("o_copied")
        gn_part, gn_sum, gn_var = sem("gn_part"), sem("gn_sum"), sem("gn_var")
        y_coeff, y_hi, y_lo = sem("y_coeff"), sem("y_hi"), sem("y_lo")
        wo_done, wo_added, ln2_var, xn2_ready = sem("wo_done"), sem("wo_added"), sem("ln2_var"), sem("xn2_ready")
        first_normed, last_normed = sem("first_normed"), sem("last_normed")
        x2t_done, x2_hi, x2_lo, x2_stored = sem("x2t_done"), sem("x2_hi"), sem("x2_lo"), sem("x2_stored")
        lg_done, lt_copied, lgn_done, l_sub, l_exp = sem("lg_done"), sem("lt_copied"), sem("lgn_done"), sem("l_sub"), sem("l_exp")
        comb_ready, ct_done, ct_copied, ct_stored = sem("comb_ready"), sem("ct_done"), sem("ct_copied"), sem("ct_stored")
        phase = sem("phase")
        tick = {n: sem(f"tick_{n}") for n in ("dve", "pool", "pe")}
        ld_w1, ld_w2, w1_split = sem("ld_w1"), sem("ld_w2"), sem("w1_split")
        w2_hi_ready, w2_lo_ready, w2_split = sem("w2_hi_ready"), sem("w2_lo_ready"), sem("w2_split")
        ld_x2, ld_gate = sem("ld_x2"), [sem(f"ld_gate{i}") for i in range(4)]
        up_done, gelu_done, gated, act_hi_ready, act_lo_ready = sem("up_done"), sem("gelu_done"), sem("gated"), sem("act_hi_ready"), sem("act_lo_ready")
        down_done, acc_a_copied, acc_r_copied = sem("down_done"), sem("acc_a_copied"), sem("acc_r_copied")
        outt_done, out_ready, out_stored = sem("outt_done"), sem("out_ready"), sem("out_stored")

        block = ctx.enter_context(nc.Block())

        def apart(eng, name):
            eng.sem_inc(tick[name], 1)

        def iterations(eng, body):
            body(0, tail=False, router=False, more=True)
            body(1, tail=True, router=False, more=True)
            with eng.Fori(2, B - 1) as b:
                body(b, tail=True, router=True, more=True)
            body(B - 1, tail=True, router=True, more=False)

        def end_of_phase_a(eng):
            eng.drain().then_inc(phase, 1)
            eng.wait_ge(phase, 5)

        def tokens(ap, b, I):
            return ap[:rows(I), bass.ds(b, 1), I, :].rearrange("p a d -> p (a d)")

        @block.sync
        def _(sp):
            def load_h(b0, b1, s):
                src = txt[b0:b1]
                sp.dma_start(h[IMG:P, b0:b1, 0, :], src[:, 0:P - IMG, :].rearrange("b p d -> p b d")).then_inc(s, 16)
                for I in range(1, NT - 1):
                    lo = I * P - IMG
                    sp.dma_start(h[:, b0:b1, I, :], src[:, lo:lo + P, :].rearrange("b p d -> p b d")).then_inc(s, 16)
                sp.dma_start(h[0:LAST, b0:b1, NT - 1, :], src[:, TXT - LAST:TXT, :].rearrange("b p d -> p b d")).then_inc(s, 16)

            sp.dma_start(gam[:, :], gammas.partition_broadcast(P)).then_inc(ld_gam, 16)
            for i in range(2):
                part = slice(i * KT // 2, (i + 1) * KT // 2)
                sp.dma_start(pat[:, part, :], patches[:, part, :]).then_inc(ld_pat[i], 16)
                sp.dma_start(tokw[:, part, :], tok_w[:, part, :]).then_inc(ld_pat[i], 16)
            sp.dma_start(tokb[:, :], tok_b).then_inc(ld_pat[1], 16)
            load_h(0, 1, ld_h0)
            sp.dma_start(aw_raw[:, :, :], attn_w).then_inc(ld_aw, 16)
            load_h(1, B, ld_h)
            sp.dma_start(w1_raw, w1[:, :, 0:W1_SHARE]).then_inc(ld_w1, 16)
            sp.dma_start(gnw[:, :], gn_w).then_inc(ld_gn, 16)
            sp.dma_start(gnb[:, :], gn_b).then_inc(ld_gn, 16)
            sp.wait_ge(decay_built, 1)
            sp.dma_start(decay_rows.rearrange("h (p l) -> p h l", l=DECAY_L), drow[:, :, :]).then_inc(decay_stored, 16)
            sp.wait_ge(decay_stored, 16)
            shifted = decay_rows[:, 127:127 + P * (DECAY_L - 1)].rearrange("h (p l) -> p h l", l=DECAY_L - 1)
            sp.dma_start(decay[:, :, :], shifted[:, :, 0:L]).then_inc(ld_decay, 16)

            def store_x2(u, src):
                sp.wait_ge(x2_lo, nth(u, 3, 3))
                sp.dma_start(x2_dram[bass.ds(u, 1), :, :].rearrange("a p n -> p (a n)"),
                             src[:, :, :].rearrange("p c n -> p (c n)").bitcast(F32)).then_inc(x2_stored, 16)

            def store_ct(u):
                sp.wait_ge(ct_copied, CREDIT + nth(u, 1, 1))
                sp.dma_start(comb_dram[bass.ds(u, 1), :, :].rearrange("a e n -> e (a n)"),
                             ct[:, :]).then_inc(ct_stored, 16)

            def load_x2(b):
                if b:
                    sp.wait_ge(ld_x2, 16 * b)
                sp.dma_start(x2_all[:, b, :, :].bitcast(F32), x2_dram[b].rearrange("p (c n) -> p c n", c=3)).then_inc(ld_x2, 16)

            def body(b, tail, router, more):
                sp.wait_ge(w1_split, nth(b, 1, 1))
                if more:
                    sp.dma_start(w1_raw, w1[:, :, bass.ds((b + 1) * W1_SHARE, W1_SHARE)]).then_inc(ld_w1, 16)
                else:
                    sp.dma_start(w2_first, w2[:, 0:W2_PART, :]).then_inc(ld_w2, 16)
                if router:
                    store_x2(b - 2, x2)
                    store_ct(b - 2)

            iterations(sp, body)
            sp.wait_ge(exp_done, nth(B - 1, H, H))
            sp.wait_ge(o_done, nth(B - 1, 2, 1))
            sp.wait_ge(x2_stored, CREDIT + 16 * (B - 2))
            load_x2(0)
            sp.wait_ge(ld_w2, 16)
            sp.dma_start(w2_others[:, :, :], w2[:, W2_PART:NW, :]).then_inc(ld_w2, 16)
            load_x2(1)
            sp.wait_ge(o_done, nth(B - 1, 2, 2))
            sp.wait_ge(ct_stored, CREDIT + 16 * (B - 2))
            for e in range(4):
                sp.dma_start(gate[e][:, :, :].rearrange("p a n -> p (a n)"),
                             comb_dram[0, e, :].partition_broadcast(P)).then_inc(ld_gate[e], 16)
            for b in range(2, B - 3):
                load_x2(b)
            store_x2(B - 2, x2)
            store_ct(B - 2)
            store_x2(B - 1, y)
            sp.wait_ge(x2_stored, CREDIT + 16 * B)
            end_of_phase_a(sp)

            def gates(b, first, end=E):
                for e in range(first, end):
                    last = LAST_OF[(e - 4) % E] + 1
                    sp.wait_ge(gated, nth(b, NW, last) if e >= 4 else nth(b - 1, NW, last))
                    src = comb_dram[bass.ds(b, 1), e, :].rearrange("a n -> (a n)").partition_broadcast(P)
                    sp.dma_start(gate[e % 4][:, :, :].rearrange("p a n -> p (a n)"), src).then_inc(ld_gate[e % 4], 16)

            def store_out(b):
                sp.wait_ge(out_ready, nth(b, 2, 2))
                dst = out[bass.ds(b, 1), :, :].rearrange("a n d -> (a n) d")
                src = h[:, bass.ds(b, 1), :, :].rearrange("p a t d -> p (a t) d")
                sp.dma_start(dst[0:(NT - 1) * P, :].rearrange("(t p) d -> p t d", p=P), src[:, 0:NT - 1, :]).then_inc(out_stored, 16)
                sp.dma_start(dst[(NT - 1) * P:L, :], src[0:LAST, NT - 1, :]).then_inc(out_stored, 16)

            store_ct(B - 1)
            gates(0, 4)
            sp.wait_ge(ct_stored, CREDIT + 16 * B)
            sp.wait_ge(w2_split, NW // W2_PART - 1)
            for b in range(B - 3, B):
                load_x2(b)
            with sp.Fori(1, B) as b:
                gates(b, 0)
                store_out(b - 1)
            store_out(B - 1)
            sp.wait_ge(out_stored, 32 * B)

        @block.gpsimd
        def _(pool):
            pool.memset(ident[:, :], 0.0)
            pool.drain()
            pool.affine_select(out=ident[:, :], in_=ident[:, :], compare_op=ALU.not_equal, fill=1.0,
                               base=0, pattern=[[-1, P]], channel_multiplier=1).then_inc(consts, 1)
            pool.memset(zeros[:, :], 0.0)
            pool.memset(neg_half[:, :], -0.5).then_inc(consts, 1)
            for t in (0, 1):
                pool.memset(sc[t][:, :], NEG)
            pool.drain()
            for t in (0, 1):
                for I in range(1, NT):
                    at = OFF[I] + WIDTH[I] - (NT - 1)
                    last = pool.memset(sc[t][:, at:at + I], 0.0)
            last.then_inc(consts, 1)
            pool.memset(v[:, :, :], 0.0)
            pool.memset(lt[:, :], 0.0)
            pool.memset(xn2[:, NT - 1, :], 0.0)
            pool.memset(head_mean[:, :], 0.0)
            pool.drain()
            pool.memset(head_mean[0:HD, 0:HD], 1.0 / HD)
            pool.memset(head_mean[HD:P, HD:P], 1.0 / HD)
            pool.drain()

            def rstd_of(b, var_sem, rs, m2, ve, nmean, ready):
                pool.wait_ge(var_sem, nth(b, 1, 1))
                pool.tensor_tensor(rs[:, :], ve[:, :], neg_half[:, :], ALU.pow)
                pool.tensor_tensor(nmean[:, :], zeros[:, :], m2[:, :, 0], ALU.subtract)
                pool.drain()
                pool.tensor_tensor(nmean[:, :], nmean[:, :], rs[:, :], ALU.mult).then_inc(ready, 1)

            def twice(normed, n, dst, ready):
                pool.wait_ge(normed, n)
                apart(pool, "pool")
                pool.tensor_copy(dst[:, :, D:256], dst[:, :, P:D]).then_inc(ready, 1)

            def halve_w1(b):
                pool.wait_ge(ld_w1, nth(b, 16, 16))
                apart(pool, "pool")
                if isinstance(b, int) and b == 0:
                    pool.wait_ge(aw_lo_ready, 1)
                    pool.wait_ge(embt_copied, 1)
                    pool.wait_ge(ld_decay, 16)
                cols = bass.ds(b * W1_SHARE, W1_SHARE)
                for c in range(2):
                    pool.tensor_copy(w1_hi[:, c, cols], w1_raw[:, c, :])
                pool.drain()
                for c in range(2):
                    last = pool.tensor_tensor(w1_lo[:, c, cols], w1_raw[:, c, :], w1_hi[:, c, cols], ALU.subtract)
                last.then_inc(w1_split, 1)

            rstd_of(0, ln1_var, rstd, mv, veps, nmr, ln1_rstd)
            pool.wait_ge(ld_gn, 32)

            def gn_coefficients(t):
                pool.wait_ge(gn_var, nth(t, 1, 1))
                pool.tensor_tensor(grstd[:, :], gvar[:, :], neg_half[:, 0:2], ALU.pow)
                pool.drain()
                pool.tensor_tensor(gscale[:, :], grstd[:, :], gnw[:, :], ALU.mult)
                pool.drain()
                pool.tensor_tensor(gsub[:, :], gtot[:, :, 0], gscale[:, :], ALU.mult)
                pool.drain()
                pool.tensor_tensor(gshift[:, :], gnb[:, :], gsub[:, :], ALU.subtract).then_inc(y_coeff, 1)

            def second_norm(u):
                rstd_of(u, ln2_var, rstdb, mvb, vepsb, nmrb, ln2_rstd)
                twice(ln2_normed, nth(u, 1, 1), xn2, xn2_ready)

            def body(b, tail, router, more):
                if router:
                    second_norm(b - 2)
                if more:
                    rstd_of(b + 1, ln1_var, rstd, mv, veps, nmr, ln1_rstd)
                halve_w1(b)
                if tail:
                    gn_coefficients(b - 1)
                if more:
                    twice(ln1_normed, nth(b, 1, 1), xn, xn_ready)

            iterations(pool, body)
            gn_coefficients(B - 1)
            second_norm(B - 2)
            rstd_of(B - 1, ln2_var, rstdb, mvb, vepsb, nmrb, ln2_rstd)
            end_of_phase_a(pool)

            pool.wait_ge(ld_w2, 32)
            for q in range(1, NW // W2_PART):
                part = slice(q * W2_PART, (q + 1) * W2_PART)
                src = w2_others[:, (q - 1) * W2_PART:q * W2_PART, :]
                pool.tensor_copy(w2_hi[:, part, :], src[:, :, 0:P])
                pool.tensor_copy(w2_r[:, part, :], src[:, :, P:256])
                pool.drain()
                pool.tensor_tensor(w2_lo[:, part, :], src[:, :, 0:P], w2_hi[:, part, :], ALU.subtract)
                pool.tensor_tensor(w2_r[:, part, HD:P], src[:, :, P + HD:256], w2_r[:, part, HD:P],
                                   ALU.subtract).then_inc(w2_split, 1)

        @block.scalar
        def _(sc_eng):
            a = sc_eng

            def copy(dst, src):
                return a.activation(dst, src, ACT.Copy)

            a.wait_ge(ld_aw, 16)
            copy(aw_hi[:, :, :], aw_raw[:, :, :]).then_inc(aw_hi_ready, 1)
            a.wait_ge(emb_done, 1)
            a.activation(emb[:, 0, :], ps[:, 0, 0:B * IMG], ACT.Identity, bias=tokb[:, 0:1])
            a.activation(emb[0:HD, 1, :], ps[0:HD, 1, 0:B * IMG], ACT.Identity, bias=tokb[0:HD, 1:2]).then_inc(emb_copied, 1)

            def norm_apply(b, rs, nmean, rs_ready, dst, normed, tiles=range(NT)):
                a.wait_ge(rs_ready, nth(b, 1, 1))
                for I in tiles:
                    r = rows(I)
                    last = a.activation(dst[:r, I, 0:D], tokens(h, b, I), ACT.Identity, bias=nmean[:r, I:I + 1],
                                        scale=rs[:r, I:I + 1])
                last.then_inc(normed, 1)

            def x_hi(b, c):
                a.wait_ge(xt_ext, nth(b, 2, c + 1))
                copy((xa_hi, xb)[c][:, :], psf[:, 1024 * c:1024 * c + LX]).then_inc(xt_hi, 1)

            def halves(bank):
                return ps[:, bank:bank + 2, 0:HALF]

            def two(ap):
                return ap.rearrange("p (a n) -> p a n", a=2)

            def scale_probs(b):
                a.wait_ge(den_ready, nth(b, 1, 1))
                for I in range(2):
                    t = pr[0][:, OFF[I]:OFF[I] + WIDTH[I]]
                    last = a.activation(t, t, ACT.Copy, scale=inv_den[0][:, I:I + 1])
                last.then_inc(probs_scaled, 1)

            def qk_round(b, tiles):
                for i, (dst, bank) in enumerate(((q01_hi, 6), (k01_hi, 4), (q2, 0), (k2_hi, 2))):
                    if i not in tiles:
                        continue
                    a.wait_ge(qk_done, nth(b, 4, i + 1))
                    copy(two(dst[:, :]), halves(bank)).then_inc(qk_hi, 1)

            def v_copy(b, parts):
                for i, (bank, t0, n) in enumerate(((5, 0, 2), (4, 2, 2), (3, 4, 1))):
                    if i not in parts:
                        continue
                    r = P if n == 2 else KEY_LAST
                    a.wait_ge(v_done, nth(b, 3, i + 1))
                    src = ps[:r, bank, 0:256 * n].rearrange("p (t d) -> p t d", t=n)
                    copy(v[:r, t0:t0 + n, 0:HD], src[:, :, 0:HD])
                    copy(v[:r, t0:t0 + n, P + HD:3 * P], src[:, :, HD:256]).then_inc(v_copied, 1)

            def exps(b, hh, tiles=range(NT)):
                s = hh % 2
                if hh == 0 and not (isinstance(b, int) and b == 0):
                    a.wait_ge(pt_done, nth(b - 1, 4 * H, 4 * H))
                for I in tiles:
                    if I == 0:
                        a.wait_ge(nm_ready, nth(b, 2 * H, 2 * hh + 1))
                    elif I == 1:
                        a.wait_ge(nm_ready, nth(b, 2 * H, 2 * hh + 2))
                        a.activation(zero_score[s][:, :], nm[s][:, :], ACT.Exp)
                    r = rows(I)
                    cols = slice(OFF[I], OFF[I] + WIDTH[I])
                    last = a.activation(pr[s][:r, cols], sc[s][:r, cols], ACT.Exp, bias=nm[s][:r, I:I + 1],
                                        accum_out=row_sum[s][:r, I:I + 1])
                    if I == NT - 1:
                        last.then_inc(exp_done, 1)

            def pt_copy(b, hh, groups=(0, 1, 2, 3)):
                for g in groups:
                    a.wait_ge(pt_done, nth(b, 4 * H, 4 * hh + g + 1))
                    if g == 0:
                        last = copy(pt[:KEY_LAST, 0, :], ps[:KEY_LAST, 5, :])
                    elif g == 1:
                        copy(pt[:KEY_LAST, 1, 0:LAST], ps[:KEY_LAST, 4, 0:LAST])
                        last = copy(pt[:, 1, 64:64 + 3 * P], ps[:, 4, 64:64 + 3 * P])
                    elif g == 2:
                        last = copy(pt[:, 2, :], ps[:, 5, :])
                    else:
                        last = copy(pt[:, 3, 0:3 * P], ps[:, 4, 0:3 * P])
                    last.then_inc(pt_copied, 1)

            def o_copy(b, i):
                a.wait_ge(o_done, nth(b, 2, i + 1))
                if i == 0 and not (isinstance(b, int) and b == 0):
                    a.wait_ge(y_lo, nth(b - 1, 2, 1))
                tail = 64 * i
                copy(ot[:, i, 0:512], ps[:, 6, :])
                copy(ot[:, i, 512:L], ps[:, 7, tail:tail + LAST]).then_inc(o_copied, 1)

            def y_of(dst, i):
                return a.activation(dst, ot[:, i, :], ACT.Identity, bias=gshift[:, i:i + 1], scale=gscale[:, i:i + 1])

            def y_round(t, i):
                if i == 0:
                    a.wait_ge(y_coeff, nth(t, 1, 1))
                y_of((y01_hi, y2)[i][:, :], i)

            def y_whole(t, i):
                y_of(ot[:, i, :], i).then_inc(y_hi, 1)

            def x2_round(t, bank, dst):
                a.wait_ge(x2t_done, nth(t, 3, 1))
                if dst is x2:
                    a.wait_ge(x2_stored, CREDIT + 16 * t)
                copy(dst[:, 0, 512:L], ps[:, bank, X2_AT:X2_AT + LAST])
                copy(dst[:, 2, 512:L], ps[:, bank, X2_AT + 64:X2_AT + 64 + LAST]).then_inc(x2_hi, 1)
                a.wait_ge(x2t_done, nth(t, 3, 2))
                copy(dst[:, 0, 0:512], ps[:, 6, :]).then_inc(x2_hi, 1)
                a.wait_ge(x2t_done, nth(t, 3, 3))
                copy(dst[:, 2, 0:512], ps[:, 7, :]).then_inc(x2_hi, 1)

            def logits_copy(t, bank):
                a.wait_ge(lg_done, nth(t, 1, 1))
                copy(lt[:, 0:L].rearrange("p (a n) -> p a n", a=2), ps[0:E, bank:bank + 2, 0:HALF]).then_inc(lt_copied, 1)

            def logits_exp(t):
                a.wait_ge(l_sub, nth(t, 1, 1))
                a.activation(lexp[:, :, :], lsub[:, :, :], ACT.Exp).then_inc(l_exp, 1)

            def comb_copy(t, bank):
                a.wait_ge(ct_done, nth(t, 1, 1))
                a.wait_ge(ct_stored, CREDIT + 16 * t)
                copy(ct[:, 0:512], ps[0:E, bank, :])
                copy(ct[:, 512:L], ps[0:E, bank + 1, 0:LAST]).then_inc(ct_copied, 1)

            def body(b, tail, router, more):
                t, u = b - 1, b - 2
                qk_round(b, (0,))
                if tail:
                    scale_probs(t)
                qk_round(b, (1, 2, 3))
                if tail:
                    pt_copy(t, 2)
                if router:
                    norm_apply(u, rstdb, nmrb, ln2_rstd, xn2, ln2_normed)
                exps(b, 0, (0,))
                if tail:
                    o_copy(t, 1)
                exps(b, 0, (1, 2, 3, 4))
                if router:
                    x2_round(u, 1, x2)
                exps(b, 1, (0,))
                v_copy(b, (0,))
                exps(b, 1, (1,))
                v_copy(b, (1,))
                exps(b, 1, (2,))
                v_copy(b, (2,))
                exps(b, 1, (3,))
                pt_copy(b, 0, (0, 1))
                if router:
                    logits_copy(u, 6)
                exps(b, 1, (4,))
                pt_copy(b, 0, (2, 3))
                if more:
                    norm_apply(b + 1, rstd, nmr, ln1_rstd, xn, ln1_normed)
                if router:
                    logits_exp(u)
                if tail:
                    y_round(t, 0)
                pt_copy(b, 1, (0, 1))
                if tail:
                    y_whole(t, 0)
                    y_round(t, 1)
                pt_copy(b, 1, (2, 3))
                if tail:
                    y_whole(t, 1)
                exps(b, 2, (0,))
                o_copy(b, 0)
                if not more:
                    exps(b, 2, (1, 2, 3, 4))
                if more:
                    x_hi(b + 1, 0)
                if router:
                    comb_copy(u, 4 if more else 0)
                if more:
                    x_hi(b + 1, 1)
                    exps(b, 2, (1, 2, 3, 4))

            def drain(t, u):
                scale_probs(t)
                pt_copy(t, 2)
                o_copy(t, 1)
                for i in range(2):
                    y_round(t, i)
                    y_whole(t, i)
                norm_apply(u, rstdb, nmrb, ln2_rstd, xn2, ln2_normed)
                x2_round(u, 4, x2)
                norm_apply(t, rstdb, nmrb, ln2_rstd, xn2, last_normed, range(DVE_TILES, NT))
                logits_copy(u, 0)
                x2_round(t, 4, y)
                logits_exp(u)
                logits_copy(t, 6)
                logits_exp(t)
                comb_copy(u, 4)
                a.activation(zero_score[0][:, :], nm[0][:, :], ACT.Gelu_apprx_tanh)
                comb_copy(t, 6)

            for s in (x2_stored, ct_stored, ct_copied):
                a.sem_inc(s, CREDIT)
            norm_apply(0, rstd, nmr, ln1_rstd, xn, first_normed, range(DVE_TILES, NT))
            x_hi(0, 0)
            x_hi(0, 1)
            iterations(a, body)
            drain(B - 1, B - 2)
            end_of_phase_a(a)

            def round_w2(k0, k1):
                copy(w2_hi[:, k0:k1, :], w2_first[:, k0:k1, 0:P])
                copy(w2_r[:, k0:k1, :], w2_first[:, k0:k1, P:256]).then_inc(w2_hi_ready, 1)

            def gelu(b, k):
                a.wait_ge(up_done, nth(b, NW, k + 1))
                if k >= 3 or not isinstance(b, int) or b:
                    a.wait_ge(act_lo_ready, nth(b, NW, k - 2))
                a.activation(act[k % 3][:, :, :], ps[:, 2 * (k % 2):2 * (k % 2) + 2, 0:HALF],
                             ACT.Gelu_apprx_tanh).then_inc(gelu_done, 1)

            def act_round(b, k):
                a.wait_ge(gated, nth(b, NW, k + 1))
                if k >= 3 or not isinstance(b, int) or b:
                    a.wait_ge(down_done, nth(b, NW, k - 2))
                copy(act_hi[k % 3][:, :, :], act[k % 3][:, :, :]).then_inc(act_hi_ready, 1)

            def ffn(b, more):
                gelu(b, 2)
                for k in range(2, NW - 1):
                    gelu(b, k + 1)
                    act_round(b, k)
                if more:
                    gelu(b + 1, 0)
                act_round(b, NW - 1)
                if more:
                    act_round(b + 1, 0)
                    gelu(b + 1, 1)
                a.wait_ge(down_done, nth(b, NW, NW))
                copy(out_a[:, :].rearrange("p (a n) -> p a n", a=2), ps[:, 4:6, 0:HALF]).then_inc(acc_a_copied, 1)
                if more:
                    act_round(b + 1, 1)

            gelu(0, 0)
            gelu(0, 1)
            round_w2(0, W2_HEAD)
            act_round(0, 0)
            act_round(0, 1)
            round_w2(W2_HEAD, W2_PART)
            ffn(0, True)
            with a.Fori(1, B - 1) as b:
                ffn(b, True)
            ffn(B - 1, False)

        @block.vector
        def _(dve):
            dve.memset(drow[:, :, :], 0.0)
            dve.drain()
            dve.memset(drow[:, :, 127:128], 1.0)
            dve.wait_ge(ld_gam, 16)
            for hh in range(H):
                dve.tensor_copy(drow[:, hh, 128:129], gam[:, hh:hh + 1])
            n = 1
            while n < L - 1:
                m = min(n, L - 1 - n)
                dve.drain()
                for hh in range(H):
                    last = dve.tensor_scalar(drow[:, hh, 128 + n:128 + n + m], drow[:, hh, 128:128 + m],
                                             drow[:, hh, 127 + n:128 + n], None, ALU.mult)
                n += m
            last.then_inc(decay_built, 1)
            dve.memset(mv[:, :, :], 1.0)
            dve.memset(xn[:, NT - 1, :], 0.0)
            dve.wait_ge(aw_hi_ready, 1)
            dve.tensor_tensor(aw_lo[:, :, :], aw_raw[:, :, :], aw_hi[:, :, :], ALU.subtract).then_inc(aw_lo_ready, 1)

            def norm_stats(b, s6, m2, ve, signal):
                norm_parts(b, s6)
                dve.drain()
                norm_join(s6, m2, ve, signal)

            def norm_parts(b, s6, tiles=range(NT)):
                for I in tiles:
                    dve.bn_stats(s6[:rows(I), I, :], tokens(h, b, I))

            def norm_join(s6, m2, ve, signal):
                for I in range(NT):
                    dve.bn_aggr(m2[:rows(I), I, :], s6[:rows(I), I, :])
                dve.drain()
                dve.tensor_scalar(ve[:, :], m2[:, :, 1], EPS, None, ALU.add).then_inc(signal, 1)

            def norm_share(b, rs, nmean, rs_ready, dst, normed):
                dve.wait_ge(rs_ready, nth(b, 1, 1))
                for I in range(NT):
                    r = rows(I)
                    for at, f0 in ((0, 0), (D, P)):
                        if at or I < DVE_TILES:
                            last = dve.tensor_scalar(dst[:r, I, at:at + D - f0], tokens(h, b, I)[:, f0:D],
                                                     rs[:r, I:I + 1], nmean[:r, I:I + 1], ALU.mult, ALU.add)
                last.then_inc(normed, 1)

            def image_tokens(i):
                return dve.tensor_copy(h[0:IMG, 2 * i:2 * i + 2, 0, :],
                                       ps[0:IMG, 2 + i, 0:2 * D].rearrange("p (b d) -> p b d", b=2))

            dve.wait_ge(ld_h0, 16 * NT)
            norm_parts(0, st6, range(1, NT))
            dve.wait_ge(embt_done, 1)
            image_tokens(0)
            dve.drain()
            norm_parts(0, st6, (0,))
            dve.drain()
            norm_join(st6, mv, veps, ln1_var)
            for i in range(1, B // 2):
                last = image_tokens(i)
            last.then_inc(embt_copied, 1)
            norm_share(0, rstd, nmr, ln1_rstd, xn, first_normed)
            for t in (0, 1):
                dve.memset(mx[t][:, :], 0.0)
                dve.memset(row_sum[t][:, :], 1.0)
            dve.memset(mvb[:, :, :], 1.0)
            for I in range(NT):
                dve.memset(lower_count[:, I:I + 1], float((P - 1) * I))

            def sub(dst, src, hi):
                return dve.tensor_tensor(dst, src, hi, ALU.subtract)

            def halves(bank, p0=0):
                return ps[p0:P, bank:bank + 2, 0:HALF]

            def two(ap):
                return ap.rearrange("p (a n) -> p a n", a=2)

            def x_ext(b):
                for i, bank in enumerate((0, 2)):
                    dve.wait_ge(xt_done, nth(b, 2, i + 1))
                    dve.memset(ps[:, bank + 1, LAST:SUMS], 0.0)
                    dve.tensor_reduce(ps[:, bank + 1, SUMS:KEY_LAST],
                                      ps[:, bank, :].rearrange("p (t n) -> p t n", n=P), AX.X, ALU.add).then_inc(xt_ext, 1)

            def x_lo(b, chunks=(0, 1)):
                for c in chunks:
                    dve.wait_ge(xt_hi, nth(b, 2, c + 1))
                    if c == 0:
                        sub(xa_lo[:, :], psf[:, 0:LX], xa_hi[:, :]).then_inc(xt_lo, 1)
                    else:
                        sub(xb[HD:P, :], psf[HD:P, 1024:1024 + LX], xb[HD:P, :]).then_inc(xt_lo, 1)

            def qk_rest(b, tiles):
                for i, (dst, hi, bank) in enumerate(((q01_lo, q01_hi, 6), (k01_lo, k01_hi, 4), (q2, q2, 0), (k2_lo, k2_hi, 2))):
                    if i not in tiles:
                        continue
                    p0 = HD if dst is q2 else 0
                    dve.wait_ge(qk_hi, nth(b, 4, i + 1))
                    sub(two(dst[p0:P, :]), halves(bank, p0), two(hi[p0:P, :])).then_inc(qk_lo, 1)

            def apply_decay(b, hh):
                s = hh % 2
                for I in range(NT):
                    r, n = rows(I), L - P * I
                    if I <= 2:
                        dve.wait_ge(s_done, nth(b, 3 * H, 3 * hh + I + 1))
                        apart(dve, "dve")
                    dst, tab = sc[s][:r, OFF[I]:OFF[I] + n], decay[:r, hh, 0:n]
                    if I == 0:
                        dst, tab, src = two(dst), two(tab), ps[:, 0:2, 0:HALF]
                    elif I == 1:
                        src = ps[:, 2, 0:n]
                    else:
                        src = ps[:r, 3, S_AT[I]:S_AT[I] + n]
                    dve.tensor_tensor_reduce(out=dst, in0=src, in1=tab, scale=1.0 / 8, scalar=0.0 if I else NEG,
                                             op0=ALU.mult, op1=ALU.max,
                                             accum_out=mx[s][:r, I:I + 1]).then_inc(decayed, 1)
                    if I in (0, NT - 1):
                        dve.drain()
                        cols = slice(0, 1) if I == 0 else slice(1, NT)
                        dve.tensor_scalar(nm[s][:, cols], mx[s][:, cols], -1.0, None, ALU.mult).then_inc(nm_ready, 1)

            def normalise(b, hh):
                s = hh % 2
                dve.wait_ge(exp_done, nth(b, H, hh + 1))
                dve.tensor_tensor(den[s][:, :], zero_score[s][:, :], lower_count[:, :], ALU.mult)
                dve.drain()
                dve.tensor_tensor(den[s][:, :], den[s][:, :], row_sum[s][:, :], ALU.add)
                dve.drain()
                last = dve.reciprocal(inv_den[s][:, :], den[s][:, :])
                if hh == 2:
                    last.then_inc(den_ready, 1)
                dve.drain()
                for I in range(2 if hh == 2 else 0, NT):
                    t = pr[s][:rows(I), OFF[I]:OFF[I] + WIDTH[I]]
                    last = dve.tensor_scalar(t, t, inv_den[s][:rows(I), I:I + 1], None, ALU.mult)
                last.then_inc(probs_ready, 1)

            def gn_partial(t):
                for i in range(2):
                    dve.wait_ge(o_copied, nth(t, 2, i + 1))
                    for j in range(2):
                        dve.bn_stats(gst[:, i, 6 * j:6 * j + 6], ot[:, i, j * HALF:(j + 1) * HALF])
                dve.drain()
                for i in range(2):
                    dve.bn_aggr(gmv[:, i, :], gst[:, i, :])
                dve.drain()
                dve.tensor_tensor(gtmp[:, :], gmv[:, :, 0], gmv[:, :, 0], ALU.mult)
                dve.drain()
                dve.tensor_tensor(gmv[:, :, 1], gmv[:, :, 1], gtmp[:, :], ALU.add).then_inc(gn_part, 1)

            def gn_variance(t):
                dve.wait_ge(gn_sum, nth(t, 1, 1))
                dve.tensor_copy(gtot[:, :, :], ps[:, 2, GN_AT:GN_AT + 4].rearrange("p (i k) -> p i k", i=2))
                dve.drain()
                dve.tensor_tensor(gtmp[:, :], gtot[:, :, 0], gtot[:, :, 0], ALU.mult)
                dve.drain()
                dve.tensor_tensor(gvar[:, :], gtot[:, :, 1], gtmp[:, :], ALU.subtract)
                dve.drain()
                dve.tensor_scalar(gvar[:, :], gvar[:, :], 0.0, EPS, ALU.max, ALU.add).then_inc(gn_var, 1)

            def y_rest(t):
                for i, (p0, lo, hi) in enumerate(((0, y01_lo, y01_hi), (HD, y2, y2))):
                    dve.wait_ge(y_hi, nth(t, 2, i + 1))
                    sub(lo[p0:P, :], ot[p0:P, i, :], hi[p0:P, :]).then_inc(y_lo, 1)

            def add_attention(t, banks, parts=(0, 1, 2)):
                for i in parts:
                    bank, t0, n = banks[i], 2 * i, (2, 2, 1)[i]
                    r = P if n == 2 else LAST
                    dve.wait_ge(wo_done, nth(t, 3, i + 1))
                    dst = h[:r, bass.ds(t, 1), t0:t0 + n, :].rearrange("p a t d -> p (a t) d")
                    src = ps[:r, bank, 0:256 * n].rearrange("p (t d) -> p t d", t=n)[:, :, 0:D]
                    dve.tensor_tensor(dst, src, dst, ALU.add).then_inc(wo_added, 1)
                dve.drain()

            def x2_rest(t, bank, dst):
                for i in range(3):
                    dve.wait_ge(x2_hi, nth(t, 3, i + 1))
                    if i == 0:
                        sub(dst[:, 1, 512:L], ps[:, bank, X2_AT:X2_AT + LAST], dst[:, 0, 512:L])
                        last = sub(dst[HD:P, 2, 512:L], ps[HD:P, bank, X2_AT + 64:X2_AT + 64 + LAST], dst[HD:P, 2, 512:L])
                    elif i == 1:
                        last = sub(dst[:, 1, 0:512], ps[:, 6, :], dst[:, 0, 0:512])
                    else:
                        last = sub(dst[HD:P, 2, 0:512], ps[HD:P, 7, :], dst[HD:P, 2, 0:512])
                    last.then_inc(x2_lo, 1)

            def wide(ap, n):
                return ap.unsqueeze(2).broadcast_to([P, NT, n])

            def router_shift(t):
                dve.wait_ge(lgn_done, nth(t, 1, 1))
                logits = ps[:, 2, LG_AT:LG_AT + NT * E].rearrange("p (t e) -> p t e", t=NT)
                dve.tensor_reduce(lmax[:, :], logits, AX.X, ALU.max)
                dve.drain()
                dve.tensor_tensor(lsub[:, :, :], logits, wide(lmax[:, :], E), ALU.subtract).then_inc(l_sub, 1)

            def router_choose(t):
                dve.wait_ge(l_exp, nth(t, 1, 1))
                apart(dve, "dve")
                for I in range(NT):
                    dve.max(top[:, I, :], lexp[:, I, :])
                dve.drain()
                for I in range(NT):
                    dve.match_replace(left[:, I, :], top[:, I, :], lexp[:, I, :], -1.0)
                dve.tensor_reduce(tsum[:, :], top[:, :, :], AX.X, ALU.add)
                dve.drain()
                dve.reciprocal(tinv[:, :], tsum[:, :])
                dve.tensor_scalar(left[:, :, :], left[:, :, :], 0.0, None, ALU.is_lt)
                dve.drain()
                dve.tensor_tensor(chosen[:, :, :], left[:, :, :], lexp[:, :, :], ALU.mult)
                dve.drain()
                dve.tensor_tensor(comb[:, :, :], chosen[:, :, :], wide(tinv[:, :], E), ALU.mult).then_inc(comb_ready, 1)

            def body(b, tail, router, more):
                t, u = b - 1, b - 2
                if isinstance(b, int) and b == 0:
                    dve.wait_ge(ld_h, 16 * NT)
                qk_rest(b, (0,))
                if router:
                    norm_parts(u, st6b, (0, 1))
                qk_rest(b, (1, 2))
                if router:
                    norm_parts(u, st6b, (2, 3))
                qk_rest(b, (3,))
                if router:
                    norm_parts(u, st6b, (4,))
                    dve.drain()
                    norm_join(st6b, mvb, vepsb, ln2_var)
                if isinstance(b, int) and b == 0:
                    dve.wait_ge(ld_decay, 16)
                    dve.wait_ge(consts, 3)
                apply_decay(b, 0)
                if more:
                    norm_stats(b + 1, st6, mv, veps, ln1_var)
                apply_decay(b, 1)
                normalise(b, 0)
                if router:
                    x2_rest(u, 1, x2)
                if tail:
                    gn_partial(t)
                normalise(b, 1)
                if tail:
                    gn_variance(t)
                if router:
                    router_shift(u)
                    router_choose(u)
                apply_decay(b, 2)
                if tail:
                    y_rest(t)
                if more:
                    x_ext(b + 1)
                    x_lo(b + 1, (0,))
                    if tail:
                        add_attention(t, (6, 4, 5), (0,))
                    x_lo(b + 1, (1,))
                    if tail:
                        add_attention(t, (6, 4, 5), (1, 2))
                normalise(b, 2)
                if not more:
                    add_attention(t, (6, 7, 3))

            def drain(t, u):
                gn_partial(t)
                gn_variance(t)
                norm_stats(u, st6b, mvb, vepsb, ln2_var)
                y_rest(t)
                for i, tiles in enumerate(((0, 1), (2, 3), (4,))):
                    add_attention(t, (0, 1, 3), (i,))
                    norm_parts(t, st6b, tiles)
                dve.drain()
                dve.wait_ge(ln2_rstd, nth(u, 1, 1))
                norm_join(st6b, mvb, vepsb, ln2_var)
                x2_rest(u, 4, x2)
                norm_share(t, rstdb, nmrb, ln2_rstd, xn2, last_normed)
                x2_rest(t, 4, y)
                router_shift(u)
                router_choose(u)
                router_shift(t)
                dve.wait_ge(ct_done, nth(u, 1, 1))
                router_choose(t)

            x_ext(0)
            x_lo(0)
            iterations(dve, body)
            drain(B - 1, B - 2)
            end_of_phase_a(dve)

            def w2_rest(i, k0, k1):
                dve.wait_ge(w2_hi_ready, i + 1)
                sub(w2_lo[:, k0:k1, :], w2_first[:, k0:k1, 0:P], w2_hi[:, k0:k1, :])
                sub(w2_r[:, k0:k1, HD:P], w2_first[:, k0:k1, P + HD:256], w2_r[:, k0:k1, HD:P]).then_inc(w2_lo_ready, 1)

            def weigh(b, k):
                e = TILE_E[k]
                dve.wait_ge(gelu_done, nth(b, NW, k + 1))
                dve.wait_ge(ld_gate[e % 4], 16 * (b * (E // 4) + e // 4 + 1))
                dve.tensor_tensor(act[k % 3][:, :, :], act[k % 3][:, :, :], gate[e % 4][:, :, :],
                                  ALU.mult).then_inc(gated, 1)

            def act_rest(b, k):
                dve.wait_ge(act_hi_ready, nth(b, NW, k + 1))
                sub(act_lo[k % 3][:, :, :], act[k % 3][:, :, :], act_hi[k % 3][:, :, :]).then_inc(act_lo_ready, 1)

            def ffn(b, more):
                weigh(b, 2)
                for k in range(2, NW - 1):
                    weigh(b, k + 1)
                    act_rest(b, k)
                if more:
                    weigh(b + 1, 0)
                act_rest(b, NW - 1)
                if more:
                    act_rest(b + 1, 0)
                dve.wait_ge(down_done, nth(b, NW, NW))
                dve.tensor_copy(out_r[:, :].rearrange("p (a n) -> p a n", a=2), ps[:, 6:8, 0:HALF]).then_inc(acc_r_copied, 1)
                if more:
                    weigh(b + 1, 1)
                dve.wait_ge(outt_done, nth(b, 1, 1))
                groups = []
                for r, t0, n, bank in ((P, 0, NT - 1, 4), (LAST, NT - 1, 1, 5)):
                    hb = h[:r, bass.ds(b, 1), t0:t0 + n, :].rearrange("p a t d -> p (a t) d")
                    main = ps[:r, bank, 0:P * n].rearrange("p (t d) -> p t d", t=n)
                    rest = ps[:r, bank + 2, 0:P * n].rearrange("p (t d) -> p t d", t=n)
                    groups.append((hb, rest, out_t[:r, t0:t0 + n, :]))
                    last = dve.tensor_tensor(hb[:, :, 0:P], main, hb[:, :, 0:P], ALU.add)
                last.then_inc(out_ready, 1)
                for hb, rest, part in groups:
                    dve.tensor_tensor(part, rest[:, :, HD:P], hb[:, :, P:D], ALU.add)
                dve.drain()
                for hb, rest, part in groups:
                    last = dve.tensor_tensor(hb[:, :, P:D], rest[:, :, 0:HD], part, ALU.add)
                last.then_inc(out_ready, 1)
                if more:
                    act_rest(b + 1, 1)

            weigh(0, 0)
            weigh(0, 1)
            w2_rest(0, 0, W2_HEAD)
            act_rest(0, 0)
            act_rest(0, 1)
            w2_rest(1, W2_HEAD, W2_PART)
            ffn(0, True)
            with dve.Fori(1, B - 1) as b:
                ffn(b, True)
            ffn(B - 1, False)

        @block.tensor
        def _(pe):
            def mm(dst, w, x, start, stop):
                return pe.matmul(dst, w, x, start=start, stop=stop)

            def series(dst, pairs):
                for i, (w, x) in enumerate(pairs):
                    last = mm(dst, w, x, i == 0, i == len(pairs) - 1)
                return last

            for k in range(KT):
                if k == 0:
                    pe.wait_ge(ld_pat[0], 32)
                if k == KT // 2:
                    pe.wait_ge(ld_pat[1], 48)
                for bank, f0, f1 in ((0, 0, P), (1, P, D)):
                    last = mm(ps[0:f1 - f0, bank, 0:B * IMG], tokw[:, k, f0:f1], pat[:, k, :], k == 0, k == KT - 1)
            last.then_inc(emb_done, 1)
            pe.wait_ge(emb_copied, 1)
            pe.wait_ge(consts, 2)
            for b in range(B):
                at = (b % 2) * D
                pe.transpose(ps[0:IMG, 2 + b // 2, at:at + P], emb[:, 0, b * IMG:(b + 1) * IMG], ident[:, :])
                last = pe.transpose(ps[0:IMG, 2 + b // 2, at + P:at + D], emb[0:HD, 1, b * IMG:(b + 1) * IMG], ident[0:HD, 0:HD])
            last.then_inc(embt_done, 1)
            pe.wait_ge(aw_lo_ready, 1)

            def weights(c0, c1):
                return aw_hi[:, 0, c0:c1], aw_lo[:, 0, c0:c1], aw_hi[:, 1, c0:c1], aw_lo[:, 1, c0:c1]

            def x_transpose(b):
                if isinstance(b, int) and b == 0:
                    pe.wait_ge(first_normed, 2)
                else:
                    pe.wait_ge(xn_ready, nth(b - 1, 1, 1))
                    pe.wait_ge(decayed, nth(b - 1, NT * H, NT * H))
                for c in range(2):
                    for I in range(NT):
                        r = rows(I)
                        bank, at = (2 * c, I * P) if I < NT - 1 else (2 * c + 1, 0)
                        last = pe.transpose(ps[:, bank, at:at + r], xn[:r, I, c * P:(c + 1) * P], ident[:r, :r])
                    last.then_inc(xt_done, 1)

            def qk(b, tail, router):
                for tile, bank in ((0, 6), (1, 4), (2, 0), (3, 2)):
                    if tile == 0 and tail:
                        pe.wait_ge(o_copied, nth(b - 1, 2, 1))
                        if router:
                            pe.wait_ge(wo_added, nth(b - 2, 3, 1))
                    if tile == 1 and router:
                        pe.wait_ge(wo_added, nth(b - 2, 3, 3))
                    ah, al, bh, bl = weights(tile * P, (tile + 1) * P)
                    passes = ((ah, xa_hi, xt_hi, 1), (al, xa_hi, None, 0), (ah, xa_lo, xt_lo, 1), (bh, xb, xt_lo, 2), (bl, xb, None, 0))
                    for i, (w, x, written, k) in enumerate(passes):
                        if tile == 0 and written:
                            pe.wait_ge(written, nth(b, 2, k))
                        for n in range(2):
                            last = mm(ps[:, bank + n, 0:HALF], w, x[:, n * HALF:(n + 1) * HALF], i == 0, i == len(passes) - 1)
                    last.then_inc(qk_done, 1)

            def values(b, tail):
                ah, al, bh, bl = weights(QK_W, QK_W + V_W)
                for I in range(NT):
                    if I == 0:
                        if tail:
                            pe.wait_ge(pt_copied, nth(b - 1, 4 * H, 4 * H))
                        else:
                            pe.wait_ge(qk_lo, nth(b, 4, 2))
                    if I == NT - 1:
                        pe.wait_ge(decayed, nth(b, NT * H, 2 * NT))
                    r = P if I < NT - 1 else KEY_LAST
                    c = slice(I * P, I * P + r)
                    bank, at = (5 - I // 2, (I % 2) * 256) if I < NT - 1 else (3, 0)
                    last = series(ps[:r, bank, at:at + 256],
                                  [(xa_hi[:, c], ah), (xa_hi[:, c], al), (xa_lo[:, c], ah), (xb[:, c], bh), (xb[:, c], bl)])
                    if I in (1, 3, 4):
                        last.then_inc(v_done, 1)

            def scores(b, hh, tail, router):
                if hh < 2:
                    g = slice(HD * hh, HD * hh + HD)
                    pairs = ((q01_hi, k01_hi), (q01_hi, k01_lo), (q01_lo, k01_hi))
                else:
                    g = slice(0, P)
                    pairs = ((q2, k2_hi), (q2, k2_lo))
                for I in range(NT):
                    if hh == 0 and I < 2:
                        pe.wait_ge(qk_lo, nth(b, 4, 3 + I))
                    elif hh and I in (0, 1, 2):
                        k = (hh - 1) * NT + (1, 2, NT)[I]
                        pe.wait_ge(decayed, nth(b, NT * H, k))
                        if hh == 2 and I == 1 and router:
                            pe.wait_ge(l_sub, nth(b - 2, 1, 1))
                        if hh == 2 and I == 1 and tail:
                            pe.wait_ge(gn_var, nth(b - 1, 1, 1))
                        if hh == 2 and I == 2:
                            pe.wait_ge(v_copied, nth(b, 3, 3))
                    r, n = rows(I), L - P * I
                    q = slice(I * P, I * P + r)
                    if I == 0:
                        parts = [(ps[:, 0, 0:HALF], 0, HALF), (ps[:, 1, 0:HALF], HALF, L)]
                    elif I == 1:
                        parts = [(ps[:, 2, 0:n], P, L)]
                    else:
                        parts = [(ps[:r, 3, S_AT[I]:S_AT[I] + n], I * P, L)]
                    for dst, m0, m1 in parts:
                        last = series(dst, [(a_[g, q], b_[g, m0:m1]) for a_, b_ in pairs])
                    if I in (0, 1, 4):
                        last.then_inc(s_done, 1)

            def gn_sums(t, head):
                if head:
                    pe.wait_ge(decayed, nth(t + 1, NT * H, NT + 2))
                pe.wait_ge(gn_part, nth(t, 1, 1))
                mm(ps[:, 2, GN_AT:GN_AT + 4], head_mean[:, :], gmv[:, :, :].rearrange("p i k -> p (i k)"), True, True).then_inc(gn_sum, 1)

            def project(t, others_free, banks):
                ah, al, bh, bl = weights(QK_W + V_W, QK_W + V_W + O_W)
                pe.wait_ge(y_lo, nth(t, 2, 1))
                for I in range(NT):
                    if I == 2 and others_free:
                        pe.wait_ge(*others_free)
                    r = rows(I)
                    c = slice(I * P, I * P + r)
                    bank, at = banks[I // 2], (I % 2) * 256
                    passes = ((y01_hi, ah), (y01_hi, al), (y01_lo, ah), (y2, bh), (y2, bl))
                    for i, (y, w) in enumerate(passes):
                        if I == 0 and i == 3:
                            pe.wait_ge(y_lo, nth(t, 2, 2))
                        last = mm(ps[:r, bank, at:at + D], y[:, c], w, i == 0, i == len(passes) - 1)
                    if I in (1, 3, 4):
                        last.then_inc(wo_done, 1)

            def probs_transpose(b, hh, groups=(0, 1, 2, 3)):
                s = hh % 2

                def tile(dst, I, J):
                    n = P if J < NT - 1 else KEY_LAST
                    r, at = rows(I), OFF[I] + (J - I) * P
                    return pe.transpose(dst, pr[s][:r, at:at + n], ident[:r, :r])

                for g in groups:
                    if g == 0:
                        pe.wait_ge(probs_ready, nth(b, H, hh + 1))
                        if hh == 2:
                            pe.wait_ge(probs_scaled, nth(b, 1, 1))
                        for I in range(NT - 1):
                            last = tile(ps[:KEY_LAST, 5, I * P:(I + 1) * P], I, NT - 1)
                    elif g == 1:
                        tile(ps[:KEY_LAST, 4, 0:LAST], NT - 1, NT - 1)
                        for I in range(3):
                            last = tile(ps[:, 4, 64 + I * P:64 + (I + 1) * P], I, 2)
                    elif g == 2:
                        pe.wait_ge(pt_copied, nth(b, 4 * H, 4 * hh + 1))
                        for I in range(4):
                            last = tile(ps[:, 5, I * P:(I + 1) * P], I, 3)
                    else:
                        pe.wait_ge(pt_copied, nth(b, 4 * H, 4 * hh + 2))
                        for I in range(2):
                            tile(ps[:, 4, I * P:(I + 1) * P], I, 1)
                        last = tile(ps[:, 4, 2 * P:3 * P], 0, 0)
                    last.then_inc(pt_done, 1)

            def attend(b, hh):
                first, last_head = hh != 1, hh != 0
                tail = 64 if hh == 2 else 0
                cols = slice(hh * P, (hh + 1) * P)
                pe.wait_ge(pt_copied, nth(b, 4 * H, 4 * hh + 2))
                mm(ps[:, 6, :], v[:KEY_LAST, 4, cols], pt[:KEY_LAST, 0, :], first, False)
                mm(ps[:, 7, tail:tail + LAST], v[:KEY_LAST, 4, cols], pt[:KEY_LAST, 1, 0:LAST], first, last_head)
                mm(ps[:, 6, 0:3 * P], v[:, 2, cols], pt[:, 1, 64:64 + 3 * P], False, False)
                pe.wait_ge(pt_copied, nth(b, 4 * H, 4 * hh + 3))
                mm(ps[:, 6, :], v[:, 3, cols], pt[:, 2, :], False, False)
                pe.wait_ge(pt_copied, nth(b, 4 * H, 4 * hh + 4))
                mm(ps[:, 6, 0:2 * P], v[:, 1, cols], pt[:, 3, 0:2 * P], False, False)
                last = mm(ps[:, 6, 0:P], v[:, 0, cols], pt[:, 3, 2 * P:3 * P], False, last_head)
                if last_head:
                    last.then_inc(o_done, 1)

            def x2_transpose(u, bank1, ready):
                pe.wait_ge(*ready)
                apart(pe, "pe")
                for c in range(2):
                    last = pe.transpose(ps[:, bank1, X2_AT + 64 * c:X2_AT + 64 * c + LAST], xn2[:LAST, NT - 1, c * P:(c + 1) * P], ident[:LAST, :LAST])
                last.then_inc(x2t_done, 1)
                for c, bank in ((0, 6), (1, 7)):
                    for I in range(NT - 1):
                        last = pe.transpose(ps[:, bank, I * P:(I + 1) * P], xn2[:, I, c * P:(c + 1) * P], ident[:, :])
                    last.then_inc(x2t_done, 1)

            def logits(u, src, banks):
                ah, al, bh, bl = weights(QK_W + V_W + O_W, AW)
                pe.wait_ge(x2_lo, nth(u, 3, 3))
                for n, bank in enumerate(banks):
                    c = slice(n * HALF, (n + 1) * HALF)
                    last = series(ps[0:E, bank, 0:HALF],
                                  [(ah, src[:, 0, c]), (al, src[:, 0, c]), (ah, src[:, 1, c]), (bh, src[:, 2, c]), (bl, src[:, 2, c])])
                last.then_inc(lg_done, 1)

            def logits_transpose(u, head):
                pe.wait_ge(lt_copied, nth(u, 1, 1))
                if head:
                    pe.wait_ge(decayed, nth(u + 2, NT * H, NT + 2))
                apart(pe, "pe")
                for I in range(NT):
                    at = LG_AT + I * E
                    last = pe.transpose(ps[:, 2, at:at + E], lt[:, I * P:(I + 1) * P], ident[0:E, 0:E])
                last.then_inc(lgn_done, 1)

            def comb_transpose(u, first):
                pe.wait_ge(comb_ready, nth(u, 1, 1))
                for I in range(NT):
                    bank, at = (first, I * P) if I < NT - 1 else (first + 1, 0)
                    last = pe.transpose(ps[0:E, bank, at:at + P], comb[:, I, :], ident[:, :])
                last.then_inc(ct_done, 1)

            def body(b, tail, router, more):
                t, u = b - 1, b - 2
                qk(b, tail, router)
                if tail:
                    pe.wait_ge(qk_lo, nth(b, 4, 2))
                    probs_transpose(t, 2, (0, 1))
                scores(b, 0, tail, router)
                if tail:
                    probs_transpose(t, 2, (2, 3))
                    pe.wait_ge(qk_lo, nth(b, 4, 1))
                    attend(t, 2)
                scores(b, 1, tail, router)
                if router:
                    pe.wait_ge(o_copied, nth(t, 2, 2))
                    pe.wait_ge(decayed, nth(b, NT * H, NT + 1))
                    x2_transpose(u, 1, (xn2_ready, nth(u, 1, 1)))
                values(b, tail)
                pe.wait_ge(v_copied, nth(b, 3, 1))
                probs_transpose(b, 0, (0,))
                pe.wait_ge(v_copied, nth(b, 3, 2))
                apart(pe, "pe")
                probs_transpose(b, 0, (1,))
                if router:
                    logits(u, x2, (6, 7))
                probs_transpose(b, 0, (2, 3))
                if router:
                    logits_transpose(u, True)
                if tail:
                    gn_sums(t, True)
                pe.wait_ge(v_copied, nth(b, 3, 3))
                if tail and not router:
                    pe.wait_ge(o_copied, nth(t, 2, 2))
                attend(b, 0)
                pe.wait_ge(pt_copied, nth(b, 4 * H, 4))
                probs_transpose(b, 1, (0, 1))
                scores(b, 2, tail, router)
                probs_transpose(b, 1, (2, 3))
                attend(b, 1)
                if more:
                    x_transpose(b + 1)
                if not more:
                    pe.wait_ge(decayed, nth(b, NT * H, NT * H))
                if router:
                    comb_transpose(u, 4 if more else 0)
                if tail and more:
                    pe.wait_ge(o_copied, nth(b, 2, 1))
                    project(t, (ct_copied, CREDIT + nth(u, 1, 1)) if router else None, (6, 4, 5))

            def up(b, k, parts=(0, 1)):
                if k == 0 and 0 in parts:
                    pe.wait_ge(ld_x2, 16 * (b + 1))
                if k >= 2 or not isinstance(b, int) or b:
                    pe.wait_ge(gelu_done, nth(b, NW, k - 1))
                w = slice(k * P, (k + 1) * P)
                for n in parts:
                    def x(c):
                        return x2_all[:, bass.ds(b, 1), c, n * HALF:(n + 1) * HALF].rearrange("p a n -> p (a n)")
                    last = series(ps[:, 2 * (k % 2) + n, 0:HALF],
                                  [(w1_hi[:, 0, w], x(0)), (w1_lo[:, 0, w], x(0)), (w1_hi[:, 0, w], x(1)),
                                   (w1_hi[:, 1, w], x(2)), (w1_lo[:, 1, w], x(2))])
                if 1 in parts:
                    last.then_inc(up_done, 1)

            def drain(t, u):
                pe.wait_ge(o_copied, nth(t, 2, 1))
                project(u, None, (6, 7, 3))
                probs_transpose(t, 2)
                pe.wait_ge(wo_added, nth(u, 3, 3))
                attend(t, 2)
                gn_sums(t, False)
                pe.wait_ge(ct_copied, CREDIT + nth(u - 1, 1, 1))
                project(t, None, (0, 1, 3))
                pe.wait_ge(o_copied, nth(t, 2, 2))
                x2_transpose(u, 4, (xn2_ready, nth(u, 1, 1)))
                pe.wait_ge(wo_added, nth(t, 3, 3))
                logits(u, x2, (0, 1))
                x2_transpose(t, 4, (last_normed, 2))
                pe.wait_ge(gn_var, nth(t, 1, 1))
                logits_transpose(u, False)
                logits(t, y, (6, 7))
                pe.wait_ge(l_sub, nth(u, 1, 1))
                logits_transpose(t, False)
                comb_transpose(u, 4)
                pe.wait_ge(w1_split, B)
                up(0, 0)
                comb_transpose(t, 6)
                up(0, 1)

            x_transpose(0)
            iterations(pe, body)
            drain(B - 1, B - 2)
            end_of_phase_a(pe)

            def down(b, k):
                pe.wait_ge(act_lo_ready, nth(b, NW, k + 1))
                if isinstance(b, int) and b == 0 and k in (0, W2_HEAD):
                    pe.wait_ge(w2_lo_ready, 2 if k else 1)
                elif isinstance(b, int) and b == 0 and k % W2_PART == 0:
                    pe.wait_ge(w2_split, k // W2_PART)
                first, last_k = k == 0, k == NW - 1
                hi, lo = act_hi[k % 3], act_lo[k % 3]
                if k == 0 and (not isinstance(b, int) or b):
                    pe.wait_ge(out_ready, nth(b - 1, 2, 1))
                for n in range(2):
                    mm(ps[:, 4 + n, 0:HALF], w2_hi[:, k, :], hi[:, n, :], first, False)
                    mm(ps[:, 4 + n, 0:HALF], w2_lo[:, k, :], hi[:, n, :], False, False)
                    mm(ps[:, 4 + n, 0:HALF], w2_hi[:, k, :], lo[:, n, :], False, last_k)
                if k == 0 and (not isinstance(b, int) or b):
                    pe.wait_ge(out_ready, nth(b - 1, 2, 2))
                for n in range(2):
                    mm(ps[:, 6 + n, 0:HALF], w2_r[:, k, :], hi[:, n, :], first, False)
                    last = mm(ps[:, 6 + n, 0:HALF], w2_r[:, k, :], lo[:, n, :], False, last_k)
                last.then_inc(down_done, 1)

            def ffn(b, more):
                for k in range(NW):
                    if 2 <= k < NW - 2:
                        up(b, k + 2)
                    elif k >= NW - 2 and more:
                        up(b + 1, k + 2 - NW)
                    down(b, k)
                if more:
                    up(b + 1, 2, (0,))
                pe.wait_ge(acc_a_copied, nth(b, 1, 1))
                pe.wait_ge(acc_r_copied, nth(b, 1, 1))
                for I in range(NT):
                    r = rows(I)
                    bank, at = (4, I * P) if I < NT - 1 else (5, 0)
                    pe.transpose(ps[:r, bank, at:at + P], out_a[:, I * P:I * P + r], ident[:, :])
                    last = pe.transpose(ps[:r, bank + 2, at:at + P], out_r[:, I * P:I * P + r], ident[:, :])
                last.then_inc(outt_done, 1)
                if more:
                    up(b + 1, 2, (1,))
                    up(b + 1, 3)

            up(0, 2)
            up(0, 3)
            ffn(0, True)
            with pe.Fori(1, B - 1) as b:
                ffn(b, True)
            ffn(B - 1, False)


DVE_TILES = 2
LG_AT = L - P
GN_AT = LG_AT + NT * E
X2_AT = 320
S_AT = {2: 0, 3: L - 2 * P, 4: (L - 2 * P) + (L - 3 * P)}


def _stack(np, wt):
    return np.ascontiguousarray(np.stack([wt[0:128], np.concatenate([wt[128:192], wt[128:192]])], axis=1))


def kernel(x, txt, L0_tok_W, L0_tok_b, L0_attn_Wq, L0_attn_Wk, L0_attn_Wv, L0_attn_Wo, L0_attn_gammas,
           L0_attn_gn_weight, L0_attn_gn_bias, L0_ffn_router_w, L0_ffn_w1, L0_ffn_w2):
    import concourse.bacc as bacc
    import numpy as np
    from concourse.bass_utils import run_bass_kernel_spmd

    f = lambda t: np.asarray(t)
    img = f(x).reshape(B, 3, 6, 16, 6, 16).transpose(1, 3, 5, 0, 2, 4).reshape(KT, P, B * IMG)
    wq, wk, wv, wo, wr = f(L0_attn_Wq).T, f(L0_attn_Wk).T, f(L0_attn_Wv).T, f(L0_attn_Wo).T, f(L0_ffn_router_w).T
    q2, k2 = wq[:, 128:], wk[:, 128:]
    attn = np.concatenate([wq[:, 0:128], wk[:, 0:128], q2, q2, k2, k2, wv, wv[:, 128:], wo, wr], axis=1)
    w2 = f(L0_ffn_w2).reshape(NW, P, D).transpose(1, 0, 2)

    def columns(vec):
        return np.stack([vec[0:128], np.concatenate([vec[128:192], vec[128:192]])], axis=1)

    arrays = {
        "patches": img.transpose(1, 0, 2),
        "txt": f(txt),
        "tok_w": f(L0_tok_W).T.reshape(KT, P, D).transpose(1, 0, 2),
        "tok_b": columns(f(L0_tok_b)),
        "gammas": f(L0_attn_gammas),
        "gn_w": columns(f(L0_attn_gn_weight)),
        "gn_b": columns(f(L0_attn_gn_bias)),
        "attn_w": _stack(np, attn),
        "w1": _stack(np, f(L0_ffn_w1)),
        "w2": np.concatenate([w2, w2[:, :, 128:]], axis=2),
    }
    arrays = {n: np.ascontiguousarray(a) for n, a in arrays.items()}
    nc = bacc.Bacc("TRN2", target_bir_lowering=False, num_devices=1)
    args = [nc.dram_tensor(n, a.shape, F32, kind="ExternalInput").ap() for n, a in arrays.items()]
    out = nc.dram_tensor("out", (B, L, D), F32, kind="ExternalOutput").ap()
    early_fusion(nc, *args, out)
    r = run_bass_kernel_spmd(nc, [arrays], core_ids=[0])
    return r.results[0]["out"]
```
